# Optimizing a Trainium2 kernel written in Bass

```python
import numpy as np
import jax
import jax.numpy as jnp

def _softmax(x, axis=-1):
    return jax.nn.softmax(x, axis=axis)

def _gelu(x):
    return jax.nn.gelu(x, approximate=True)

def _silu(x):
    return jax.nn.silu(x)

def _sigmoid(x):
    return jax.nn.sigmoid(x)

def _layernorm(x, axis=-1, eps=1e-05):
    m = jnp.mean(x, axis=axis, keepdims=True)
    v = jnp.var(x, axis=axis, keepdims=True)
    return (x - m) / jnp.sqrt(v + eps)

def _scatter_add(tgt, idx, src, axis=0):
    return tgt.at[idx].add(src)

def _segment_sum(src, seg, n):
    return jax.ops.segment_sum(src, seg, n)
kernel_name = 'mk_sandwich_d1_jaxref_r8_35064e'

def setup_inputs(seed: int=0):
    np.random.seed(seed)
    _w = jnp.asarray

    def _L0_attn_setup():
        import jax, jax.numpy as jnp
        import numpy as np
        D_MODEL = 128
        NUM_HEADS = 16
        HEAD_DIM = D_MODEL // NUM_HEADS
        key = jax.random.key(seed)
        ks = jax.random.split(key, 9)
        B, S = (4, 256)
        s = 1.0 / np.sqrt(D_MODEL)
        return {'x': jax.random.normal(ks[0], (B, S, D_MODEL), dtype=jnp.float32), 'Wq': jax.random.normal(ks[1], (D_MODEL, D_MODEL), dtype=jnp.float32) * s, 'bq': jnp.zeros((D_MODEL,), dtype=jnp.float32), 'Wk': jax.random.normal(ks[2], (D_MODEL, HEAD_DIM), dtype=jnp.float32) * s, 'bk': jnp.zeros((HEAD_DIM,), dtype=jnp.float32), 'Wv': jax.random.normal(ks[3], (D_MODEL, HEAD_DIM), dtype=jnp.float32) * s, 'bv': jnp.zeros((HEAD_DIM,), dtype=jnp.float32), 'Wo': jax.random.normal(ks[4], (D_MODEL, D_MODEL), dtype=jnp.float32) * s, 'bo': jnp.zeros((D_MODEL,), dtype=jnp.float32)}
    _L0_attn_in = _L0_attn_setup()

    def _L0_ffn_setup():
        import jax, jax.numpy as jnp
        import numpy as np
        DIM = 128
        DEPTH = 6
        HEADS = 16
        DIM_HEAD = 64
        WINDOW = 32
        INNER = HEADS * DIM_HEAD
        DIM_INNER = int(DIM * 4 * 2 / 3)
        QK_SCALE = 8.0

        def shift_tokens(t):
            a, s = jnp.split(t, 2, -1)
            s = jnp.pad(s, ((0, 0), (1, 0), (0, 0)))[:, :-1]
            return jnp.concatenate([a, s], -1)

        def l2norm(t):
            return t / jnp.maximum(jnp.linalg.norm(t, axis=-1, keepdims=True), 1e-12)

        def rotate_half(x):
            x1, x2 = jnp.split(x, 2, -1)
            return jnp.concatenate([-x2, x1], -1)

        def rotary_tables(n):
            half = jnp.arange(0, DIM_HEAD, 2, dtype=jnp.float32)
            inv_freq = 1.0 / 10000.0 ** (half / DIM_HEAD)
            t = jnp.arange(n, dtype=jnp.float32)
            freqs = t[:, None] * inv_freq[None, :]
            freqs = jnp.concatenate([freqs, freqs], -1)
            base_scale = (half + 0.4 * DIM_HEAD) / (1.4 * DIM_HEAD)
            power = (t - n // 2) / (WINDOW // 2)
            scale = base_scale[None, :] ** power[:, None]
            scale = jnp.concatenate([scale, scale], -1)
            return (freqs, scale)

        def local_attention(q, k, v):
            b, h, n, d = q.shape
            w = WINDOW
            nw = n // w
            bq = q.reshape(b, h, nw, w, d)
            bk = k.reshape(b, h, nw, w, d)
            bv = v.reshape(b, h, nw, w, d)

            def look(t):
                p = jnp.pad(t, ((0, 0), (0, 0), (1, 0), (0, 0), (0, 0)))
                return jnp.concatenate([p[:, :, :nw], p[:, :, 1:]], axis=3)
            bk2, bv2 = (look(bk), look(bv))
            seq = jnp.arange(n).reshape(nw, w)
            seq_p = jnp.pad(seq, ((1, 0), (0, 0)), constant_values=-1)
            jt = jnp.concatenate([seq_p[:nw], seq_p[1:]], axis=1)
            it = seq[:, :, None]
            jb = jt[:, None, :]
            mask = (it < jb) | (it > jb + w) | (jb == -1)
            sim = jnp.einsum('bhwie,bhwje->bhwij', bq, bk2) * QK_SCALE
            sim = jnp.where(mask, -jnp.finfo(sim.dtype).max, sim)
            attn = jax.nn.softmax(sim, -1)
            out = jnp.einsum('bhwij,bhwje->bhwie', attn, bv2)
            return out.reshape(b, h, n, d)

        def attn_layer(x, Wqkv, qs, ksc, Wo):
            b, n, _ = x.shape
            qkv = x @ Wqkv
            q, k, v = jnp.split(qkv, 3, -1)
            sh = lambda t: t.reshape(b, n, HEADS, DIM_HEAD).transpose(0, 2, 1, 3)
            q, k, v = (sh(q), sh(k), sh(v))
            q = l2norm(q) * qs
            k = l2norm(k) * ksc
            freqs, scale = rotary_tables(n)
            cos, sin = (jnp.cos(freqs), jnp.sin(freqs))
            q = q * cos * scale + rotate_half(q) * sin * scale
            inv = 1.0 / scale
            k = k * cos * inv + rotate_half(k) * sin * inv
            out = local_attention(q, k, v)
            out = out.transpose(0, 2, 1, 3).reshape(b, n, INNER)
            return out @ Wo

        def ffn_layer(x, g, bln, W1, b1, W2, b2):
            mu = x.mean(-1, keepdims=True)
            var = ((x - mu) ** 2).mean(-1, keepdims=True)
            xn = (x - mu) / jnp.sqrt(var + 1e-05) * g + bln
            hg = xn @ W1 + b1
            a, gate = jnp.split(hg, 2, -1)
            return a * jax.nn.gelu(gate, approximate=False) @ W2 + b2
        key = jax.random.key(seed)
        ks = jax.random.split(key, 8)
        B, N = (2, 256)
        init = lambda k, shape: jax.random.normal(k, shape, jnp.float32) * 0.02
        return {'x': jax.random.normal(ks[0], (B, N, DIM), jnp.float32), 'Wqkv': init(ks[1], (DEPTH, DIM, 3 * INNER)), 'q_scale': jnp.ones((DEPTH, DIM_HEAD), jnp.float32), 'k_scale': jnp.ones((DEPTH, DIM_HEAD), jnp.float32), 'Wo': init(ks[2], (DEPTH, INNER, DIM)), 'ln_g': jnp.ones((DEPTH, DIM), jnp.float32), 'ln_b': jnp.zeros((DEPTH, DIM), jnp.float32), 'W1': init(ks[3], (DEPTH, DIM, 2 * DIM_INNER)), 'b1': jnp.zeros((DEPTH, 2 * DIM_INNER), jnp.float32), 'W2': init(ks[4], (DEPTH, DIM_INNER, DIM)), 'b2': jnp.zeros((DEPTH, DIM), jnp.float32)}
    _L0_ffn_in = _L0_ffn_setup()
    _d = {'L0_attn_x': _L0_attn_in['x'], 'L0_attn_Wq': _L0_attn_in['Wq'], 'L0_attn_bq': _L0_attn_in['bq'], 'L0_attn_Wk': _L0_attn_in['Wk'], 'L0_attn_bk': _L0_attn_in['bk'], 'L0_attn_Wv': _L0_attn_in['Wv'], 'L0_attn_bv': _L0_attn_in['bv'], 'L0_attn_Wo': _L0_attn_in['Wo'], 'L0_attn_bo': _L0_attn_in['bo'], 'L0_ffn_Wqkv': _L0_ffn_in['Wqkv'], 'L0_ffn_q_scale': _L0_ffn_in['q_scale'], 'L0_ffn_k_scale': _L0_ffn_in['k_scale'], 'L0_ffn_Wo': _L0_ffn_in['Wo'], 'L0_ffn_ln_g': _L0_ffn_in['ln_g'], 'L0_ffn_ln_b': _L0_ffn_in['ln_b'], 'L0_ffn_W1': _L0_ffn_in['W1'], 'L0_ffn_b1': _L0_ffn_in['b1'], 'L0_ffn_W2': _L0_ffn_in['W2'], 'L0_ffn_b2': _L0_ffn_in['b2']}
    _x0 = _d['L0_attn_x']
    _d['L0_attn_x'] = jax.random.normal(jax.random.fold_in(jax.random.key(seed), 1), (8, 512, 128), dtype=_x0.dtype)
    del _x0
    return _d

def reference(L0_attn_x, L0_attn_Wq, L0_attn_bq, L0_attn_Wk, L0_attn_bk, L0_attn_Wv, L0_attn_bv, L0_attn_Wo, L0_attn_bo, L0_ffn_Wqkv, L0_ffn_q_scale, L0_ffn_k_scale, L0_ffn_Wo, L0_ffn_ln_g, L0_ffn_ln_b, L0_ffn_W1, L0_ffn_b1, L0_ffn_W2, L0_ffn_b2):

    def _L0_attn_ref(x, Wq, bq, Wk, bk, Wv, bv, Wo, bo):
        import jax, jax.numpy as jnp
        import numpy as np
        D_MODEL = 128
        NUM_HEADS = 16
        HEAD_DIM = D_MODEL // NUM_HEADS
        B, S, _ = x.shape
        H, Dh = (NUM_HEADS, HEAD_DIM)
        Q = (x @ Wq + bq).reshape(B, S, H, Dh).transpose(0, 2, 1, 3)
        K = x @ Wk + bk
        V = x @ Wv + bv
        A = jnp.einsum('bhqd,bkd->bhqk', Q, K)
        causal = jnp.tril(jnp.ones((S, S), dtype=bool))
        A = jnp.where(causal, A, -jnp.inf)
        P = jax.nn.softmax(A / np.sqrt(Dh).astype(np.float32), axis=-1)
        O = jnp.einsum('bhqk,bkd->bhqd', P, V)
        O = O.transpose(0, 2, 1, 3).reshape(B, S, H * Dh)
        return O @ Wo + bo

    def _L0_ffn_ref(x, Wqkv, q_scale, k_scale, Wo, ln_g, ln_b, W1, b1, W2, b2):
        import jax, jax.numpy as jnp
        import numpy as np
        DIM = 128
        DEPTH = 6
        HEADS = 16
        DIM_HEAD = 64
        WINDOW = 32
        INNER = HEADS * DIM_HEAD
        DIM_INNER = int(DIM * 4 * 2 / 3)
        QK_SCALE = 8.0

        def shift_tokens(t):
            a, s = jnp.split(t, 2, -1)
            s = jnp.pad(s, ((0, 0), (1, 0), (0, 0)))[:, :-1]
            return jnp.concatenate([a, s], -1)

        def l2norm(t):
            return t / jnp.maximum(jnp.linalg.norm(t, axis=-1, keepdims=True), 1e-12)

        def rotate_half(x):
            x1, x2 = jnp.split(x, 2, -1)
            return jnp.concatenate([-x2, x1], -1)

        def rotary_tables(n):
            half = jnp.arange(0, DIM_HEAD, 2, dtype=jnp.float32)
            inv_freq = 1.0 / 10000.0 ** (half / DIM_HEAD)
            t = jnp.arange(n, dtype=jnp.float32)
            freqs = t[:, None] * inv_freq[None, :]
            freqs = jnp.concatenate([freqs, freqs], -1)
            base_scale = (half + 0.4 * DIM_HEAD) / (1.4 * DIM_HEAD)
            power = (t - n // 2) / (WINDOW // 2)
            scale = base_scale[None, :] ** power[:, None]
            scale = jnp.concatenate([scale, scale], -1)
            return (freqs, scale)

        def local_attention(q, k, v):
            b, h, n, d = q.shape
            w = WINDOW
            nw = n // w
            bq = q.reshape(b, h, nw, w, d)
            bk = k.reshape(b, h, nw, w, d)
            bv = v.reshape(b, h, nw, w, d)

            def look(t):
                p = jnp.pad(t, ((0, 0), (0, 0), (1, 0), (0, 0), (0, 0)))
                return jnp.concatenate([p[:, :, :nw], p[:, :, 1:]], axis=3)
            bk2, bv2 = (look(bk), look(bv))
            seq = jnp.arange(n).reshape(nw, w)
            seq_p = jnp.pad(seq, ((1, 0), (0, 0)), constant_values=-1)
            jt = jnp.concatenate([seq_p[:nw], seq_p[1:]], axis=1)
            it = seq[:, :, None]
            jb = jt[:, None, :]
            mask = (it < jb) | (it > jb + w) | (jb == -1)
            sim = jnp.einsum('bhwie,bhwje->bhwij', bq, bk2) * QK_SCALE
            sim = jnp.where(mask, -jnp.finfo(sim.dtype).max, sim)
            attn = jax.nn.softmax(sim, -1)
            out = jnp.einsum('bhwij,bhwje->bhwie', attn, bv2)
            return out.reshape(b, h, n, d)

        def attn_layer(x, Wqkv, qs, ksc, Wo):
            b, n, _ = x.shape
            qkv = x @ Wqkv
            q, k, v = jnp.split(qkv, 3, -1)
            sh = lambda t: t.reshape(b, n, HEADS, DIM_HEAD).transpose(0, 2, 1, 3)
            q, k, v = (sh(q), sh(k), sh(v))
            q = l2norm(q) * qs
            k = l2norm(k) * ksc
            freqs, scale = rotary_tables(n)
            cos, sin = (jnp.cos(freqs), jnp.sin(freqs))
            q = q * cos * scale + rotate_half(q) * sin * scale
            inv = 1.0 / scale
            k = k * cos * inv + rotate_half(k) * sin * inv
            out = local_attention(q, k, v)
            out = out.transpose(0, 2, 1, 3).reshape(b, n, INNER)
            return out @ Wo

        def ffn_layer(x, g, bln, W1, b1, W2, b2):
            mu = x.mean(-1, keepdims=True)
            var = ((x - mu) ** 2).mean(-1, keepdims=True)
            xn = (x - mu) / jnp.sqrt(var + 1e-05) * g + bln
            hg = xn @ W1 + b1
            a, gate = jnp.split(hg, 2, -1)
            return a * jax.nn.gelu(gate, approximate=False) @ W2 + b2
        for i in range(DEPTH):
            x = attn_layer(shift_tokens(x), Wqkv[i], q_scale[i], k_scale[i], Wo[i]) + x
            x = ffn_layer(shift_tokens(x), ln_g[i], ln_b[i], W1[i], b1[i], W2[i], b2[i]) + x
        return x
    x = L0_attn_x
    x = x + _layernorm(_L0_attn_ref(_layernorm(x, axis=-1), L0_attn_Wq, L0_attn_bq, L0_attn_Wk, L0_attn_bk, L0_attn_Wv, L0_attn_bv, L0_attn_Wo, L0_attn_bo), axis=-1)
    x = x + _layernorm(_L0_ffn_ref(_layernorm(x, axis=-1), L0_ffn_Wqkv, L0_ffn_q_scale, L0_ffn_k_scale, L0_ffn_Wo, L0_ffn_ln_g, L0_ffn_ln_b, L0_ffn_W1, L0_ffn_b1, L0_ffn_W2, L0_ffn_b2), axis=-1)
    return x

_drawn_inputs = setup_inputs


def setup_inputs(seed=0):
    import zlib

    import numpy as np

    out = dict(_drawn_inputs(seed))
    spreads = {'L0_attn_bq': (0.0, 0.1),
     'L0_attn_bk': (0.0, 2.0),
     'L0_attn_bv': (0.0, 0.1),
     'L0_attn_bo': (0.0, 0.1),
     'L0_ffn_q_scale': (1.0, 0.6),
     'L0_ffn_k_scale': (1.0, 0.6),
     'L0_ffn_ln_g': (1.0, 0.6),
     'L0_ffn_ln_b': (0.0, 0.8),
     'L0_ffn_b1': (0.0, 0.8),
     'L0_ffn_b2': (0.0, 0.358)}
    factors = {'L0_ffn_W1': 4.48, 'L0_ffn_W2': 4.391}
    for name, (base, spread) in spreads.items():
        noise = np.random.default_rng([zlib.crc32(name.encode()), seed]).standard_normal(out[name].shape)
        drawn = base * np.exp(spread * noise) if base else spread * noise
        out[name] = jnp.asarray(drawn.astype(out[name].dtype))
    for name, factor in factors.items():
        out[name] = (out[name] * factor).astype(out[name].dtype)
    return out
```

```python
from contextlib import ExitStack

import numpy as np

import concourse.bass as bass
from concourse import mybir
from concourse.alu_op_type import AluOpType as ALU

ACT = mybir.ActivationFunctionType
AX = mybir.AxisListType
F32 = mybir.dt.float32
F32R = mybir.dt.float32r
BF16 = mybir.dt.bfloat16

P = 128
B, S, D = 8, 512, 128
TILES = S // P
MQA_H, MQA_D = 16, 8
DEPTH, H, DH = 6, 16, 64
INNER = H * DH
WINDOW = 32
FF = int(D * 4 * 2 / 3)
FC = -(-FF // P)
FR = FF - (FC - 1) * P
BIAS_ROW = 96
QK_SCALE = 8.0
MASKED = -1e30
LN_EPS = 1e-5
L2_EPS2 = 1e-24


class Events:

    def __init__(self, semaphore, per):
        self.sem, self.per = semaphore, per

    def at(self, k, cycle):
        return cycle * self.per + (self.per + k)


def rotary_tables():
    half = np.arange(0, DH, 2, dtype=np.float32)
    inv_freq = (np.float32(1.0) / np.power(np.float32(10000.0), half / np.float32(DH))).astype(np.float32)
    t = np.arange(S, dtype=np.float32)
    freqs = (t[:, None] * inv_freq[None, :]).astype(np.float32)
    base = ((half + np.float32(0.4 * DH)) / np.float32(1.4 * DH)).astype(np.float32)
    power = ((t - S // 2) / np.float32(WINDOW // 2)).astype(np.float32)
    scale = np.power(base[None, :].astype(np.float64), power[:, None].astype(np.float64))
    cos, sin = np.cos(freqs.astype(np.float64)), np.sin(freqs.astype(np.float64))
    both = lambda a, b: np.concatenate([a, b], -1)
    return np.stack([both(cos * scale, cos * scale), both(sin * scale, -sin * scale),
                     both(cos / scale, cos / scale), both(sin / scale, -sin / scale)]).astype(np.float32)


def constants_stage(nc, c, x_in, credits):
    with ExitStack() as ctx:
        zeroed = ctx.enter_context(nc.semaphore("zeroed"))
        selected = ctx.enter_context(nc.semaphore("selected"))
        loaded = ctx.enter_context(nc.semaphore("loaded"))
        block = ctx.enter_context(nc.Block())

        @block.sync
        def _(sp):
            for b in range(B):
                sp.dma_start(c["x_tok"][:, b * TILES:(b + 1) * TILES, :],
                             x_in[b].rearrange("(t p) d -> p t d", p=P)).then_inc(loaded, 16)
            for e in credits:
                sp.sem_inc(e.sem, e.per)
            sp.wait_ge(loaded, 16 * B)

        @block.vector
        def _(dve):
            nc.vector.memset(c["ones"][:, :], 1.0)
            nc.vector.memset(c["mean_of"][:, :], 1.0 / D)
            nc.vector.memset(c["minus_half"][:, :], -0.5)
            nc.vector.memset(c["ident"][:, :], 0.0)
            nc.vector.memset(c["ident_bf"][:, :], 0.0)
            nc.vector.memset(c["mask_qk"][:, :], 0.0)
            nc.vector.memset(c["mask_kq"][:, :], 0.0)
            nc.vector.memset(c["mask_band"][:, :, :], 0.0).then_inc(zeroed, 1)

        @block.gpsimd
        def _(pool):
            pool.wait_ge(zeroed, 1)
            step = [0]

            def select(out, pattern, compare, base, fill, channel):
                nc.gpsimd.affine_select(out=out, in_=out, compare_op=compare, fill=fill, base=base,
                                        pattern=pattern, channel_multiplier=channel).then_inc(selected, 1)
                step[0] += 1
                pool.wait_ge(selected, step[0])

            select(c["ident"][:, :], [[-1, P]], ALU.not_equal, 0, 1.0, 1)
            select(c["ident_bf"][:, :], [[-1, P]], ALU.not_equal, 0, 1.0, 1)
            select(c["mask_qk"][:, :], [[-1, P]], ALU.is_ge, 0, MASKED, 1)
            select(c["mask_kq"][:, :], [[1, P]], ALU.is_ge, 0, MASKED, -1)
            select(c["mask_band"][:, :, :], [[0, 3], [-1, WINDOW + P]], ALU.is_ge, WINDOW, MASKED, 1)
            select(c["mask_band"][:, :, :], [[0, 3], [1, WINDOW + P]], ALU.is_ge, 0, MASKED, -1)


SLOTS = 32
GROUPS = MQA_H * SLOTS // P
PER_GROUP = MQA_H // GROUPS
QKV_W = D + 2 * MQA_D
SCORE_SCALE = float(np.float32(1.0) / np.sqrt(np.float32(MQA_D)))
PROB_AT = {0: 0, 1: 512, 3: 896, 2: 1024}
PROB_BANKS = ((0,), (1, 3), (2,))
PROBS_W = 1280


def mqa_events(sem):
    return {
        "stats": Events(sem("a_stats"), 6), "var": Events(sem("a_var"), 3), "rstd": Events(sem("a_rstd"), 3),
        "xn": Events(sem("a_xn"), 1), "xnT_full": Events(sem("a_xnT_full"), 1), "xnT": Events(sem("a_xnT"), 1),
        "qkv_full": Events(sem("a_qkv_full"), 2), "hi": Events(sem("a_hi"), 2), "lo": Events(sem("a_lo"), 2),
        "t1_full": Events(sem("a_t1_full"), 5), "t1": Events(sem("a_t1"), 5),
        "s_full": Events(sem("a_s_full"), MQA_H * TILES), "s_max": Events(sem("a_s_max"), MQA_H * TILES),
        "m_hi": Events(sem("a_m_hi"), GROUPS), "m": Events(sem("a_m"), GROUPS),
        "t2_full": Events(sem("a_t2_full"), GROUPS), "t2": Events(sem("a_t2"), GROUPS),
        "st_full": Events(sem("a_st_full"), 3 * MQA_H), "exp": Events(sem("a_exp"), 3 * MQA_H),
        "pv_full": Events(sem("a_pv_full"), MQA_H), "pv": Events(sem("a_pv"), GROUPS),
        "pvT_full": Events(sem("a_pvT_full"), GROUPS), "recip": Events(sem("a_recip"), GROUPS),
        "attn": Events(sem("a_attn"), GROUPS),
        "oT_full": Events(sem("a_oT_full"), 1), "oT": Events(sem("a_oT"), 1), "proj": Events(sem("a_proj"), 1),
        "o": Events(sem("a_o"), 1), "x2": Events(sem("a_x2"), 1), "y": Events(sem("a_y"), 1),
        "yT_full": Events(sem("a_yT_full"), 1), "yT": Events(sem("a_yT"), 1),
    }


def mqa_stage(nc, c, e, weights, residual):
    with ExitStack() as ctx:
        def sb(name, shape, dt=F32):
            return ctx.enter_context(nc.sbuf_tensor(name, shape, dt))

        def bank(name):
            return ctx.enter_context(nc.psum_tensor(name, [P, 512], F32))

        wqkv = sb("a_wqkv", [P, QKV_W])
        bqkv = sb("a_bqkv", [1, QKV_W])
        wo, bo = sb("a_wo", [P, D]), sb("a_bo", [1, D])
        stat6, stat = sb("a_stat6", [P, 2, TILES, 6]), sb("a_stat", [P, 3, TILES, 2])
        var, rstd = sb("a_varb", [P, 3, TILES]), sb("a_rstdb", [P, 3, TILES])
        xn, xnT = sb("a_xnb", [P, TILES, D]), sb("a_xnTb", [P, S])
        qa = sb("a_qa", [P, TILES, MQA_H, SLOTS], F32R)
        ka = sb("a_ka", [P, TILES, PER_GROUP, SLOTS], F32R)
        va = sb("a_va", [P, TILES, SLOTS])
        qT0 = sb("a_qT0", [P, GROUPS, S], F32R)
        qT1 = sb("a_qT1", [P, GROUPS, S], F32R)
        kT = sb("a_kT", [P, S], F32R)
        row_max = sb("a_row_max", [P, TILES, MQA_H])
        probs = sb("a_probs", [P, 2, PROBS_W])
        pv = sb("a_pvb", [P, S])
        recip = sb("a_recipb", [P, GROUPS, TILES, PER_GROUP])
        attn, attnT = sb("a_attnb", [P, TILES, D]), sb("a_attnTb", [P, S])
        o, y = sb("a_ob", [P, TILES, D]), sb("a_yb", [P, TILES, D])
        carrier = sb("a_carrier", [P, 1])
        turn = [bank("a_turn0"), bank("a_turn1")]
        score = [bank("a_score0"), bank("a_score1")]
        scoreT = [bank("a_scoreT0"), bank("a_scoreT1"), bank("a_scoreT2")]
        pv_bank = bank("a_pv_bank")
        w_loaded = ctx.enter_context(nc.semaphore("a_w_loaded"))
        padded = ctx.enter_context(nc.semaphore("a_padded"))
        stored = ctx.enter_context(nc.semaphore("a_stored"))
        block = ctx.enter_context(nc.Block())
        ident, ident_bf, ones = c["ident"], c["ident_bf"], c["ones"]
        x_tok, xT = c["x_tok"], c["xT"]
        pvT = turn[1][:, :].rearrange("p (t h s) -> p t h s", t=TILES, h=PER_GROUP)

        @block.sync
        def _(sp):
            at = 0
            for w, b_, n in (("Wq", "bq", D), ("Wk", "bk", MQA_D), ("Wv", "bv", MQA_D)):
                sp.dma_start(wqkv[:, at:at + n], weights[w]).then_inc(w_loaded, 16)
                sp.dma_start(bqkv[:, at:at + n], weights[b_].rearrange("(a n) -> a n", a=1)).then_inc(w_loaded, 16)
                at += n
            sp.dma_start(wo[:, :], weights["Wo"]).then_inc(w_loaded, 16)
            sp.dma_start(bo[:, :], weights["bo"].rearrange("(a n) -> a n", a=1)).then_inc(w_loaded, 16)
            sp.wait_ge(w_loaded, 16 * 8)
            with sp.Fori(0, B) as b:
                sp.wait_ge(w_loaded, 16 * 8)
                sp.wait_ge(e["x2"].sem, e["x2"].at(1, b))
                sp.dma_start(residual[:, bass.ds(b * TILES, TILES), :], x_tok[:, bass.ds(b * TILES, TILES), :])\
                    .then_inc(stored, 16)
            sp.wait_ge(stored, 16 * B)

        @block.gpsimd
        def _(pool):
            nc.gpsimd.memset(va[:, :, :], 0.0)
            nc.gpsimd.memset(qa[:, :, :, :].bitcast(F32), 0.0)
            nc.gpsimd.memset(ka[:, :, :, :].bitcast(F32), 0.0).then_inc(padded, 1)
            pool.wait_ge(padded, 1)
            nc.gpsimd.memset(ka[:, :, :, 24:26].bitcast(F32), 1.0)
            nc.gpsimd.memset(va[:, :, MQA_D:MQA_D + 1], 1.0).then_inc(padded, 1)
            with pool.Fori(0, B) as b:
                for k in range(3):
                    pool.wait_ge(e["var"].sem, e["var"].at(k + 1, b))
                    nc.gpsimd.tensor_tensor(rstd[:, k, :], var[:, k, :], c["minus_half"][:, 0:TILES],
                                            ALU.pow).then_inc(e["rstd"].sem, 1)

        @block.tensor
        def _(pe):
            pe.wait_ge(w_loaded, 16 * 8)
            pe.wait_ge(padded, 2)

            def scores(b, g, i):
                for qt in range(TILES):
                    s = (g * PER_GROUP + i) * TILES + qt
                    n = P * (qt + 1)
                    out = score[s % 2]
                    pe.wait_ge(e["s_max"].sem, e["s_max"].at(s - 1, b))
                    nc.tensor.matmul(out[:, 0:n], qT0[32 * i:32 * i + 32, g, qt * P:(qt + 1) * P],
                                     kT[32 * i:32 * i + 32, 0:n], start=True, stop=False)
                    nc.tensor.matmul(out[:, n - P:n], ident_bf[:, :], c["mask_qk"][:, :],
                                     start=False, stop=True).then_inc(e["s_full"].sem, 1)

            def scoresT(b, g, i):
                h = g * PER_GROUP + i
                for n_bank, tiles in enumerate(PROB_BANKS):
                    pe.wait_ge(e["exp"].sem, e["exp"].at(3 * h + n_bank - 2, b))
                    at = 0
                    for kt in tiles:
                        n = S - kt * P
                        out = scoreT[n_bank]
                        nc.tensor.matmul(out[:, at:at + n], kT[32 * i:32 * i + 32, kt * P:(kt + 1) * P],
                                         qT1[32 * i:32 * i + 32, g, kt * P:S], start=True, stop=False)
                        last = nc.tensor.matmul(out[:, at:at + P], ident_bf[:, :], c["mask_kq"][:, :],
                                                start=False, stop=True)
                        at += n
                    last.then_inc(e["st_full"].sem, 1)

            def weighted_values(b, h):
                rows = slice(32 * (h % PER_GROUP), 32 * (h % PER_GROUP) + 32)
                pe.wait_ge(e["exp"].sem, e["exp"].at(3 * (h + 1), b))
                if h % PER_GROUP == 0:
                    pe.wait_ge(e["pv"].sem, e["pv"].at(h // PER_GROUP, b))
                for kt in range(TILES):
                    last = nc.tensor.matmul(pv_bank[rows, kt * P:S], va[:, kt, :],
                                            probs[:, h % 2, PROB_AT[kt]:PROB_AT[kt] + S - kt * P],
                                            start=(kt == 0), stop=(kt == TILES - 1))
                last.then_inc(e["pv_full"].sem, 1)

            def turn_values(b, g):
                pe.wait_ge(e["pv"].sem, e["pv"].at(g + 1, b))
                pe.wait_ge(e["attn"].sem, e["attn"].at(g, b))
                for t in range(TILES):
                    last = nc.tensor.transpose(turn[1][:, t * P:(t + 1) * P], pv[:, t * P:(t + 1) * P], ident[:, :])
                last.then_inc(e["pvT_full"].sem, 1)

            with pe.Fori(0, B) as b:
                pe.wait_ge(e["xn"].sem, e["xn"].at(1, b))
                pe.wait_ge(e["yT"].sem, e["yT"].at(0, b))
                for t in range(TILES):
                    last = nc.tensor.transpose(turn[0][:, t * P:(t + 1) * P], xn[:, t, :], ident[:, :])
                last.then_inc(e["xnT_full"].sem, 1)
                pe.wait_ge(e["xnT"].sem, e["xnT"].at(1, b))
                pe.wait_ge(e["o"].sem, e["o"].at(0, b))
                for u in range(2):
                    for t in (2 * u, 2 * u + 1):
                        out = turn[1 - u][:, (t % 2) * QKV_W:(t % 2 + 1) * QKV_W]
                        nc.tensor.matmul(out, xnT[:, t * P:(t + 1) * P], wqkv[:, :], start=True, stop=False)
                        last = nc.tensor.matmul(out, ones[0:1, 0:P], bqkv[0:1, :], start=False, stop=True)
                    last.then_inc(e["qkv_full"].sem, 1)
                pe.wait_ge(e["lo"].sem, e["lo"].at(2, b))
                for t in range(TILES):
                    last = nc.tensor.transpose(turn[1][:, t * P:(t + 1) * P],
                                               ka[:, t, :, :].bitcast(F32).rearrange("p r s -> p (r s)"), ident[:, :])
                last.then_inc(e["t1_full"].sem, 1)
                for g in range(GROUPS):
                    if g >= 1:
                        pe.wait_ge(e["t1"].sem, e["t1"].at(g, b))
                    for t in range(TILES):
                        last = nc.tensor.transpose(
                            turn[g % 2][:, t * P:(t + 1) * P],
                            qa[:, t, g * PER_GROUP:(g + 1) * PER_GROUP, :].bitcast(F32).rearrange("p r s -> p (r s)"),
                            ident[:, :])
                    last.then_inc(e["t1_full"].sem, 1)
                pe.wait_ge(e["t1"].sem, e["t1"].at(5, b))
                for i in range(PER_GROUP):
                    scores(b, 0, i)
                for g in range(GROUPS):
                    pe.wait_ge(e["m"].sem, e["m"].at(g + 1, b))
                    for t in range(TILES):
                        last = nc.tensor.transpose(
                            turn[0][:, t * P:(t + 1) * P],
                            qa[:, t, g * PER_GROUP:(g + 1) * PER_GROUP, :].bitcast(F32).rearrange("p r s -> p (r s)"),
                            ident[:, :])
                    last.then_inc(e["t2_full"].sem, 1)
                    pe.wait_ge(e["t2"].sem, e["t2"].at(g + 1, b))
                    for i in range(PER_GROUP):
                        scoresT(b, g, i)
                        if g + 1 < GROUPS:
                            scores(b, g + 1, i)
                        h = g * PER_GROUP + i
                        if h > PER_GROUP and i == 1:
                            turn_values(b, g - 1)
                        if h >= 1:
                            weighted_values(b, h - 1)
                weighted_values(b, MQA_H - 1)
                turn_values(b, GROUPS - 1)
                pe.wait_ge(e["attn"].sem, e["attn"].at(GROUPS, b))
                for t in range(TILES):
                    last = nc.tensor.transpose(turn[0][:, t * P:(t + 1) * P], attn[:, t, :], ident[:, :])
                last.then_inc(e["oT_full"].sem, 1)
                pe.wait_ge(e["oT"].sem, e["oT"].at(1, b))
                for t in range(TILES):
                    out = turn[1][:, t * P:(t + 1) * P]
                    nc.tensor.matmul(out, attnT[:, t * P:(t + 1) * P], wo[:, :], start=True, stop=False)
                    last = nc.tensor.matmul(out, ones[0:1, 0:P], bo[0:1, :], start=False, stop=True)
                last.then_inc(e["proj"].sem, 1)
                pe.wait_ge(e["y"].sem, e["y"].at(1, b))
                for t in range(TILES):
                    last = nc.tensor.transpose(turn[0][:, t * P:(t + 1) * P], y[:, t, :], ident[:, :])
                last.then_inc(e["yT_full"].sem, 1)

        @block.scalar
        def _(act):
            act.wait_ge(padded, 2)

            def copy(out, in_):
                return nc.scalar.activation(out, in_, ACT.Copy)

            def exps(b, h):
                for n_bank, (at, n) in enumerate(((0, 512), (512, 512), (1024, 256))):
                    act.wait_ge(e["st_full"].sem, e["st_full"].at(3 * h + n_bank + 1, b))
                    if n_bank == 0:
                        act.wait_ge(e["pv_full"].sem, e["pv_full"].at(h - 1, b))
                    nc.scalar.activation(probs[:, h % 2, at:at + n], scoreT[n_bank][:, 0:n], ACT.Exp,
                                         scale=SCORE_SCALE).then_inc(e["exp"].sem, 1)

            with act.Fori(0, B) as b:
                act.wait_ge(e["xnT_full"].sem, e["xnT_full"].at(1, b))
                copy(xnT[:, :], turn[0][:, :]).then_inc(e["xnT"].sem, 1)
                for u in range(2):
                    act.wait_ge(e["qkv_full"].sem, e["qkv_full"].at(u + 1, b))
                    qkv = turn[1 - u][:, 0:2 * QKV_W].rearrange("p (t n) -> p t n", t=2)
                    two = slice(2 * u, 2 * u + 2)
                    q = qkv[:, :, 0:D].rearrange("p t (h d) -> p t h d", d=MQA_D)
                    k = qkv[:, :, D:D + MQA_D].unsqueeze(2).broadcast_to([P, 2, PER_GROUP, MQA_D])
                    copy(qa[:, two, :, 0:8], q)
                    copy(qa[:, two, :, 16:24], q)
                    copy(ka[:, two, :, 0:8], k)
                    copy(ka[:, two, :, 8:16], k)
                    copy(va[:, two, 0:8], qkv[:, :, D + MQA_D:QKV_W]).then_inc(e["hi"].sem, 1)
                for k in range(5):
                    act.wait_ge(e["t1_full"].sem, e["t1_full"].at(k + 1, b))
                    copy(kT[:, :] if k == 0 else qT0[:, k - 1, :], turn[(k + 1) % 2][:, :]).then_inc(e["t1"].sem, 1)
                for g in range(GROUPS):
                    act.wait_ge(e["t2_full"].sem, e["t2_full"].at(g + 1, b))
                    copy(qT1[:, g, :], turn[0][:, :]).then_inc(e["t2"].sem, 1)
                    for i in range(PER_GROUP):
                        exps(b, g * PER_GROUP + i)
                        if g >= 1 and i == 0:
                            act.wait_ge(e["pv_full"].sem, e["pv_full"].at(g * PER_GROUP, b))
                            copy(pv[:, :], pv_bank[:, :]).then_inc(e["pv"].sem, 1)
                act.wait_ge(e["pv_full"].sem, e["pv_full"].at(MQA_H, b))
                copy(pv[:, :], pv_bank[:, :]).then_inc(e["pv"].sem, 1)
                act.wait_ge(e["oT_full"].sem, e["oT_full"].at(1, b))
                copy(attnT[:, :], turn[0][:, :]).then_inc(e["oT"].sem, 1)
                act.wait_ge(e["yT_full"].sem, e["yT_full"].at(1, b))
                copy(xT[:, b, :], turn[0][:, :]).then_inc(e["yT"].sem, 1)

        @block.vector
        def _(dve):
            dve.wait_ge(padded, 2)

            def mean_and_var(b, norm, tiles, after=None):
                half = norm % 2
                dve.wait_ge(padded, 2)
                if after:
                    dve.wait_ge(e[after].sem, e[after].at(1, b))
                for t, tile in enumerate(tiles):
                    last = nc.vector.bn_stats(stat6[:, half, t, :], tile)
                last.then_inc(e["stats"].sem, 1)
                dve.wait_ge(e["stats"].sem, e["stats"].at(2 * norm + 1, b))
                nc.vector.memset(carrier[:, :], 0.0)
                for t in range(TILES):
                    last = nc.vector.bn_aggr(stat[:, norm, t, :], stat6[:, half, t, :])
                last.then_inc(e["stats"].sem, 1)
                dve.wait_ge(e["stats"].sem, e["stats"].at(2 * norm + 2, b))
                nc.vector.tensor_scalar(var[:, norm, :], stat[:, norm, :, 1], LN_EPS, None,
                                        ALU.add).then_inc(e["var"].sem, 1)
                dve.wait_ge(e["rstd"].sem, e["rstd"].at(norm + 1, b))

            def normalised(norm, out, tiles):
                for t, tile in enumerate(tiles):
                    last = nc.vector.tensor_scalar(out[:, t, :], tile, stat[:, norm, t, 0:1], rstd[:, norm, t:t + 1],
                                                   ALU.subtract, ALU.mult)
                return last

            def weighted(b, g):
                dve.wait_ge(e["pvT_full"].sem, e["pvT_full"].at(g + 1, b))
                nc.vector.reciprocal(recip[:, g, :, :], pvT[:, :, :, MQA_D]).then_inc(e["recip"].sem, 1)
                dve.wait_ge(e["recip"].sem, e["recip"].at(g + 1, b))
                width = PER_GROUP * MQA_D
                nc.vector.tensor_tensor(
                    attn[:, :, g * width:(g + 1) * width].rearrange("p t (h d) -> p t h d", d=MQA_D),
                    pvT[:, :, :, 0:MQA_D], recip[:, g, :, :].unsqueeze(3).broadcast_to([P, TILES, PER_GROUP, MQA_D]),
                    ALU.mult).then_inc(e["attn"].sem, 1)

            with dve.Fori(0, B) as b:
                tiles = [x_tok[:, b * TILES + t, :] for t in range(TILES)]
                four = x_tok[:, bass.ds(b * TILES, TILES), :]
                mean_and_var(b, 0, tiles)
                normalised(0, xn, tiles).then_inc(e["xn"].sem, 1)
                for u in range(2):
                    dve.wait_ge(e["hi"].sem, e["hi"].at(u + 1, b))
                    qkv = turn[1 - u][:, 0:2 * QKV_W].rearrange("p (t n) -> p t n", t=2)
                    two = slice(2 * u, 2 * u + 2)
                    q = qkv[:, :, 0:D].rearrange("p t (h d) -> p t h d", d=MQA_D)
                    k = qkv[:, :, D:D + MQA_D].unsqueeze(2).broadcast_to([P, 2, PER_GROUP, MQA_D])
                    nc.vector.tensor_tensor(qa[:, two, :, 8:16], q, qa[:, two, :, 0:8].bitcast(F32), ALU.subtract)
                    nc.vector.memset(qa[:, two, :, 24:26].bitcast(F32), 0.0)
                    nc.vector.tensor_tensor(ka[:, two, :, 16:24], k, ka[:, two, :, 0:8].bitcast(F32),
                                            ALU.subtract).then_inc(e["lo"].sem, 1)
                for g in range(GROUPS):
                    for i in range(PER_GROUP):
                        for qt in range(TILES):
                            h = g * PER_GROUP + i
                            s = h * TILES + qt
                            dve.wait_ge(e["s_full"].sem, e["s_full"].at(s + 1, b))
                            nc.vector.tensor_reduce(row_max[:, qt, h:h + 1], score[s % 2][:, 0:P * (qt + 1)], AX.X,
                                                    ALU.max).then_inc(e["s_max"].sem, 1)
                        if g >= 2 and i == 1:
                            weighted(b, g - 2)
                    heads = slice(g * PER_GROUP, (g + 1) * PER_GROUP)
                    dve.wait_ge(e["s_max"].sem, e["s_max"].at((g + 1) * PER_GROUP * TILES, b))
                    nc.vector.tensor_scalar(qa[:, :, heads, 24], row_max[:, :, heads], -1.0, None,
                                            ALU.mult).then_inc(e["m_hi"].sem, 1)
                    dve.wait_ge(e["m_hi"].sem, e["m_hi"].at(g + 1, b))
                    nc.vector.scalar_tensor_tensor(out=qa[:, :, heads, 25], in0=row_max[:, :, heads], scalar=-1.0,
                                                   in1=qa[:, :, heads, 24].bitcast(F32), op0=ALU.mult,
                                                   op1=ALU.subtract).then_inc(e["m"].sem, 1)
                weighted(b, GROUPS - 2)
                weighted(b, GROUPS - 1)
                projected = [turn[1][:, t * P:(t + 1) * P] for t in range(TILES)]
                mean_and_var(b, 1, projected, "proj")
                normalised(1, o, projected).then_inc(e["o"].sem, 1)
                dve.wait_ge(e["o"].sem, e["o"].at(1, b))
                nc.vector.tensor_tensor(four, four, o[:, :, :], ALU.add).then_inc(e["x2"].sem, 1)
                mean_and_var(b, 2, tiles, "x2")
                normalised(2, y, tiles).then_inc(e["y"].sem, 1)


QKV = 3 * INNER
CHUNK = 512
HEADS_C = CHUNK // DH
PAIRS = H // 2
KEYS = WINDOW + P
PAD = P - WINDOW
SCORE_GROUPS = ((0, 2, 4), (1, 3, 5), (6, 8, 10), (7, 9, 11), (12, 14), (13, 15))
GROUP_END = (3, 6, 9, 12, 14, 16)
LOADS = 10 + 2 * FC + 2

SLOT = (("O", 0), ("S", 0), ("P", 0), ("S", 1), ("O", 1), ("P", 1), ("S", 2), ("W",), ("P", 2), ("T", 0), ("S", 3),
        ("P", 3), ("X", 0), ("T", 1), ("S", 4), ("XP", 0), ("X", 1), ("P", 4), ("V", 0), ("T", 2), ("S", 5),
        ("P", 5), ("T", 3), ("X", 2), ("XP", 1), ("X", 3), ("V", 1))
FFN_AT = {(0, 27): ("F0",), (1, 3): ("F1",), (1, 12): ("F2",), (1, 24): ("F3",), (2, 1): ("G", 0), (2, 8): ("A", 0),
          (2, 16): ("G", 1), (2, 22): ("A", 1), (3, 2): ("G", 2), (3, 8): ("A", 2), (3, 16): ("F4",)}
TAIL = (("O", 0), ("O", 1), ("W",), ("F0",), ("F1",), ("F2",), ("F3",), ("G", 0), ("A", 0), ("G", 1), ("A", 1),
        ("G", 2), ("A", 2), ("F4",))


def steps_of(kind):
    steps = []
    for t in range(TILES):
        if t == TILES - 1 and kind != "last":
            steps.append((("XS",), t))
        for n, step in enumerate(SLOT):
            skip = (step[0] in "OW" and t == 0 and kind == "first") or \
                   (step[0] in "PT" and t == TILES - 1 and kind == "last") or (step[0] == "XP" and t == 0)
            if not skip:
                steps.append((step, t))
            if kind != "first" and (t, n + 1) in FFN_AT:
                steps.append((FFN_AT[(t, n + 1)], t))
    if kind == "last":
        steps += [(step, TILES) for step in TAIL]
    return steps


def layer_events(sem):
    return {
        "xs_hi": Events(sem("xs_hi"), 1), "xs": Events(sem("xs"), 1), "proj_full": Events(sem("proj_full"), 6 * TILES),
        "square": Events(sem("square"), 4 * TILES), "rotated": Events(sem("rotated"), 4 * TILES),
        "sums": Events(sem("sums"), 4 * TILES), "floor": Events(sem("floor"), 4 * TILES),
        "added": Events(sem("added"), 2 * TILES), "norm": Events(sem("norm"), 4 * TILES),
        "qk": Events(sem("qk"), 4 * TILES), "v": Events(sem("v"), 2 * TILES),
        "qkT_full": Events(sem("qkT_full"), 4 * TILES), "qkT": Events(sem("qkT"), 4 * TILES),
        "s_full": Events(sem("s_full"), 6 * TILES), "row_max": Events(sem("row_max"), 6 * TILES),
        "bias": Events(sem("bias"), 6 * TILES), "exp": Events(sem("exp"), H * TILES),
        "pT_full": Events(sem("pT_full"), 4 * TILES), "pT": Events(sem("pT"), 4 * TILES),
        "ppT_full": Events(sem("ppT_full"), 2 * TILES - 2), "ppT": Events(sem("ppT"), 2 * TILES - 2),
        "pv_full": Events(sem("pv_full"), 2 * TILES), "recip": Events(sem("recip"), 2 * TILES),
        "attn": Events(sem("attn"), 2 * TILES),
        "oT_full": Events(sem("oT_full"), 2 * TILES), "oT": Events(sem("oT"), 2 * TILES),
        "w_full": Events(sem("w_full"), TILES), "x_mid": Events(sem("x_mid"), TILES),
        "xf": Events(sem("xf"), 1), "mean_full": Events(sem("mean_full"), 1), "centred": Events(sem("centred"), 1),
        "f_square": Events(sem("f_square"), 1), "var_full": Events(sem("var_full"), 1), "f_var": Events(sem("f_var"), 1),
        "f_rstd": Events(sem("f_rstd"), 1), "diag": Events(sem("diag"), 1), "spread_full": Events(sem("spread_full"), 1),
        "xn": Events(sem("xn"), 1), "xn_hi": Events(sem("xn_hi"), 1), "xn_lo": Events(sem("xn_lo"), 1),
        "gate_full": Events(sem("gate_full"), FC), "gelu": Events(sem("gelu"), FC),
        "up_full": Events(sem("up_full"), FC), "gated": Events(sem("gated"), FC),
        "y_full": Events(sem("y_full"), 1), "x_new": Events(sem("x_new"), 1),
    }


def layers_stage(nc, c, e, w, tables_in):
    with ExitStack() as ctx:
        def sb(name, shape, dt=F32):
            return ctx.enter_context(nc.sbuf_tensor(name, shape, dt))

        def bank(name):
            return ctx.enter_context(nc.psum_tensor(name, [P, 512], F32))

        def sem(name):
            return ctx.enter_context(nc.semaphore(name))

        in_qkv, in_wo = sb("in_qkv", [P, QKV]), sb("in_wo", [P, INNER // P, D])
        in_w1, in_w2 = sb("in_w1", [P, 2, FC * P]), sb("in_w2", [P, FC, D])
        in_b1, in_g, in_b = sb("in_b1", [P, 2, FC]), sb("in_g", [P, 1]), sb("in_b", [P, 1])
        in_qs, in_ks = sb("in_qs", [P, DH]), sb("in_ks", [P, DH])
        qkv_hi, qkv_lo = sb("qkv_hi", [P, QKV], F32R), sb("qkv_lo", [P, QKV], F32R)
        wo = sb("wo", [P, INNER // P, D])
        w1 = sb("w1", [P, 2, FC * P])
        w1_hi, w1_lo = sb("w1_hi", [P, 2, FC * P], F32R), sb("w1_lo", [P, 2, FC * P], F32R)
        b1, w2 = sb("b1", [P, 2 * FC]), sb("w2", [P, FC, D])
        tables = sb("tables_sb", [P, 4, TILES, DH])
        turns = sb("turns", [P, 4, TILES, DH])
        xs_hi, xs_lo = sb("xs_hib", [P, S], F32R), sb("xs_lob", [P, S], F32R)
        squares = sb("squares", [P, 2, CHUNK])
        sums, norms = sb("sumsb", [P, 2, 4, HEADS_C]), sb("norms", [P, 2, 4, HEADS_C])
        by_cos, by_sin = sb("by_cos", [P, 2, CHUNK]), sb("by_sin", [P, 2, CHUNK])
        qk = sb("qkb", [P, 2, CHUNK])
        qT = sb("qT", [P, 2, PAIRS, P])
        kT = sb("kT", [P, PAIRS, S])
        v = sb("vb", [P, TILES, INNER])
        row_max, bias = sb("row_maxb", [P, 2, 3]), sb("biasb", [P, 2, 16])
        probs = sb("probs", [P, 2, PAD + H * KEYS])
        row_sum, recip = sb("row_sum", [P, 2, H]), sb("recipb", [P, 2, HEADS_C])
        pT, ppT = sb("pTb", [P, 2, 4, P]), sb("ppTb", [P, 2, HEADS_C, WINDOW])
        attn, attnT = sb("attnb", [P, 2, CHUNK]), sb("attnT", [P, INNER // P, P])
        xf, xc, xn = sb("xfb", [P, S]), sb("xcb", [P, S]), sb("xnb", [P, S])
        fsq = xn
        xn_hi, xn_lo = sb("xn_hib", [P, S], F32R), sb("xn_lob", [P, S], F32R)
        f_var, f_rstd = sb("f_varb", [P, TILES]), sb("f_rstdb", [P, TILES])
        carrier = sb("carrier", [P, 1])
        gate, hidden = sb("gateb", [P, 2, S]), sb("hidden", [P, FC, S])
        diag = gate[:, 0, :].rearrange("p (t n) -> p t n", t=TILES)
        proj = [bank("proj0"), bank("proj1")]
        score = [bank("score0"), bank("score1")]
        turn = [bank("turn0"), bank("turn1")]
        pv_bank, out_bank = bank("pv_bank"), bank("out_bank")
        loaded, padded, tables_loaded = sem("loaded"), sem("padded"), sem("tables_loaded")
        p_hi, p_scaled, p_pool = sem("p_hi"), sem("p_scaled"), sem("p_pool")
        p_w1_hi, p_bias_full, p_ready = sem("p_w1_hi"), sem("p_bias_full"), sem("p_ready")
        block = ctx.enter_context(nc.Block())
        ident, ident_bf, ones = c["ident"], c["ident_bf"], c["ones"]
        xT = c["xT"]
        pv_v = pv_bank[:, :].rearrange("p (h d) -> p h d", d=DH)

        def at(name, t, k, cyc):
            return e[name].at(t * (e[name].per // TILES) + k, cyc)

        def wait_tile(eng, name, t, k, cyc):
            eng.wait_ge(e[name].sem, at(name, t, k, cyc))

        def wait(eng, name, k, cyc):
            eng.wait_ge(e[name].sem, e[name].at(k, cyc))

        def prev_parts(t, k):
            return 2 * (t - 1) + k

        def run_layer(eng, layer, before, step, next_cycle=lambda: None):
            before(layer)
            for s_, t in steps_of("first"):
                step(s_, t, layer * B, 0)
            next_cycle()
            with eng.Fori(1, B - 1) as b:
                cyc = eng.snap(layer * B + b)
                for s_, t in steps_of("middle"):
                    step(s_, t, cyc, b)
            next_cycle()
            for s_, t in steps_of("last"):
                step(s_, t, layer * B + (B - 1), B - 1)

        @block.sync
        def _(sp):
            for k in range(4):
                sp.dma_start(tables[:, k, :, :], tables_in[k].rearrange("(t p) d -> p t d", p=P)).then_inc(tables_loaded, 16)
            sp.wait_ge(padded, 2)
            with sp.Fori(0, DEPTH) as layer:
                sp.wait_ge(padded, 2)
                sp.wait_ge(p_ready, layer * 4)
                one = bass.ds(layer, 1)
                flat = lambda x: x.rearrange("a n -> (a n)")

                def load(out, in_):
                    sp.dma_start(out, in_).then_inc(loaded, 16)

                for k in range(2):
                    half = slice(k * QKV // 2, (k + 1) * QKV // 2)
                    load(in_qkv[:, half], w["Wqkv"][one, :, half].rearrange("a k n -> (a k) n"))
                load(in_wo[:, :, :], w["Wo"][one].rearrange("a (c p) n -> p (a c) n", p=P))
                for k in range(2):
                    load(in_w1[:, k, 0:FF], w["W1"][one, :, k * FF:(k + 1) * FF].rearrange("a k n -> (a k) n"))
                    for j in range(FC):
                        n = P if j < FC - 1 else FR
                        load(in_b1[0:n, k, j:j + 1],
                             flat(w["b1"][one, k * FF + j * P:k * FF + j * P + n]).rearrange("(n a) -> n a", a=1))
                load(in_w2[:, 0:FC - 1, :], w["W2"][one, 0:(FC - 1) * P, :].rearrange("a (c p) n -> p (a c) n", p=P))
                load(in_w2[0:FR, FC - 1, :], w["W2"][one, (FC - 1) * P:FF, :].rearrange("a p n -> (a p) n"))
                load(in_w2[BIAS_ROW:BIAS_ROW + 1, FC - 1, :], w["b2"][one])
                load(in_g[:, :], flat(w["ln_g"][one]).rearrange("(n a) -> n a", a=1))
                load(in_b[:, :], flat(w["ln_b"][one]).rearrange("(n a) -> n a", a=1))
                load(in_qs[:, :], w["q_scale"][one].broadcast_to([P, DH]))
                load(in_ks[:, :], w["k_scale"][one].broadcast_to([P, DH]))
            sp.wait_ge(loaded, DEPTH * 16 * LOADS)

        @block.gpsimd
        def _(pool):
            nc.gpsimd.memset(xs_hi[:, 0:1].bitcast(F32), 0.0)
            nc.gpsimd.memset(xs_lo[:, 0:1].bitcast(F32), 0.0)
            nc.gpsimd.memset(xf[:, 0:1], 0.0)
            nc.gpsimd.memset(in_w1[:, :, :], 0.0)
            nc.gpsimd.memset(in_w2[:, FC - 1, :], 0.0)
            nc.gpsimd.memset(in_b1[:, :, :], 0.0)
            nc.gpsimd.memset(hidden[:, FC - 1, :], 0.0)
            for k in range(2):
                last = nc.gpsimd.memset(probs[:, k, 0:PAD], 0.0)
            last.then_inc(padded, 1)
            pool.wait_ge(padded, 1)
            nc.gpsimd.memset(hidden[BIAS_ROW:BIAS_ROW + 1, FC - 1, :], 1.0).then_inc(padded, 1)

            def before(layer):
                pool.wait_ge(loaded, layer * (16 * LOADS) + 16 * LOADS)
                wait(pool, "x_new", 0, layer * B)
                nc.gpsimd.tensor_tensor(carrier[:, :], c["minus_half"][:, 0:1], c["minus_half"][:, 0:1], ALU.mult)
                nc.gpsimd.tensor_copy(wo[:, :, :], in_wo[:, :, :])
                nc.gpsimd.tensor_copy(w2[:, :, :], in_w2[:, :, :]).then_inc(p_ready, 1)
                for j in range(4):
                    step(("P", j), -1, layer * B, 0)

            def step(s_, t, cyc, b):
                kind, k = s_[0], s_[-1]
                if kind == "P" and k < 4:
                    m, j = t + 1, k % 2
                    wait_tile(pool, "floor", m, k + 1, cyc)
                    nc.gpsimd.tensor_tensor(norms[:, m % 2, k, :], sums[:, m % 2, k, :], c["minus_half"][:, 0:HEADS_C],
                                            ALU.pow).then_inc(e["norm"].sem, 1)
                    wait_tile(pool, "rotated", m, k + 1, cyc)
                    wait_tile(pool, "qkT_full", m, k - 1, cyc)
                    if k < 2:
                        nc.gpsimd.tensor_tensor(qk[:, j, :], by_cos[:, j, :], by_sin[:, j, :],
                                                ALU.add).then_inc(e["qk"].sem, 1)
                    else:
                        nc.gpsimd.tensor_tensor(by_cos[:, j, :], by_cos[:, j, :], by_sin[:, j, :],
                                                ALU.add).then_inc(e["added"].sem, 1)
                        wait_tile(pool, "added", m, k - 1, cyc)
                        heads = by_cos[:, j, :].rearrange("p (h d) -> p h d", d=DH)
                        nc.gpsimd.tensor_tensor(
                            qk[:, j, :].rearrange("p (h d) -> p h d", d=DH), heads,
                            norms[:, m % 2, k, :].unsqueeze(2).broadcast_to([P, HEADS_C, DH]),
                            ALU.mult).then_inc(e["qk"].sem, 1)
                elif kind == "F2":
                    wait(pool, "f_var", 1 if t == TILES else 0, cyc)
                    nc.gpsimd.tensor_tensor(f_rstd[:, :], f_var[:, :], c["minus_half"][:, 0:TILES],
                                            ALU.pow).then_inc(e["f_rstd"].sem, 1)

            with pool.Fori(0, DEPTH) as layer:
                run_layer(pool, layer, before, step)

        @block.tensor
        def _(pe):
            pe.wait_ge(padded, 2)
            user = {}

            def free(name, cyc):
                kind, t, k = user[name]
                if kind == "ppT":
                    pe.wait_ge(e["ppT"].sem, e["ppT"].at(prev_parts(t, k), cyc))
                else:
                    wait_tile(pe, kind, t, k, cyc)

            def next_cycle():
                for name, (kind, t, k) in user.items():
                    user[name] = (kind, t - TILES, k)

            def before(layer):
                pe.wait_ge(loaded, layer * (16 * LOADS) + 16 * LOADS)
                wait(pe, "x_new", 0, layer * B)
                for k in range(2):
                    for j in range(FC):
                        n = k * FC + j
                        last = nc.tensor.matmul(out_bank[:, n:n + 1], in_w1[:, k, j * P:(j + 1) * P], in_b[:, :],
                                                start=True, stop=True)
                last.then_inc(p_bias_full, 1)
                user["out"] = ("x_new", 0, 0)
                user["turn0"], user["turn1"] = ("oT", -1, 1), ("oT", -1, 2)
                pe.wait_ge(p_ready, layer * 4 + 4)
                for j in range(6):
                    step(("P", j), -1, layer * B, 0)
                    if j >= 2:
                        step(("T", j - 2), -1, layer * B, 0)

            def step(s_, t, cyc, b):
                kind, k = s_[0], s_[-1]
                if kind == "P":
                    m = t + 1
                    if k == 0 and m % TILES == 0:
                        wait(pe, "xs", m // TILES + 1, cyc)
                    if k in (0, 1):
                        wait_tile(pe, "v", m, k - 1, cyc)
                    else:
                        wait_tile(pe, "rotated", m, k - 1, cyc)
                    tile = slice((m % TILES) * P, (m % TILES + 1) * P)
                    cols = slice(k * CHUNK, (k + 1) * CHUNK)
                    out = proj[k % 2][:, :]
                    nc.tensor.matmul(out, xs_hi[:, tile], qkv_hi[:, cols], start=True, stop=False)
                    nc.tensor.matmul(out, xs_hi[:, tile], qkv_lo[:, cols], start=False, stop=False)
                    nc.tensor.matmul(out, xs_lo[:, tile], qkv_hi[:, cols], start=False,
                                     stop=True).then_inc(e["proj_full"].sem, 1)
                elif kind == "T":
                    m = t + 1
                    free(f"turn{k % 2}", cyc)
                    wait_tile(pe, "qk", m, k + 1, cyc)
                    for i in range(4):
                        last = nc.tensor.transpose(turn[k % 2][:, i * P:(i + 1) * P], qk[:, k % 2, i * P:(i + 1) * P],
                                                   ident[:, :])
                    last.then_inc(e["qkT_full"].sem, 1)
                    user[f"turn{k % 2}"] = ("qkT", m, k + 1)
                elif kind == "S":
                    heads = SCORE_GROUPS[k]
                    n = len(heads)
                    if k == 0:
                        wait_tile(pe, "qkT", t, 4, cyc)
                    if k < 2:
                        wait_tile(pe, "exp", t - 1, GROUP_END[k + 4], cyc)
                    else:
                        wait_tile(pe, "exp", t, GROUP_END[k - 2], cyc)
                    first = 0 if t else WINDOW
                    out = score[k % 2][:, 0:n * KEYS].rearrange("p (h k) -> p h k", k=KEYS)
                    nc.tensor.matmul(out[:, :, first:], ident_bf[:, :], c["mask_band"][:, 0:n, first:],
                                     start=True, stop=False)
                    for i, h in enumerate(heads):
                        rows = slice((h % 2) * DH, (h % 2 + 1) * DH)
                        last = nc.tensor.matmul(out[:, i, first:], qT[rows, t % 2, h // 2, :],
                                                kT[rows, h // 2, t * P - WINDOW + first:(t + 1) * P],
                                                start=False, stop=(i == n - 1))
                    last.then_inc(e["s_full"].sem, 1)
                elif kind == "X":
                    wait_tile(pe, "exp", t, (6, 12, 12, 16)[k], cyc)
                    free(f"turn{k % 2}", cyc)
                    for i in range(4):
                        col = PAD + (4 * k + i) * KEYS + WINDOW
                        last = nc.tensor.transpose(turn[k % 2][:, i * P:(i + 1) * P], probs[:, t % 2, col:col + P],
                                                   ident[:, :])
                    last.then_inc(e["pT_full"].sem, 1)
                    user[f"turn{k % 2}"] = ("pT", t, k + 1)
                elif kind == "XP":
                    free(f"turn{k % 2}", cyc)
                    wait_tile(pe, "exp", t, (12, 16)[k], cyc)
                    for i in range(HEADS_C):
                        col = (HEADS_C * k + i) * KEYS
                        out, part = turn[k % 2][:, i * WINDOW:(i + 1) * WINDOW], probs[0:WINDOW, t % 2, col:col + P]
                        if i == 0:
                            nc.tensor.matmul(out, part, ident[0:WINDOW, 0:WINDOW], start=True, stop=True)
                        else:
                            last = nc.tensor.transpose(out, part, ident[0:WINDOW, 0:WINDOW])
                    last.then_inc(e["ppT_full"].sem, 1)
                    user[f"turn{k % 2}"] = ("ppT", t, k + 1)
                elif kind == "V":
                    wait_tile(pe, "v", t, 2, cyc)
                    wait_tile(pe, "attn", t, k, cyc)
                    if t:
                        pe.wait_ge(e["ppT"].sem, e["ppT"].at(prev_parts(t, k + 1), cyc))
                    for i in range(HEADS_C):
                        h = HEADS_C * k + i
                        if i % 4 == 0:
                            wait_tile(pe, "pT", t, h // 4 + 1, cyc)
                        cols = slice(h * DH, (h + 1) * DH)
                        last = nc.tensor.matmul(pv_v[:, i, :], pT[:, h // 4 % 2, h % 4, :], v[:, t, cols],
                                                start=True, stop=True)
                        if t:
                            last = nc.tensor.matmul(pv_v[0:WINDOW, i, :], ppT[:, k, i, :], v[:, t - 1, cols],
                                                    start=False, stop=True, skip_group_check=True)
                    last.then_inc(e["pv_full"].sem, 1)
                elif kind == "O":
                    wait_tile(pe, "attn", t - 1, k + 1, cyc)
                    free(f"turn{k}", cyc)
                    for i in range(4):
                        last = nc.tensor.transpose(turn[k][:, i * P:(i + 1) * P], attn[:, k, i * P:(i + 1) * P],
                                                   ident[:, :])
                    last.then_inc(e["oT_full"].sem, 1)
                    user[f"turn{k}"] = ("oT", t - 1, k + 1)
                elif kind == "W":
                    wait_tile(pe, "oT", t - 1, 2, cyc)
                    free_out(t, cyc)
                    for i in range(INNER // P):
                        last = nc.tensor.matmul(out_bank[:, 0:P], wo[:, i, :], attnT[:, i, :], start=(i == 0),
                                                stop=(i == INNER // P - 1))
                    last.then_inc(e["w_full"].sem, 1)
                    user["out"] = ("x_mid", t - 1, 1)
                else:
                    ffn(s_, t, cyc)

            def free_out(t, cyc):
                if t == 0:
                    wait_tile(pe, "x_mid", -1, 0, cyc)
                    wait(pe, "x_new", -1, cyc)
                else:
                    kind, tile, k = user["out"]
                    if kind == "x_mid":
                        wait_tile(pe, kind, tile, k, cyc)
                    else:
                        wait(pe, kind, k, cyc)

            def ffn(s_, t, cyc):
                kind, k = s_[0], s_[-1]
                ahead = 1 if t == TILES else 0
                if kind == "F0":
                    wait(pe, "xf", ahead, cyc)
                    free_out(t or 1, cyc)
                    nc.tensor.matmul(out_bank[:, :], c["mean_of"][:, :], xf[:, :], start=True,
                                     stop=True).then_inc(e["mean_full"].sem, 1)
                    user["out"] = ("centred", 0, ahead)
                elif kind == "F1":
                    wait(pe, "f_square", ahead, cyc)
                    free_out(t, cyc)
                    for i in range(TILES):
                        last = nc.tensor.matmul(out_bank[:, i:i + 1], fsq[:, i * P:(i + 1) * P], c["mean_of"][:, 0:1],
                                                start=True, stop=True)
                    last.then_inc(e["var_full"].sem, 1)
                    user["out"] = ("f_var", 0, ahead)
                elif kind == "F3":
                    wait(pe, "diag", ahead, cyc)
                    free_out(t, cyc)
                    nc.tensor.matmul(out_bank[:, :], ones[:, :], diag[:, :, :].rearrange("p t n -> p (t n)"), start=True,
                                     stop=True).then_inc(e["spread_full"].sem, 1)
                    user["out"] = ("xn", 0, ahead)
                elif kind in "GA":
                    part = 1 if kind == "G" else 0
                    done = ahead * FC + k + 1
                    wait(pe, "xn_lo", ahead, cyc)
                    free_out(t, cyc)
                    cols = slice(k * P, (k + 1) * P)
                    nc.tensor.matmul(out_bank[:, :], w1_hi[:, part, cols], xn_hi[:, :], start=True, stop=False)
                    nc.tensor.matmul(out_bank[:, :], w1_hi[:, part, cols], xn_lo[:, :], start=False, stop=False)
                    nc.tensor.matmul(out_bank[:, :], w1_lo[:, part, cols], xn_hi[:, :], start=False,
                                     stop=True).then_inc(e["gate_full" if part else "up_full"].sem, 1)
                    user["out"] = ("gelu" if part else "gated", 0, done - FC)
                elif kind == "F4":
                    wait(pe, "gated", ahead * FC, cyc)
                    free_out(t, cyc)
                    for j in range(FC):
                        n = P if j < FC - 1 else BIAS_ROW + 1
                        last = nc.tensor.matmul(out_bank[:, :], w2[0:n, j, :], hidden[0:n, j, :], start=(j == 0),
                                                stop=(j == FC - 1))
                    last.then_inc(e["y_full"].sem, 1)
                    user["out"] = ("x_new", 0, ahead)

            with pe.Fori(0, DEPTH) as layer:
                run_layer(pe, layer, before, step, next_cycle)

        @block.scalar
        def _(act):
            act.wait_ge(padded, 2)

            def copy(out, in_):
                return nc.scalar.activation(out, in_, ACT.Copy)

            def before(layer):
                act.wait_ge(loaded, layer * (16 * LOADS) + 16 * LOADS)
                wait(act, "x_new", 0, layer * B)
                for k in range(2):
                    half = slice(k * QKV // 2, (k + 1) * QKV // 2)
                    last = copy(qkv_hi[:, half], in_qkv[:, half])
                last.then_inc(p_hi, 1)
                shifted(1, layer * B, 0)
                act.wait_ge(p_scaled, layer + 1)
                copy(w1_hi[:, :, :], w1[:, :, :]).then_inc(p_w1_hi, 1)
                for j in range(6):
                    step(("P", j), -1, layer * B, 0)
                    if j >= 2:
                        step(("T", j - 2), -1, layer * B, 0)

            def shifted(ahead, cyc, b):
                wait_tile(act, "proj_full", 0 if ahead == 1 else TILES, 0, cyc)
                copy(xs_hi[0:P // 2, :], xT[0:P // 2, bass.ds(b, 1), :].rearrange("p a n -> p (a n)"))
                copy(xs_hi[P // 2:P, 1:S], xT[P // 2:P, bass.ds(b, 1), 0:S - 1].rearrange("p a n -> p (a n)"))\
                    .then_inc(e["xs_hi"].sem, 1)

            def step(s_, t, cyc, b):
                kind, k = s_[0], s_[-1]
                if kind == "XS":
                    shifted(2, cyc, b + 1)
                elif kind == "P":
                    m = t + 1
                    wait_tile(act, "proj_full", m, k + 1, cyc)
                    if k < 4:
                        wait_tile(act, "sums", m, k - 1, cyc)
                        nc.scalar.activation(squares[:, k % 2, :], proj[k % 2][:, :], ACT.Square)\
                            .then_inc(e["square"].sem, 1)
                    else:
                        wait_tile(act, "pv_full", m - 2, 2, cyc)
                        copy(v[:, m % TILES, (k - 4) * CHUNK:(k - 3) * CHUNK], proj[k % 2][:, :])\
                            .then_inc(e["v"].sem, 1)
                elif kind == "T":
                    m = t + 1
                    wait_tile(act, "qkT_full", m, k + 1, cyc)
                    bank_ = turn[k % 2][:, :].rearrange("p (a n) -> p a n", n=P)
                    pairs = slice((k % 2) * 4, (k % 2) * 4 + 4)
                    if k < 2:
                        wait_tile(act, "s_full", m - 2, 6, cyc)
                        out = qT[:, m % 2, pairs, :]
                    else:
                        out = kT[:, pairs, (m % TILES) * P:(m % TILES + 1) * P]
                    copy(out, bank_).then_inc(e["qkT"].sem, 1)
                elif kind == "S":
                    wait_tile(act, "bias", t, k + 1, cyc)
                    if k == 0:
                        wait_tile(act, "pT_full", t - 1, 0, cyc)
                        wait_tile(act, "recip", t - 1, 0, cyc)
                    first = 0 if t else WINDOW
                    for i, h in enumerate(SCORE_GROUPS[k]):
                        col = PAD + h * KEYS
                        nc.scalar.activation(
                            probs[:, t % 2, col + first:col + KEYS], score[k % 2][:, i * KEYS + first:(i + 1) * KEYS],
                            ACT.Exp, scale=norms[:, t % 2, h // HEADS_C, h % HEADS_C:h % HEADS_C + 1],
                            bias=bias[:, t % 2, h:h + 1], accum_out=row_sum[:, t % 2, h:h + 1]).then_inc(e["exp"].sem, 1)
                elif kind == "O":
                    wait_tile(act, "oT_full", t - 1, k + 1, cyc)
                    wait_tile(act, "w_full", t - 1, 0, cyc)
                    copy(attnT[:, 4 * k:4 * k + 4, :], turn[k][:, :].rearrange("p (a n) -> p a n", n=P))\
                        .then_inc(e["oT"].sem, 1)
                elif kind in ("F1", "F3", "G"):
                    ahead = 1 if t == TILES else 0
                    if kind == "F1":
                        wait(act, "centred", ahead, cyc)
                        nc.scalar.activation(fsq[:, :], xc[:, :], ACT.Square).then_inc(e["f_square"].sem, 1)
                    elif kind == "F3":
                        wait(act, "xn", ahead, cyc)
                        copy(xn_hi[:, :], xn[:, :]).then_inc(e["xn_hi"].sem, 1)
                    else:
                        wait(act, "gate_full", ahead * FC + k + 1 - FC, cyc)
                        wait(act, "gated", ahead * FC + k - 1 - FC, cyc)
                        n = FC + k
                        nc.scalar.activation(gate[:, k % 2, :], out_bank[:, :], ACT.Gelu, bias=b1[:, n:n + 1])\
                            .then_inc(e["gelu"].sem, 1)

            with act.Fori(0, DEPTH) as layer:
                run_layer(act, layer, before, step)

        @block.vector
        def _(dve):
            dve.wait_ge(padded, 2)
            dve.wait_ge(tables_loaded, 16 * 4)

            def before(layer):
                dve.wait_ge(loaded, layer * (16 * LOADS) + 16 * LOADS)
                wait(dve, "x_new", 0, layer * B)
                for k, scale in enumerate((in_qs, in_qs, in_ks, in_ks)):
                    nc.vector.tensor_tensor(turns[:, k, :, :], tables[:, k, :, :],
                                            scale[:, :].unsqueeze(1).broadcast_to([P, TILES, DH]), ALU.mult)
                nc.vector.tensor_scalar(w1[:, :, :], in_w1[:, :, :], in_g[:, 0:1], None, ALU.mult).then_inc(p_scaled, 1)
                dve.wait_ge(p_hi, layer + 1)
                nc.vector.tensor_tensor(qkv_lo[:, :], in_qkv[:, :], qkv_hi[:, :].bitcast(F32),
                                        ALU.subtract).then_inc(p_ready, 1)
                shifted(1, layer * B, 0)
                dve.wait_ge(p_bias_full, layer + 1)
                nc.vector.tensor_tensor(b1[:, :], out_bank[:, 0:2 * FC], in_b1[:, :, :].rearrange("p a j -> p (a j)"),
                                        ALU.add).then_inc(p_ready, 1)
                dve.wait_ge(p_w1_hi, layer + 1)
                nc.vector.tensor_tensor(w1_lo[:, :, :], w1[:, :, :], w1_hi[:, :, :].bitcast(F32),
                                        ALU.subtract).then_inc(p_ready, 1)
                for j in range(4):
                    step(("P", j), -1, layer * B, 0)

            def shifted(ahead, cyc, b):
                wait(dve, "xs_hi", ahead, cyc)
                nc.vector.tensor_tensor(xs_lo[0:P // 2, :], xT[0:P // 2, bass.ds(b, 1), :].rearrange("p a n -> p (a n)"),
                                        xs_hi[0:P // 2, :].bitcast(F32), ALU.subtract)
                nc.vector.tensor_tensor(xs_lo[P // 2:P, 1:S],
                                        xT[P // 2:P, bass.ds(b, 1), 0:S - 1].rearrange("p a n -> p (a n)"),
                                        xs_hi[P // 2:P, 1:S].bitcast(F32), ALU.subtract).then_inc(e["xs"].sem, 1)

            def step(s_, t, cyc, b):
                kind, k = s_[0], s_[-1]
                if kind == "XS":
                    shifted(2, cyc, b + 1)
                elif kind == "P" and k < 4:
                    m, j = t + 1, k % 2
                    tile = m % TILES
                    wait_tile(dve, "square", m, k + 1, cyc)
                    if k >= 2:
                        wait_tile(dve, "qk", m, k - 1, cyc)
                    else:
                        wait_tile(dve, "qk", m - 1, k + 3, cyc)
                    heads = proj[j][:, :].rearrange("p (h a d) -> p h a d", a=2, d=DH // 2)
                    which = 0 if k < 2 else 2

                    def table(n):
                        return turns[:, which + n, tile, :].rearrange("p (a d) -> p a d", a=2).unsqueeze(1)\
                            .broadcast_to([P, HEADS_C, 2, DH // 2])

                    nc.vector.tensor_tensor(by_cos[:, j, :].rearrange("p (h a d) -> p h a d", a=2, d=DH // 2), heads,
                                            table(0), ALU.mult)
                    swapped = by_sin[:, j, :].rearrange("p (h a d) -> p h a d", a=2, d=DH // 2)[:, :, ::-1, :]
                    nc.vector.tensor_tensor(swapped, heads, table(1), ALU.mult).then_inc(e["rotated"].sem, 1)
                    if k == 0:
                        wait_tile(dve, "exp", m - 2, H, cyc)
                    nc.vector.tensor_reduce(sums[:, m % 2, k, :], squares[:, j, :].rearrange("p (h d) -> p h d", d=DH),
                                            AX.X, ALU.add).then_inc(e["sums"].sem, 1)
                    wait_tile(dve, "sums", m, k + 1, cyc)
                    unit = 1.0 / (QK_SCALE * QK_SCALE) if k < 2 else 1.0
                    nc.vector.tensor_scalar(sums[:, m % 2, k, :], sums[:, m % 2, k, :], unit, L2_EPS2 * unit,
                                            ALU.mult, ALU.max).then_inc(e["floor"].sem, 1)
                elif kind == "S":
                    n = len(SCORE_GROUPS[k])
                    wait_tile(dve, "s_full", t, k + 1, cyc)
                    first = 0 if t else WINDOW
                    scores = score[k % 2][:, 0:n * KEYS].rearrange("p (h k) -> p h k", k=KEYS)[:, :, first:]
                    nc.vector.tensor_reduce(row_max[:, k % 2, 0:n], scores, AX.X, ALU.max)\
                        .then_inc(e["row_max"].sem, 1)
                    wait_tile(dve, "row_max", t, k + 1, cyc)
                    if k == 0:
                        wait_tile(dve, "norm", t, 2, cyc)
                    h = SCORE_GROUPS[k][0]
                    stop = SCORE_GROUPS[k][-1] + 1
                    scales = norms[:, t % 2, :, :].rearrange("p c h -> p (c h)")[:, h:stop:2]
                    nc.vector.scalar_tensor_tensor(out=bias[:, t % 2, h:stop:2], in0=row_max[:, k % 2, 0:n], scalar=-1.0,
                                                   in1=scales, op0=ALU.mult, op1=ALU.mult).then_inc(e["bias"].sem, 1)
                elif kind == "X":
                    wait_tile(dve, "pT_full", t, k + 1, cyc)
                    wait_tile(dve, "pv_full", t, k // 2, cyc)
                    nc.vector.tensor_copy(pT[:, k % 2, :, :].rearrange("p h q -> p (h q)"), turn[k % 2][:, :])\
                        .then_inc(e["pT"].sem, 1)
                elif kind == "XP":
                    dve.wait_ge(e["ppT_full"].sem, e["ppT_full"].at(prev_parts(t, k + 1), cyc))
                    wait_tile(dve, "pv_full", t - 1, k + 1, cyc)
                    nc.vector.tensor_copy(ppT[:, k, :, :].rearrange("p h q -> p (h q)"),
                                          turn[k % 2][:, 0:HEADS_C * WINDOW]).then_inc(e["ppT"].sem, 1)
                elif kind == "V":
                    wait_tile(dve, "exp", t, H if k else 12, cyc)
                    nc.vector.reciprocal(recip[:, k, :], row_sum[:, t % 2, k * HEADS_C:(k + 1) * HEADS_C])\
                        .then_inc(e["recip"].sem, 1)
                    wait_tile(dve, "recip", t, k + 1, cyc)
                    wait_tile(dve, "pv_full", t, k + 1, cyc)
                    wait_tile(dve, "oT_full", t - 1, k + 1, cyc)
                    nc.vector.tensor_tensor(attn[:, k, :].rearrange("p (h d) -> p h d", d=DH), pv_v[:, :, :],
                                            recip[:, k, :].unsqueeze(2).broadcast_to([P, HEADS_C, DH]),
                                            ALU.mult).then_inc(e["attn"].sem, 1)
                elif kind == "W":
                    wait_tile(dve, "w_full", t - 1, 1, cyc)
                    seq = b - 1 if t == 0 else b
                    tile = (t - 1) % TILES
                    x = xT[:, bass.ds(seq, 1), tile * P:(tile + 1) * P].rearrange("p a n -> p (a n)")
                    nc.vector.tensor_tensor(x, out_bank[:, 0:P], x, ALU.add).then_inc(e["x_mid"].sem, 1)
                elif kind in ("F0", "F1", "F2", "F3", "A", "F4"):
                    ffn(s_, t, cyc, b)

            def ffn(s_, t, cyc, b):
                kind, k = s_[0], s_[-1]
                ahead, seq = (1, b) if t == TILES else (0, b - 1)
                rows = lambda lo, hi, stop: xT[lo:hi, bass.ds(seq, 1), 0:stop].rearrange("p a n -> p (a n)")
                if kind == "F0":
                    wait_tile(dve, "x_mid", TILES * ahead, 0, cyc)
                    nc.vector.tensor_copy(xf[0:P // 2, :], rows(0, P // 2, S))
                    nc.vector.tensor_copy(xf[P // 2:P, 1:S], rows(P // 2, P, S - 1)).then_inc(e["xf"].sem, 1)
                    wait(dve, "mean_full", ahead, cyc)
                    nc.vector.tensor_tensor(xc[:, :], xf[:, :], out_bank[:, :], ALU.subtract)\
                        .then_inc(e["centred"].sem, 1)
                elif kind == "F1":
                    wait(dve, "var_full", ahead, cyc)
                    nc.vector.tensor_scalar(f_var[:, :], out_bank[:, 0:TILES], LN_EPS, None, ALU.add)\
                        .then_inc(e["f_var"].sem, 1)
                elif kind == "F2":
                    wait(dve, "f_rstd", ahead, cyc)
                    nc.vector.tensor_tensor(diag[:, :, :], ident[:, :].unsqueeze(1).broadcast_to([P, TILES, P]),
                                            f_rstd[:, :].unsqueeze(2).broadcast_to([P, TILES, P]), ALU.mult)\
                        .then_inc(e["diag"].sem, 1)
                elif kind == "F3":
                    wait(dve, "spread_full", ahead, cyc)
                    nc.vector.tensor_tensor(xn[:, :], xc[:, :], out_bank[:, :], ALU.mult).then_inc(e["xn"].sem, 1)
                    wait(dve, "xn_hi", ahead, cyc)
                    nc.vector.tensor_tensor(xn_lo[:, :], xn[:, :], xn_hi[:, :].bitcast(F32), ALU.subtract)\
                        .then_inc(e["xn_lo"].sem, 1)
                elif kind == "A":
                    n = P if k < FC - 1 else FR
                    wait(dve, "up_full", ahead * FC + k + 1 - FC, cyc)
                    wait(dve, "gelu", ahead * FC + k + 1 - FC, cyc)
                    nc.vector.scalar_tensor_tensor(out=hidden[0:n, k, :], in0=out_bank[0:n, :], scalar=b1[0:n, k:k + 1],
                                                   in1=gate[0:n, k % 2, :], op0=ALU.add, op1=ALU.mult)\
                        .then_inc(e["gated"].sem, 1)
                elif kind == "F4":
                    wait(dve, "y_full", ahead, cyc)
                    x = rows(0, P, S)
                    nc.vector.tensor_tensor(x, out_bank[:, :], x, ALU.add).then_inc(e["x_new"].sem, 1)

            with dve.Fori(0, DEPTH) as layer:
                run_layer(dve, layer, before, step)


def output_stage(nc, c, residual, out_dram):
    with ExitStack() as ctx:
        def sb(name, shape, dt=F32):
            return ctx.enter_context(nc.sbuf_tensor(name, shape, dt))

        def sem(name):
            return ctx.enter_context(nc.semaphore(name))

        held, stat6, stat = sb("o_held", [P, S]), sb("o_stat6", [P, TILES, 6]), sb("o_stat", [P, TILES, 2])
        var, rstd, o = sb("o_var", [P, TILES]), sb("o_rstd", [P, TILES]), sb("o_o", [P, TILES, D])
        x = sb("o_x", [P, B * TILES, D])
        carrier = sb("o_carrier", [P, 1])
        turn = ctx.enter_context(nc.psum_tensor("o_turn", [P, 512], F32))
        fetched, turned, stats, summed = sem("o_fetched"), sem("o_turned"), sem("o_stats"), sem("o_summed")
        var_done, rstd_done, normalised, stored = sem("o_vard"), sem("o_rstdd"), sem("o_normalised"), sem("o_stored")
        x_loaded = sem("o_x_loaded")
        block = ctx.enter_context(nc.Block())

        @block.scalar
        def _(act):
            with act.Fori(0, B) as b:
                act.wait_ge(turned, b)
                nc.scalar.activation(held[:, :], c["xT"][:, bass.ds(b, 1), :].rearrange("p a n -> p (a n)"), ACT.Copy)\
                    .then_inc(fetched, 1)

        @block.tensor
        def _(pe):
            with pe.Fori(0, B) as b:
                pe.wait_ge(fetched, b + 1)
                pe.wait_ge(normalised, b)
                for t in range(TILES):
                    last = nc.tensor.transpose(turn[:, t * P:(t + 1) * P], held[:, t * P:(t + 1) * P], c["ident"][:, :])
                last.then_inc(turned, 1)

        @block.gpsimd
        def _(pool):
            with pool.Fori(0, B) as b:
                pool.wait_ge(var_done, b + 1)
                nc.gpsimd.tensor_tensor(rstd[:, :], var[:, :], c["minus_half"][:, 0:TILES], ALU.pow).then_inc(rstd_done, 1)

        @block.vector
        def _(dve):
            dve.wait_ge(x_loaded, 16)
            with dve.Fori(0, B) as b:
                dve.wait_ge(x_loaded, 16)
                dve.wait_ge(turned, b + 1)
                for t in range(TILES):
                    last = nc.vector.bn_stats(stat6[:, t, :], turn[:, t * P:(t + 1) * P])
                last.then_inc(stats, 1)
                dve.wait_ge(stats, b * 2 + 1)
                nc.vector.memset(carrier[:, :], 0.0)
                for t in range(TILES):
                    last = nc.vector.bn_aggr(stat[:, t, :], stat6[:, t, :])
                last.then_inc(stats, 1)
                dve.wait_ge(stats, b * 2 + 2)
                nc.vector.tensor_scalar(var[:, :], stat[:, :, 1], LN_EPS, None, ALU.add).then_inc(var_done, 1)
                dve.wait_ge(rstd_done, b + 1)
                for t in range(TILES):
                    last = nc.vector.tensor_scalar(o[:, t, :], turn[:, t * P:(t + 1) * P], stat[:, t, 0:1],
                                                   rstd[:, t:t + 1], ALU.subtract, ALU.mult)
                last.then_inc(normalised, 1)
                dve.wait_ge(normalised, b + 1)
                four = x[:, bass.ds(b * TILES, TILES), :]
                nc.vector.tensor_tensor(four, four, o[:, :, :], ALU.add).then_inc(summed, 1)

        @block.sync
        def _(sp):
            sp.dma_start(x[:, :, :], residual).then_inc(x_loaded, 16)
            with sp.Fori(0, B) as b:
                sp.wait_ge(x_loaded, 16)
                sp.wait_ge(summed, b + 1)
                sp.dma_start(out_dram[bass.ds(b, 1)].rearrange("a (t p) d -> p (a t) d", p=P),
                             x[:, bass.ds(b * TILES, TILES), :]).then_inc(stored, 16)
            sp.wait_ge(stored, 16 * B)


def program(nc, a, out_dram):
    with ExitStack() as ctx:
        def sb(name, shape, dt=F32):
            return ctx.enter_context(nc.sbuf_tensor(name, shape, dt))

        def sem(name):
            return ctx.enter_context(nc.semaphore(name))

        c = {
            "xT": sb("xT", [P, B, S]),
            "ident": sb("ident", [P, P]), "ident_bf": sb("ident_bf", [P, P], BF16),
            "ones": sb("ones", [P, P]), "mean_of": sb("mean_of", [P, P]), "minus_half": sb("minus_half", [P, 8]),
            "mask_qk": sb("mask_qk", [P, P], BF16), "mask_kq": sb("mask_kq", [P, P], BF16),
            "mask_band": sb("mask_band", [P, 3, KEYS], BF16),
        }
        mqa, layers = mqa_events(sem), layer_events(sem)
        residual = nc.dram_tensor("residual", (P, B * TILES, D), F32, kind="Internal").ap()
        with nc.sbuf_tensor("x_tok", [P, B * TILES, D], F32) as x_tok:
            c["x_tok"] = x_tok
            constants_stage(nc, c, a["L0_attn_x"], list(mqa.values()) + list(layers.values()))
            mqa_stage(nc, c, mqa, {n: a["L0_attn_" + n] for n in ("Wq", "bq", "Wk", "bk", "Wv", "bv", "Wo", "bo")},
                      residual)
        layers_stage(nc, c, layers, {n: a["L0_ffn_" + n] for n in FFN_INPUTS}, a["tables"])
        output_stage(nc, c, residual, out_dram)


FFN_INPUTS = ("Wqkv", "q_scale", "k_scale", "Wo", "ln_g", "ln_b", "W1", "b1", "W2", "b2")


def kernel(**inputs):
    import concourse.bacc as bacc
    from concourse.bass_utils import run_bass_kernel_spmd

    nc = bacc.Bacc("TRN2", target_bir_lowering=False, num_devices=1)
    arrays = {name: np.ascontiguousarray(a) for name, a in inputs.items()}
    arrays["tables"] = rotary_tables()
    args = {n: nc.dram_tensor(n, a.shape, mybir.dt.from_np(a.dtype), kind="ExternalInput").ap()
            for n, a in arrays.items()}
    out = nc.dram_tensor("out", (B, S, D), F32, kind="ExternalOutput").ap()
    program(nc, args, out)
    return run_bass_kernel_spmd(nc, [arrays], core_ids=[0]).results[0]["out"]
```

```python
from contextlib import ExitStack

import numpy as np

import concourse.bass as bass
from concourse import mybir
from concourse.alu_op_type import AluOpType as ALU

ACT = mybir.ActivationFunctionType
AX = mybir.AxisListType
F32 = mybir.dt.float32
F32R = mybir.dt.float32r
BF16 = mybir.dt.bfloat16

P = 128
B, S, D = 8, 512, 128
TILES = S // P
MQA_H, MQA_D = 16, 8
DEPTH, H, DH = 6, 16, 64
INNER = H * DH
WINDOW = 32
FF = int(D * 4 * 2 / 3)
FC = -(-FF // P)
FR = FF - (FC - 1) * P
BIAS_ROW = 96
QK_SCALE = 8.0
MASKED = -1e30
LN_EPS = 1e-5
L2_EPS2 = 1e-24


class Events:

    def __init__(self, semaphore, per):
        self.sem, self.per = semaphore, per

    def at(self, k, cycle):
        return cycle * self.per + (self.per + k)


def rotary_tables():
    half = np.arange(0, DH, 2, dtype=np.float32)
    inv_freq = (np.float32(1.0) / np.power(np.float32(10000.0), half / np.float32(DH))).astype(np.float32)
    t = np.arange(S, dtype=np.float32)
    freqs = (t[:, None] * inv_freq[None, :]).astype(np.float32)
    base = ((half + np.float32(0.4 * DH)) / np.float32(1.4 * DH)).astype(np.float32)
    power = ((t - S // 2) / np.float32(WINDOW // 2)).astype(np.float32)
    scale = np.power(base[None, :].astype(np.float64), power[:, None].astype(np.float64))
    cos, sin = np.cos(freqs.astype(np.float64)), np.sin(freqs.astype(np.float64))
    both = lambda a, b: np.concatenate([a, b], -1)
    return np.stack([both(cos * scale, cos * scale), both(sin * scale, -sin * scale),
                     both(cos / scale, cos / scale), both(sin / scale, -sin / scale)]).astype(np.float32)


def constants_stage(nc, c, x_in, credits):
    with ExitStack() as ctx:
        zeroed = ctx.enter_context(nc.semaphore("zeroed"))
        selected = ctx.enter_context(nc.semaphore("selected"))
        loaded = ctx.enter_context(nc.semaphore("loaded"))
        block = ctx.enter_context(nc.Block())

        @block.sync
        def _(sp):
            for b in range(B):
                sp.dma_start(c["x_tok"][:, b * TILES:(b + 1) * TILES, :],
                             x_in[b].rearrange("(t p) d -> p t d", p=P)).then_inc(loaded, 16)
            for e in credits:
                sp.sem_inc(e.sem, e.per)
            sp.wait_ge(loaded, 16 * B)

        @block.vector
        def _(dve):
            nc.vector.memset(c["ones"][:, :], 1.0)
            nc.vector.memset(c["mean_of"][:, :], 1.0 / D)
            nc.vector.memset(c["minus_half"][:, :], -0.5)
            nc.vector.memset(c["ident"][:, :], 0.0)
            nc.vector.memset(c["ident_bf"][:, :], 0.0)
            nc.vector.memset(c["mask_qk"][:, :], 0.0)
            nc.vector.memset(c["mask_kq"][:, :], 0.0)
            nc.vector.memset(c["mask_band"][:, :, :], 0.0).then_inc(zeroed, 1)

        @block.gpsimd
        def _(pool):
            pool.wait_ge(zeroed, 1)
            step = [0]

            def select(out, pattern, compare, base, fill, channel):
                nc.gpsimd.affine_select(out=out, in_=out, compare_op=compare, fill=fill, base=base,
                                        pattern=pattern, channel_multiplier=channel).then_inc(selected, 1)
                step[0] += 1
                pool.wait_ge(selected, step[0])

            select(c["ident"][:, :], [[-1, P]], ALU.not_equal, 0, 1.0, 1)
            select(c["ident_bf"][:, :], [[-1, P]], ALU.not_equal, 0, 1.0, 1)
            select(c["mask_qk"][:, :], [[-1, P]], ALU.is_ge, 0, MASKED, 1)
            select(c["mask_kq"][:, :], [[1, P]], ALU.is_ge, 0, MASKED, -1)
            select(c["mask_band"][:, :, :], [[0, 3], [-1, WINDOW + P]], ALU.is_ge, WINDOW, MASKED, 1)
            select(c["mask_band"][:, :, :], [[0, 3], [1, WINDOW + P]], ALU.is_ge, 0, MASKED, -1)


SLOTS = 32
AHEAD = 5
GROUPS = MQA_H * SLOTS // P
PER_GROUP = MQA_H // GROUPS
QKV_W = D + 2 * MQA_D
SCORE_SCALE = float(np.float32(1.0) / np.sqrt(np.float32(MQA_D)))
PROB_AT = {0: 0, 1: 512, 3: 896, 2: 1024}
PROB_BANKS = ((0,), (1, 3), (2,))
PROBS_W = 1280


def mqa_events(sem):
    return {
        **{f"{name}{k}": Events(sem(f"a_{name}{k}"), n) for name, n in (("stats", 2), ("var", 1), ("rstd", 1))
           for k in range(3)},
        "kv": Events(sem("a_kv"), 1),
        "xn": Events(sem("a_xn"), 1), "xnT_full": Events(sem("a_xnT_full"), 1), "xnT": Events(sem("a_xnT"), 1),
        "qkv_full": Events(sem("a_qkv_full"), 2), "hi": Events(sem("a_hi"), 2), "lo": Events(sem("a_lo"), 2),
        "t1_full": Events(sem("a_t1_full"), 5), "t1": Events(sem("a_t1"), 5),
        "s_full": Events(sem("a_s_full"), MQA_H * TILES), "s_max": Events(sem("a_s_max"), MQA_H * TILES),
        "m_hi": Events(sem("a_m_hi"), GROUPS), "m": Events(sem("a_m"), GROUPS),
        "t2_full": Events(sem("a_t2_full"), GROUPS), "t2": Events(sem("a_t2"), GROUPS),
        "st_full": Events(sem("a_st_full"), 3 * MQA_H), "exp": Events(sem("a_exp"), 3 * MQA_H),
        "pv_full": Events(sem("a_pv_full"), MQA_H), "pv": Events(sem("a_pv"), GROUPS),
        "pvT_full": Events(sem("a_pvT_full"), GROUPS), "recip": Events(sem("a_recip"), GROUPS),
        "attn": Events(sem("a_attn"), GROUPS),
        "oT_full": Events(sem("a_oT_full"), 1), "oT": Events(sem("a_oT"), 1), "proj": Events(sem("a_proj"), 1),
        "o": Events(sem("a_o"), 1), "x2": Events(sem("a_x2"), 1), "y": Events(sem("a_y"), 1),
        "yT_full": Events(sem("a_yT_full"), 1), "yT": Events(sem("a_yT"), 1),
    }


def mqa_stage(nc, c, e, weights, residual):
    with ExitStack() as ctx:
        def sb(name, shape, dt=F32):
            return ctx.enter_context(nc.sbuf_tensor(name, shape, dt))

        def bank(name):
            return ctx.enter_context(nc.psum_tensor(name, [P, 512], F32))

        wqkv = sb("a_wqkv", [P, QKV_W])
        bqkv = sb("a_bqkv", [1, QKV_W])
        wo, bo = sb("a_wo", [P, D]), sb("a_bo", [1, D])
        stat6, stat = sb("a_stat6", [P, 3, TILES, 6]), sb("a_stat", [P, 3, TILES, 2])
        var, rstd = sb("a_varb", [P, 3, TILES]), sb("a_rstdb", [P, 3, TILES])
        xn, xnT = sb("a_xnb", [P, TILES, D]), sb("a_xnTb", [P, S])
        qa = sb("a_qa", [P, TILES, MQA_H, SLOTS], F32R)
        ka = sb("a_ka", [P, TILES, PER_GROUP, SLOTS], F32R)
        va = sb("a_va", [P, TILES, SLOTS])
        qT0 = sb("a_qT0", [P, GROUPS, S], F32R)
        qT1 = sb("a_qT1", [P, GROUPS, S], F32R)
        kT = sb("a_kT", [P, S], F32R)
        kT1 = sb("a_kT1", [P, S], F32R)
        v_next = sb("a_v_next", [P, TILES, MQA_D])
        row_max = sb("a_row_max", [P, TILES, MQA_H])
        probs = sb("a_probs", [P, 2, PROBS_W])
        pv = sb("a_pvb", [P, S])
        recip = sb("a_recipb", [P, GROUPS, TILES, PER_GROUP])
        attn, attnT = sb("a_attnb", [P, TILES, D]), sb("a_attnTb", [P, S])
        o, y = sb("a_ob", [P, TILES, D]), sb("a_yb", [P, TILES, D])
        carrier = sb("a_carrier", [P, 1])
        turn = [bank("a_turn0"), bank("a_turn1")]
        score = [bank("a_score0"), bank("a_score1")]
        scoreT = [bank("a_scoreT0"), bank("a_scoreT1"), bank("a_scoreT2")]
        pv_bank = bank("a_pv_bank")
        w_loaded = ctx.enter_context(nc.semaphore("a_w_loaded"))
        padded = ctx.enter_context(nc.semaphore("a_padded"))
        stored = ctx.enter_context(nc.semaphore("a_stored"))
        block = ctx.enter_context(nc.Block())
        ident, ident_bf, ones = c["ident"], c["ident_bf"], c["ones"]
        x_tok, xT = c["x_tok"], c["xT"]
        pvT = turn[1][:, :].rearrange("p (t h s) -> p t h s", t=TILES, h=PER_GROUP)

        def each(eng, sequence, next_sequence=lambda: None):
            sequence(0, first=True)
            next_sequence()
            with eng.Fori(1, B - 1) as b:
                sequence(b)
            next_sequence()
            sequence(B - 1, last=True)

        @block.sync
        def _(sp):
            at = 0
            for w, b_, n in (("Wq", "bq", D), ("Wk", "bk", MQA_D), ("Wv", "bv", MQA_D)):
                sp.dma_start(wqkv[:, at:at + n], weights[w]).then_inc(w_loaded, 16)
                sp.dma_start(bqkv[:, at:at + n], weights[b_].rearrange("(a n) -> a n", a=1)).then_inc(w_loaded, 16)
                at += n
            sp.dma_start(wo[:, :], weights["Wo"]).then_inc(w_loaded, 16)
            sp.dma_start(bo[:, :], weights["bo"].rearrange("(a n) -> a n", a=1)).then_inc(w_loaded, 16)
            sp.wait_ge(w_loaded, 16 * 8)
            with sp.Fori(0, B) as b:
                sp.wait_ge(w_loaded, 16 * 8)
                sp.wait_ge(e["x2"].sem, e["x2"].at(1, b))
                sp.dma_start(residual[:, bass.ds(b * TILES, TILES), :], x_tok[:, bass.ds(b * TILES, TILES), :])\
                    .then_inc(stored, 16)
            sp.wait_ge(stored, 16 * B)

        @block.gpsimd
        def _(pool):
            nc.gpsimd.memset(va[:, :, :], 0.0)
            nc.gpsimd.memset(qa[:, :, :, :].bitcast(F32), 0.0)
            nc.gpsimd.memset(ka[:, :, :, :].bitcast(F32), 0.0).then_inc(padded, 1)
            pool.wait_ge(padded, 1)
            nc.gpsimd.memset(ka[:, :, :, 24:26].bitcast(F32), 1.0)
            nc.gpsimd.memset(va[:, :, MQA_D:MQA_D + 1], 1.0).then_inc(padded, 1)

            def inverse_deviation(norm, b):
                pool.wait_ge(e[f"var{norm}"].sem, e[f"var{norm}"].at(1, b))
                nc.gpsimd.tensor_tensor(rstd[:, norm, :], var[:, norm, :], c["minus_half"][:, 0:TILES],
                                        ALU.pow).then_inc(e[f"rstd{norm}"].sem, 1)

            def sequence(b, first=False, last=False):
                if not first:
                    inverse_deviation(1, b - 1)
                    inverse_deviation(2, b - 1)
                if not last:
                    inverse_deviation(0, b + 1)

            inverse_deviation(0, 0)
            each(pool, sequence)
            inverse_deviation(1, B - 1)
            inverse_deviation(2, B - 1)

        @block.tensor
        def _(pe):
            pe.wait_ge(w_loaded, 16 * 8)
            pe.wait_ge(padded, 2)

            def scores(b, g, i, qt):
                s = (g * PER_GROUP + i) * TILES + qt
                n = P * (qt + 1)
                out = score[s % 2]
                pe.wait_ge(e["s_max"].sem, e["s_max"].at(s - 1, b))
                nc.tensor.matmul(out[:, 0:n], qT0[32 * i:32 * i + 32, g, qt * P:(qt + 1) * P],
                                 kT[32 * i:32 * i + 32, 0:n], start=True, stop=False)
                nc.tensor.matmul(out[:, n - P:n], ident_bf[:, :], c["mask_qk"][:, :],
                                 start=False, stop=True).then_inc(e["s_full"].sem, 1)

            def scoresT(b, g, i, n_bank):
                h = g * PER_GROUP + i
                pe.wait_ge(e["exp"].sem, e["exp"].at(3 * h + n_bank - 2, b))
                at = 0
                for kt in PROB_BANKS[n_bank]:
                    n = S - kt * P
                    out = scoreT[n_bank]
                    nc.tensor.matmul(out[:, at:at + n], kT1[32 * i:32 * i + 32, kt * P:(kt + 1) * P],
                                     qT1[32 * i:32 * i + 32, g, kt * P:S], start=True, stop=False)
                    last = nc.tensor.matmul(out[:, at:at + P], ident_bf[:, :], c["mask_kq"][:, :],
                                            start=False, stop=True)
                    at += n
                last.then_inc(e["st_full"].sem, 1)

            def weighted_values(b, h, kt):
                rows = slice(32 * (h % PER_GROUP), 32 * (h % PER_GROUP) + 32)
                if kt == 0:
                    pe.wait_ge(e["exp"].sem, e["exp"].at(3 * (h + 1), b))
                    if h % PER_GROUP == 0:
                        pe.wait_ge(e["pv"].sem, e["pv"].at(h // PER_GROUP, b))
                last = nc.tensor.matmul(pv_bank[rows, kt * P:S], va[:, kt, :],
                                        probs[:, h % 2, PROB_AT[kt]:PROB_AT[kt] + S - kt * P],
                                        start=(kt == 0), stop=(kt == TILES - 1))
                if kt == TILES - 1:
                    last.then_inc(e["pv_full"].sem, 1)

            def turn_with_max(b, g):
                pe.wait_ge(e["m"].sem, e["m"].at(g + 1, b))
                turned(b, 0, stacked(g), "t2_full", ("t2", g + 1, 0))

            def head(b, shifted=None, for_max=None, weighted=None, between=None):
                for what, k in (("T", 0), ("S", 0), ("T", 1), ("S", 1), ("V", 0), ("T", 2), ("S", 2), ("V", 1),
                                ("S", 3), ("V", 2), ("V", 3)):
                    if what == "T" and shifted:
                        scoresT(b, *shifted, k)
                    elif what == "S" and for_max:
                        scores(*for_max, k)
                    elif what == "V" and weighted is not None:
                        weighted_values(b, weighted, k)
                    if (what, k) == ("S", 1) and between:
                        between()

            user = {}

            def free(bank_, b):
                if bank_ in user:
                    name, k, ahead = user[bank_]
                    pe.wait_ge(e[name].sem, e[name].at(k, b + ahead))

            def next_sequence():
                for bank_, (name, k, ahead) in user.items():
                    user[bank_] = (name, k, ahead - 1)

            def turned(b, bank_, sources, full, used):
                free(bank_, b)
                for t, source in enumerate(sources):
                    last = nc.tensor.transpose(turn[bank_][:, t * P:(t + 1) * P], source, ident[:, :])
                last.then_inc(e[full].sem, 1)
                user[bank_] = used

            def turn_values(b, g):
                pe.wait_ge(e["pv"].sem, e["pv"].at(g + 1, b))
                turned(b, 1, [pv[:, t * P:(t + 1) * P] for t in range(TILES)], "pvT_full", ("attn", g + 1, 0))

            def turn_xn(b):
                pe.wait_ge(e["xn"].sem, e["xn"].at(1, b + 1))
                turned(b, 0, [xn[:, t, :] for t in range(TILES)], "xnT_full", ("xnT", 1, 1))

            def project(b, u):
                pe.wait_ge(e["xnT"].sem, e["xnT"].at(1, b + 1))
                free(0, b)
                for t in (2 * u, 2 * u + 1):
                    out = turn[0][:, (t % 2) * QKV_W:(t % 2 + 1) * QKV_W]
                    nc.tensor.matmul(out, xnT[:, t * P:(t + 1) * P], wqkv[:, :], start=True, stop=False)
                    last = nc.tensor.matmul(out, ones[0:1, 0:P], bqkv[0:1, :], start=False, stop=True)
                last.then_inc(e["qkv_full"].sem, 1)
                user[0] = ("lo", u + 1, 1)

            def stacked(g):
                return [qa[:, t, g * PER_GROUP:(g + 1) * PER_GROUP, :].bitcast(F32).rearrange("p r s -> p (r s)")
                        for t in range(TILES)]

            def turn_keys(b):
                pe.wait_ge(e["lo"].sem, e["lo"].at(2, b + 1))
                turned(b, 0, [ka[:, t, :, :].bitcast(F32).rearrange("p r s -> p (r s)") for t in range(TILES)],
                       "t1_full", ("t1", 1, 1))

            def turn_queries(b, g):
                turned(b, 0, stacked(g), "t1_full", ("t1", g + 2, 1))

            def turn_attn(b):
                pe.wait_ge(e["attn"].sem, e["attn"].at(GROUPS, b))
                turned(b, 0, [attn[:, t, :] for t in range(TILES)], "oT_full", ("oT", 1, 0))

            def project_out(b):
                pe.wait_ge(e["oT"].sem, e["oT"].at(1, b))
                free(1, b)
                for t in range(TILES):
                    out = turn[1][:, t * P:(t + 1) * P]
                    nc.tensor.matmul(out, attnT[:, t * P:(t + 1) * P], wo[:, :], start=True, stop=False)
                    last = nc.tensor.matmul(out, ones[0:1, 0:P], bo[0:1, :], start=False, stop=True)
                last.then_inc(e["proj"].sem, 1)
                user[1] = ("o", 1, 0)

            def turn_y(b, ahead):
                pe.wait_ge(e["y"].sem, e["y"].at(1, b + ahead))
                turned(b, 0, [y[:, t, :] for t in range(TILES)], "yT_full", ("yT", 1, ahead))

            def sequence(b, first=False, last=False):
                pe.wait_ge(e["kv"].sem, e["kv"].at(1, b))
                pe.wait_ge(e["t1"].sem, e["t1"].at(5, b))
                for g in range(GROUPS):
                    pe.wait_ge(e["t2"].sem, e["t2"].at(g + 1, b))
                    for i in range(PER_GROUP):
                        h = g * PER_GROUP + i
                        then = h + AHEAD
                        head(b, shifted=(g, i), weighted=h - 1 if h else None,
                             for_max=(b, then // PER_GROUP, then % PER_GROUP) if then < MQA_H else None,
                             between=(lambda: turn_with_max(b, g + 1)) if i == 3 and g + 1 < GROUPS else None)
                        if h > PER_GROUP and i == 1:
                            turn_values(b, g - 1)
                        if (g, i) == (1, 1) and not first:
                            turn_y(b, -1)
                        if last:
                            continue
                        if (g, i) == (2, 2):
                            turn_xn(b)
                        elif g == 3 and i < 2:
                            project(b, i)
                        elif (g, i) == (3, 2):
                            turn_keys(b)
                        elif (g, i) == (3, 3):
                            turn_queries(b, 0)
                if last:
                    head(b, weighted=MQA_H - 1)
                    turn_values(b, GROUPS - 1)
                    turn_attn(b)
                    project_out(b)
                    turn_y(b, 0)
                    return
                pe.wait_ge(e["t1"].sem, e["t1"].at(2, b + 1))
                head(b, for_max=(b + 1, 0, 0), weighted=MQA_H - 1)
                turn_values(b, GROUPS - 1)
                turn_queries(b, 1)
                head(b, for_max=(b + 1, 0, 1))
                turn_attn(b)
                turn_queries(b, 2)
                head(b, for_max=(b + 1, 0, 2))
                project_out(b)
                head(b, for_max=(b + 1, 0, 3))
                turn_queries(b, 3)
                head(b, for_max=(b + 1, 1, 0), between=lambda: turn_first(b))

            def turn_first(b):
                pe.wait_ge(e["m"].sem, e["m"].at(1, b + 1))
                turned(b, 0, stacked(0), "t2_full", ("t2", 1, 1))

            turn_xn(-1)
            for u in range(2):
                project(-1, u)
            turn_keys(-1)
            for g in range(GROUPS):
                turn_queries(-1, g)
            pe.wait_ge(e["t1"].sem, e["t1"].at(3, 0))
            for i in range(PER_GROUP):
                head(-1, for_max=(0, 0, i))
            head(-1, for_max=(0, 1, 0), between=lambda: turn_first(-1))
            next_sequence()
            each(pe, sequence, next_sequence)

        @block.scalar
        def _(act):
            act.wait_ge(padded, 2)

            def copy(out, in_):
                return nc.scalar.activation(out, in_, ACT.Copy)

            def exps(b, h):
                for n_bank, (at, n) in enumerate(((0, 512), (512, 512), (1024, 256))):
                    act.wait_ge(e["st_full"].sem, e["st_full"].at(3 * h + n_bank + 1, b))
                    if n_bank == 0:
                        act.wait_ge(e["pv_full"].sem, e["pv_full"].at(h - 1, b))
                    nc.scalar.activation(probs[:, h % 2, at:at + n], scoreT[n_bank][:, 0:n], ACT.Exp,
                                         scale=SCORE_SCALE).then_inc(e["exp"].sem, 1)

            def turned_input(b):
                act.wait_ge(e["xnT_full"].sem, e["xnT_full"].at(1, b + 1))
                copy(xnT[:, :], turn[0][:, :]).then_inc(e["xnT"].sem, 1)

            def hi_parts(b, u):
                act.wait_ge(e["qkv_full"].sem, e["qkv_full"].at(u + 1, b + 1))
                qkv = turn[0][:, 0:2 * QKV_W].rearrange("p (t n) -> p t n", t=2)
                two = slice(2 * u, 2 * u + 2)
                q = qkv[:, :, 0:D].rearrange("p t (h d) -> p t h d", d=MQA_D)
                k = qkv[:, :, D:D + MQA_D].unsqueeze(2).broadcast_to([P, 2, PER_GROUP, MQA_D])
                copy(qa[:, two, :, 0:8], q)
                copy(qa[:, two, :, 16:24], q)
                copy(ka[:, two, :, 0:8], k)
                copy(ka[:, two, :, 8:16], k)
                copy(v_next[:, two, :], qkv[:, :, D + MQA_D:QKV_W]).then_inc(e["hi"].sem, 1)

            def first_turned(b, k):
                act.wait_ge(e["t1_full"].sem, e["t1_full"].at(k + 1, b + 1))
                copy(kT[:, :] if k == 0 else qT0[:, k - 1, :], turn[0][:, :]).then_inc(e["t1"].sem, 1)

            def keys_and_values(b):
                act.wait_ge(e["t1"].sem, e["t1"].at(1, b + 1))
                copy(kT1[:, :], kT[:, :].bitcast(F32))
                copy(va[:, :, 0:MQA_D], v_next[:, :, :]).then_inc(e["kv"].sem, 1)

            def values_group(b, g):
                act.wait_ge(e["pv_full"].sem, e["pv_full"].at((g + 1) * PER_GROUP, b))
                copy(pv[:, :], pv_bank[:, :]).then_inc(e["pv"].sem, 1)

            def attn_turned(b):
                act.wait_ge(e["oT_full"].sem, e["oT_full"].at(1, b))
                copy(attnT[:, :], turn[0][:, :]).then_inc(e["oT"].sem, 1)

            def output_turned(b):
                act.wait_ge(e["yT_full"].sem, e["yT_full"].at(1, b))
                out = xT[:, b, :] if isinstance(b, int) else xT[:, bass.ds(b, 1), :].rearrange("p a n -> p (a n)")
                copy(out, turn[0][:, :]).then_inc(e["yT"].sem, 1)

            def turned_with_max(b, g):
                act.wait_ge(e["t2_full"].sem, e["t2_full"].at(g + 1, b))
                copy(qT1[:, g, :], turn[0][:, :]).then_inc(e["t2"].sem, 1)

            def sequence(b, first=False, last=False):
                for g in range(GROUPS):
                    for i in range(PER_GROUP):
                        exps(b, g * PER_GROUP + i)
                        if i == 3 and g + 1 < GROUPS:
                            turned_with_max(b, g + 1)
                        if g >= 1 and i == 0:
                            values_group(b, g - 1)
                        if (g, i) == (1, 1) and not first:
                            output_turned(b - 1)
                        if last:
                            continue
                        if (g, i) == (2, 2):
                            turned_input(b)
                        elif g == 3 and i < 2:
                            hi_parts(b, i)
                        elif g == 3:
                            first_turned(b, i - 2)
                values_group(b, GROUPS - 1)
                if last:
                    attn_turned(b)
                    output_turned(b)
                    return
                keys_and_values(b)
                first_turned(b, 2)
                attn_turned(b)
                first_turned(b, 3)
                first_turned(b, 4)
                turned_with_max(b + 1, 0)

            turned_input(-1)
            for u in range(2):
                hi_parts(-1, u)
            for k in range(5):
                first_turned(-1, k)
            keys_and_values(-1)
            turned_with_max(0, 0)
            each(act, sequence)

        @block.vector
        def _(dve):
            dve.wait_ge(padded, 2)

            def mean_and_var(b, norm, tiles, after=None):
                stats = e[f"stats{norm}"]
                dve.wait_ge(padded, 2)
                if after:
                    dve.wait_ge(e[after].sem, e[after].at(1, b))
                for t, tile in enumerate(tiles):
                    last = nc.vector.bn_stats(stat6[:, norm, t, :], tile)
                last.then_inc(stats.sem, 1)
                dve.wait_ge(stats.sem, stats.at(1, b))
                nc.vector.memset(carrier[:, :], 0.0)
                for t in range(TILES):
                    last = nc.vector.bn_aggr(stat[:, norm, t, :], stat6[:, norm, t, :])
                last.then_inc(stats.sem, 1)
                dve.wait_ge(stats.sem, stats.at(2, b))
                nc.vector.tensor_scalar(var[:, norm, :], stat[:, norm, :, 1], LN_EPS, None,
                                        ALU.add).then_inc(e[f"var{norm}"].sem, 1)

            def normalised(b, norm, out, tiles):
                dve.wait_ge(e[f"rstd{norm}"].sem, e[f"rstd{norm}"].at(1, b))
                for t, tile in enumerate(tiles):
                    last = nc.vector.tensor_scalar(out[:, t, :], tile, stat[:, norm, t, 0:1], rstd[:, norm, t:t + 1],
                                                   ALU.subtract, ALU.mult)
                return last

            def weighted(b, g):
                dve.wait_ge(e["pvT_full"].sem, e["pvT_full"].at(g + 1, b))
                nc.vector.reciprocal(recip[:, g, :, :], pvT[:, :, :, MQA_D]).then_inc(e["recip"].sem, 1)
                dve.wait_ge(e["recip"].sem, e["recip"].at(g + 1, b))
                width = PER_GROUP * MQA_D
                nc.vector.tensor_tensor(
                    attn[:, :, g * width:(g + 1) * width].rearrange("p t (h d) -> p t h d", d=MQA_D),
                    pvT[:, :, :, 0:MQA_D], recip[:, g, :, :].unsqueeze(3).broadcast_to([P, TILES, PER_GROUP, MQA_D]),
                    ALU.mult).then_inc(e["attn"].sem, 1)

            def lo_parts(b, u):
                dve.wait_ge(e["hi"].sem, e["hi"].at(u + 1, b + 1))
                qkv = turn[0][:, 0:2 * QKV_W].rearrange("p (t n) -> p t n", t=2)
                two = slice(2 * u, 2 * u + 2)
                q = qkv[:, :, 0:D].rearrange("p t (h d) -> p t h d", d=MQA_D)
                k = qkv[:, :, D:D + MQA_D].unsqueeze(2).broadcast_to([P, 2, PER_GROUP, MQA_D])
                nc.vector.tensor_tensor(qa[:, two, :, 8:16], q, qa[:, two, :, 0:8].bitcast(F32), ALU.subtract)
                nc.vector.memset(qa[:, two, :, 24:26].bitcast(F32), 0.0)
                nc.vector.tensor_tensor(ka[:, two, :, 16:24], k, ka[:, two, :, 0:8].bitcast(F32),
                                        ALU.subtract).then_inc(e["lo"].sem, 1)

            def maxima(b, g, i):
                for qt in range(TILES):
                    h = g * PER_GROUP + i
                    s = h * TILES + qt
                    dve.wait_ge(e["s_full"].sem, e["s_full"].at(s + 1, b))
                    nc.vector.tensor_reduce(row_max[:, qt, h:h + 1], score[s % 2][:, 0:P * (qt + 1)], AX.X,
                                            ALU.max).then_inc(e["s_max"].sem, 1)

            def negated_maxima(b, g):
                heads = slice(g * PER_GROUP, (g + 1) * PER_GROUP)
                dve.wait_ge(e["s_max"].sem, e["s_max"].at((g + 1) * PER_GROUP * TILES, b))
                dve.wait_ge(e["t1_full"].sem, e["t1_full"].at(g + 2, b))
                nc.vector.tensor_scalar(qa[:, :, heads, 24], row_max[:, :, heads], -1.0, None,
                                        ALU.mult).then_inc(e["m_hi"].sem, 1)
                dve.wait_ge(e["m_hi"].sem, e["m_hi"].at(g + 1, b))
                nc.vector.scalar_tensor_tensor(out=qa[:, :, heads, 25], in0=row_max[:, :, heads], scalar=-1.0,
                                               in1=qa[:, :, heads, 24].bitcast(F32), op0=ALU.mult,
                                               op1=ALU.subtract).then_inc(e["m"].sem, 1)

            def tiles_of(b):
                return [x_tok[:, b * TILES + t, :] for t in range(TILES)]

            projected = [turn[1][:, t * P:(t + 1) * P] for t in range(TILES)]

            def add_output(b):
                dve.wait_ge(e["o"].sem, e["o"].at(1, b))
                four = x_tok[:, bass.ds(b * TILES, TILES), :]
                nc.vector.tensor_tensor(four, four, o[:, :, :], ALU.add).then_inc(e["x2"].sem, 1)

            def sequence(b, first=False, last=False):
                for g in range(GROUPS):
                    for i in range(PER_GROUP):
                        then = g * PER_GROUP + i + AHEAD
                        if then < MQA_H:
                            maxima(b, then // PER_GROUP, then % PER_GROUP)
                        if i == 2 and g + 1 < GROUPS:
                            negated_maxima(b, g + 1)
                        if g >= 1 and i == 2:
                            weighted(b, g - 1)
                        if not first:
                            if (g, i) == (0, 0):
                                mean_and_var(b - 1, 1, projected, "proj")
                            elif (g, i) == (0, 1):
                                normalised(b - 1, 1, o, projected).then_inc(e["o"].sem, 1)
                            elif (g, i) == (0, 2):
                                add_output(b - 1)
                            elif (g, i) == (0, 3):
                                mean_and_var(b - 1, 2, tiles_of(b - 1), "x2")
                            elif (g, i) == (1, 0):
                                normalised(b - 1, 2, y, tiles_of(b - 1)).then_inc(e["y"].sem, 1)
                        if last:
                            continue
                        if (g, i) == (1, 3):
                            mean_and_var(b + 1, 0, tiles_of(b + 1))
                        elif (g, i) == (2, 0):
                            normalised(b + 1, 0, xn, tiles_of(b + 1)).then_inc(e["xn"].sem, 1)
                        elif g == 3 and i < 2:
                            lo_parts(b, i)
                if last:
                    weighted(b, GROUPS - 1)
                    mean_and_var(b, 1, projected, "proj")
                    normalised(b, 1, o, projected).then_inc(e["o"].sem, 1)
                    add_output(b)
                    mean_and_var(b, 2, tiles_of(b), "x2")
                    normalised(b, 2, y, tiles_of(b)).then_inc(e["y"].sem, 1)
                    return
                for i in range(PER_GROUP):
                    maxima(b + 1, 0, i)
                    if i == 0:
                        weighted(b, GROUPS - 1)
                negated_maxima(b + 1, 0)
                maxima(b + 1, 1, 0)

            mean_and_var(0, 0, tiles_of(0))
            normalised(0, 0, xn, tiles_of(0)).then_inc(e["xn"].sem, 1)
            for u in range(2):
                lo_parts(-1, u)
            for i in range(PER_GROUP):
                maxima(0, 0, i)
            negated_maxima(0, 0)
            maxima(0, 1, 0)
            each(dve, sequence)


QKV = 3 * INNER
CHUNK = 512
HEADS_C = CHUNK // DH
PAIRS = H // 2
KEYS = WINDOW + P
PAD = P - WINDOW
SCORE_GROUPS = ((0, 2, 4), (1, 3, 5), (6, 8, 10), (7, 9, 11), (12, 14), (13, 15))
GROUP_END = (3, 6, 9, 12, 14, 16)
LOADS = 10 + 2 * FC + 2

SLOT = {
    "PE": (("P", 0), ("S", 0), ("P", 1), ("XP-", 1), ("S", 1), ("X-", 3), ("P", 2), ("S", 2), ("T", 0), ("V-", 1),
    ("P", 3), ("O", 0), ("S", 3), ("P", 4), ("T", 1), ("X", 0), ("S", 4), ("O", 1), ("P", 5), ("T", 2), ("X", 1),
    ("W",), ("XP", 0), ("S", 5), ("T", 3), ("V", 0), ("X", 2)),
    "Act": (("P", 0), ("P", 1), ("S", 0), ("S", 1), ("T", 0), ("P", 2), ("S", 2), ("P", 3), ("O", 0), ("T", 1),
    ("S", 3), ("O", 1), ("T", 2), ("P", 4), ("S", 4), ("S", 5), ("T", 3), ("P", 5)),
    "DVE": (("P", 0), ("S", 0), ("XP-", 1), ("S", 1), ("P", 1), ("X-", 3), ("S", 2), ("P", 2), ("V-", 1), ("S", 3),
    ("P", 3), ("X", 0), ("S", 4), ("W",), ("X", 1), ("XP", 0), ("S", 5), ("V", 0), ("X", 2)),
    "Pool": (("P", 0), ("P", 1), ("P", 2), ("P", 3)),
}
FFN_AT = {
    "PE": {(0, 23): [("F0",)], (1, 1): [("F1",)], (1, 24): [("F3",)], (2, 1): [("G", 0)], (2, 9): [("A", 0)], (2,
    18): [("G", 1)], (2, 22): [("A", 1)], (2, 23): [("G", 2)], (2, 27): [("A", 2)], (3, 13): [("F4",)]},
    "Act": {(0, 17): [("F1",)], (1, 17): [("F3",)], (2, 1): [("G", 0)], (2, 12): [("G", 1)], (2, 15): [("G", 2)]},
    "DVE": {(0, 15): [("F0",)], (1, 4): [("F1",)], (1, 12): [("F2",)], (1, 17): [("F3",)], (2, 7): [("A", 0)], (2,
    15): [("A", 1)], (3, 6): [("A", 2)], (3, 13): [("F4",)]},
    "Pool": {(1, 2): [("F2",)]},
}
FFN = (("F0",), ("F1",), ("F2",), ("F3",), ("G", 0), ("A", 0), ("G", 1), ("A", 1), ("G", 2), ("A", 2), ("F4",))


def steps_of(engine, kind):
    steps = []
    if kind == "start":
        steps = [(("NQ", k), -1) for k in range(6)] + [(("XS",), -1)]
        for k in range(6):
            steps += [(("P", k), -1)] + [(("T", k - 2), -1)] * (k >= 2)
        steps += [(("NO",), -1), (("NF",), -1)]
    late = [step for step in SLOT[engine] if step[0][-1] == "-"]
    for t in range(TILES):
        if t == TILES - 1 and kind == "last" and engine == "DVE":
            steps += [(("NQ", 4), t), (("NQ", 5), t)]
        if t == TILES - 1 and kind != "end":
            steps.append((("XS",), t))
        for n, step in enumerate(SLOT[engine]):
            tile = t - (step[0][-1] == "-")
            name = step[0].rstrip("-")
            skip = ((name in "OW" or tile < 0) and t == 0 and kind == "start") or \
                   (name in "PT" and t == TILES - 1 and kind == "end") or (name == "XP" and tile % TILES == 0)
            if not skip:
                steps.append(((name, *step[1:]), tile))
                if name == "P" and t == TILES - 2 and kind == "last":
                    steps.append((("NQ", step[1]), t))
                if name == "W" and t == 0 and kind == "first":
                    steps.append((("NO",), t))
            if kind != "start":
                for f in FFN_AT[engine].get((t, n + 1), ()):
                    steps.append((f, t))
        if t == 0 and kind == "first" and engine == "Pool":
            steps.append((("NO",), t))
        if t == TILES - 1 and kind == "first":
            steps.append((("NF",), t))
    if kind == "end":
        steps += [((name[:-1], k), TILES - 1) for name, k in late]
        steps += [(step, TILES) for step in (("O", 0), ("O", 1), ("W",)) + FFN]
    return steps


def layer_events(sem):
    return {
        "xs_hi": Events(sem("xs_hi"), 1), "xs": Events(sem("xs"), 1), "proj_full": Events(sem("proj_full"), 6 * TILES),
        "square": Events(sem("square"), 4 * TILES), "rotated": Events(sem("rotated"), 4 * TILES),
        "sums": Events(sem("sums"), 4 * TILES), "floor": Events(sem("floor"), 4 * TILES),
        "added": Events(sem("added"), 2 * TILES), "norm": Events(sem("norm"), 4 * TILES),
        "qk": Events(sem("qk"), 4 * TILES), "v": Events(sem("v"), 2 * TILES),
        "qkT_full": Events(sem("qkT_full"), 4 * TILES), "qkT": Events(sem("qkT"), 4 * TILES),
        "s_full": Events(sem("s_full"), 6 * TILES), "row_max": Events(sem("row_max"), 6 * TILES),
        "bias": Events(sem("bias"), 6 * TILES), "exp": Events(sem("exp"), H * TILES),
        "pT_full": Events(sem("pT_full"), 4 * TILES), "pT": Events(sem("pT"), 4 * TILES),
        "ppT_full": Events(sem("ppT_full"), 2 * TILES - 2), "ppT": Events(sem("ppT"), 2 * TILES - 2),
        "pv_full": Events(sem("pv_full"), 2 * TILES), "recip": Events(sem("recip"), 2 * TILES),
        "attn": Events(sem("attn"), 2 * TILES),
        "oT_full": Events(sem("oT_full"), 2 * TILES), "oT": Events(sem("oT"), 2 * TILES),
        "w_full": Events(sem("w_full"), TILES), "x_mid": Events(sem("x_mid"), TILES),
        "xf": Events(sem("xf"), 1), "mean_full": Events(sem("mean_full"), 1), "centred": Events(sem("centred"), 1),
        "f_square": Events(sem("f_square"), 1), "var_full": Events(sem("var_full"), 1), "f_var": Events(sem("f_var"), 1),
        "f_rstd": Events(sem("f_rstd"), 1), "diag": Events(sem("diag"), 1), "spread_full": Events(sem("spread_full"), 1),
        "xn": Events(sem("xn"), 1), "xn_hi": Events(sem("xn_hi"), 1), "xn_lo": Events(sem("xn_lo"), 1),
        "gate_full": Events(sem("gate_full"), FC), "gelu": Events(sem("gelu"), FC),
        "up_full": Events(sem("up_full"), FC), "gated": Events(sem("gated"), FC),
        "y_full": Events(sem("y_full"), 1), "x_new": Events(sem("x_new"), 1),
    }


def layers_stage(nc, c, e, w, tables_in):
    with ExitStack() as ctx:
        def sb(name, shape, dt=F32):
            return ctx.enter_context(nc.sbuf_tensor(name, shape, dt))

        def bank(name):
            return ctx.enter_context(nc.psum_tensor(name, [P, 512], F32))

        def sem(name):
            return ctx.enter_context(nc.semaphore(name))

        in_qkv, in_wo = sb("in_qkv", [P, QKV]), sb("in_wo", [P, INNER // P, D])
        in_w1, in_w2 = sb("in_w1", [P, 2, FC * P]), sb("in_w2", [P, FC, D])
        in_b1, in_g, in_b = sb("in_b1", [P, 2, FC]), sb("in_g", [P, 1]), sb("in_b", [P, 1])
        in_qs, in_ks = sb("in_qs", [P, DH]), sb("in_ks", [P, DH])
        qkv_hi, qkv_lo = sb("qkv_hi", [P, QKV], F32R), sb("qkv_lo", [P, QKV], F32R)
        wo = sb("wo", [P, INNER // P, D])
        w1 = sb("w1", [P, 2, FC * P])
        w1_hi, w1_lo = sb("w1_hi", [P, 2, FC * P], F32R), sb("w1_lo", [P, 2, FC * P], F32R)
        b1, w2 = sb("b1", [P, 2 * FC]), sb("w2", [P, FC, D])
        tables = sb("tables_sb", [P, 4, TILES, DH])
        turns = sb("turns", [P, 4, TILES, DH])
        xs_hi, xs_lo = sb("xs_hib", [P, S], F32R), sb("xs_lob", [P, S], F32R)
        squares = sb("squares", [P, 2, CHUNK])
        sums, norms = sb("sumsb", [P, 2, 4, HEADS_C]), sb("norms", [P, 2, 4, HEADS_C])
        by_cos, by_sin = sb("by_cos", [P, 2, CHUNK]), sb("by_sin", [P, 2, CHUNK])
        qk = sb("qkb", [P, 2, CHUNK])
        qT = sb("qT", [P, 2, PAIRS, P])
        kT = sb("kT", [P, PAIRS, S])
        v = sb("vb", [P, TILES, INNER])
        row_max, bias = sb("row_maxb", [P, 2, 3]), sb("biasb", [P, 2, 16])
        probs = sb("probs", [P, 2, PAD + H * KEYS])
        row_sum, recip = sb("row_sum", [P, 2, H]), sb("recipb", [P, 2, HEADS_C])
        pT, ppT = sb("pTb", [P, 2, 4, P]), sb("ppTb", [P, 2, HEADS_C, WINDOW])
        attn, attnT = sb("attnb", [P, 2, CHUNK]), sb("attnT", [P, INNER // P, P])
        xf, xc, xn = sb("xfb", [P, S]), sb("xcb", [P, S]), sb("xnb", [P, S])
        fsq = xn
        xn_hi, xn_lo = sb("xn_hib", [P, S], F32R), sb("xn_lob", [P, S], F32R)
        f_var, f_rstd = sb("f_varb", [P, TILES]), sb("f_rstdb", [P, TILES])
        gate, hidden = sb("gateb", [P, FC, S]), sb("hidden", [P, FC, S])
        diag = gate[:, 0, :].rearrange("p (t n) -> p t n", t=TILES)
        proj = [bank("proj0"), bank("proj1")]
        score = [bank("score0"), bank("score1")]
        turn = [bank("turn0"), bank("turn1")]
        pv_bank, out_bank = bank("pv_bank"), bank("out_bank")
        loaded, padded, tables_loaded = sem("loaded"), sem("padded"), sem("tables_loaded")
        p_hi, p_lo, p_wo, p_scaled = sem("p_hi"), sem("p_lo"), sem("p_wo"), sem("p_scaled")
        p_w1_hi, p_bias_full, p_bias, p_used = sem("p_w1_hi"), sem("p_bias_full"), sem("p_bias"), sem("p_used")
        block = ctx.enter_context(nc.Block())
        ident, ident_bf, ones = c["ident"], c["ident_bf"], c["ones"]
        xT = c["xT"]
        pv_v = pv_bank[:, :].rearrange("p (h d) -> p h d", d=DH)

        def at(name, t, k, cyc):
            return e[name].at(t * (e[name].per // TILES) + k, cyc)

        def wait_tile(eng, name, t, k, cyc):
            eng.wait_ge(e[name].sem, at(name, t, k, cyc))

        def wait(eng, name, k, cyc):
            eng.wait_ge(e[name].sem, e[name].at(k, cyc))

        def prev_parts(t, k):
            return 2 * (t - 1 if t > 0 else t) + k

        def run(eng, name, step, next_cycle=lambda: None):
            def cycle(kind, cyc, b, new=None):
                for s_, t in steps_of(name, kind):
                    step(s_, t, cyc, b, new)

            def middle(layer):
                with eng.Fori(1, B - 1) as b:
                    cycle("middle", eng.snap(layer * B + b), b)

            cycle("start", 0, 0, 0)
            next_cycle()
            with eng.Fori(0, DEPTH - 1) as layer:
                middle(layer)
                next_cycle()
                cycle("last", layer * B + (B - 1), B - 1, layer + 1)
                next_cycle()
                cycle("first", layer * B + B, 0, layer + 1)
                next_cycle()
            middle(DEPTH - 1)
            next_cycle()
            cycle("end", DEPTH * B - 1, B - 1)

        def all_loaded(new):
            return new * (16 * LOADS) + 16 * LOADS

        def previous(b):
            return B - 1 if isinstance(b, int) and b == 0 else b - 1

        @block.sync
        def _(sp):
            for k in range(4):
                sp.dma_start(tables[:, k, :, :], tables_in[k].rearrange("(t p) d -> p t d", p=P)).then_inc(tables_loaded, 16)
            sp.wait_ge(padded, 2)
            sp.sem_inc(p_used, 2)
            with sp.Fori(0, DEPTH) as layer:
                sp.wait_ge(padded, 2)
                sp.wait_ge(p_used, layer * 2 + 2)
                one = bass.ds(layer, 1)
                flat = lambda x: x.rearrange("a n -> (a n)")

                def load(out, in_):
                    sp.dma_start(out, in_).then_inc(loaded, 16)

                for k in range(2):
                    half = slice(k * QKV // 2, (k + 1) * QKV // 2)
                    load(in_qkv[:, half], w["Wqkv"][one, :, half].rearrange("a k n -> (a k) n"))
                load(in_wo[:, :, :], w["Wo"][one].rearrange("a (c p) n -> p (a c) n", p=P))
                for k in range(2):
                    load(in_w1[:, k, 0:FF], w["W1"][one, :, k * FF:(k + 1) * FF].rearrange("a k n -> (a k) n"))
                    for j in range(FC):
                        n = P if j < FC - 1 else FR
                        load(in_b1[0:n, k, j:j + 1],
                             flat(w["b1"][one, k * FF + j * P:k * FF + j * P + n]).rearrange("(n a) -> n a", a=1))
                load(in_w2[:, 0:FC - 1, :], w["W2"][one, 0:(FC - 1) * P, :].rearrange("a (c p) n -> p (a c) n", p=P))
                load(in_w2[0:FR, FC - 1, :], w["W2"][one, (FC - 1) * P:FF, :].rearrange("a p n -> (a p) n"))
                load(in_w2[BIAS_ROW:BIAS_ROW + 1, FC - 1, :], w["b2"][one])
                load(in_g[:, :], flat(w["ln_g"][one]).rearrange("(n a) -> n a", a=1))
                load(in_b[:, :], flat(w["ln_b"][one]).rearrange("(n a) -> n a", a=1))
                load(in_qs[:, :], w["q_scale"][one].broadcast_to([P, DH]))
                load(in_ks[:, :], w["k_scale"][one].broadcast_to([P, DH]))
            sp.wait_ge(loaded, DEPTH * 16 * LOADS)

        @block.gpsimd
        def _(pool):
            nc.gpsimd.memset(xs_hi[:, 0:1].bitcast(F32), 0.0)
            nc.gpsimd.memset(xs_lo[:, 0:1].bitcast(F32), 0.0)
            nc.gpsimd.memset(xf[:, 0:1], 0.0)
            nc.gpsimd.memset(in_w1[:, :, :], 0.0)
            nc.gpsimd.memset(in_w2[:, FC - 1, :], 0.0)
            nc.gpsimd.memset(in_b1[:, :, :], 0.0)
            nc.gpsimd.memset(hidden[:, FC - 1, :], 0.0)
            for k in range(2):
                last = nc.gpsimd.memset(probs[:, k, 0:PAD], 0.0)
            last.then_inc(padded, 1)
            pool.wait_ge(padded, 1)
            nc.gpsimd.memset(hidden[BIAS_ROW:BIAS_ROW + 1, FC - 1, :], 1.0).then_inc(padded, 1)

            def step(s_, t, cyc, b, new):
                kind, k = s_[0], s_[-1]
                if kind == "P" and k < 4:
                    m, j = t + 1, k % 2
                    wait_tile(pool, "floor", m, k + 1, cyc)
                    nc.gpsimd.tensor_tensor(norms[:, m % 2, k, :], sums[:, m % 2, k, :], c["minus_half"][:, 0:HEADS_C],
                                            ALU.pow).then_inc(e["norm"].sem, 1)
                    wait_tile(pool, "rotated", m, k + 1, cyc)
                    wait_tile(pool, "qkT_full", m, k - 1, cyc)
                    if k < 2:
                        nc.gpsimd.tensor_tensor(qk[:, j, :], by_cos[:, j, :], by_sin[:, j, :],
                                                ALU.add).then_inc(e["qk"].sem, 1)
                    else:
                        nc.gpsimd.tensor_tensor(by_cos[:, j, :], by_cos[:, j, :], by_sin[:, j, :],
                                                ALU.add).then_inc(e["added"].sem, 1)
                        wait_tile(pool, "added", m, k - 1, cyc)
                        heads = by_cos[:, j, :].rearrange("p (h d) -> p h d", d=DH)
                        nc.gpsimd.tensor_tensor(
                            qk[:, j, :].rearrange("p (h d) -> p h d", d=DH), heads,
                            norms[:, m % 2, k, :].unsqueeze(2).broadcast_to([P, HEADS_C, DH]),
                            ALU.mult).then_inc(e["qk"].sem, 1)
                elif kind == "NO":
                    pool.wait_ge(loaded, all_loaded(new))
                    wait_tile(pool, "w_full", -1 if t < 0 else 0, 0, cyc)
                    nc.gpsimd.tensor_tensor(wo[:, :, :], in_wo[:, :, :], ones[:, :].unsqueeze(1).broadcast_to([P, INNER // P, D]),
                                            ALU.mult).then_inc(p_wo, 1)
                elif kind == "NF":
                    wait(pool, "y_full", 0, cyc)
                    nc.gpsimd.tensor_tensor(w2[:, :, :], in_w2[:, :, :], ones[:, :].unsqueeze(1).broadcast_to([P, FC, D]),
                                            ALU.mult).then_inc(p_used, 1)
                elif kind == "F2":
                    wait(pool, "f_var", 1 if t == TILES else 0, cyc)
                    nc.gpsimd.tensor_tensor(f_rstd[:, :], f_var[:, :], c["minus_half"][:, 0:TILES],
                                            ALU.pow).then_inc(e["f_rstd"].sem, 1)

            run(pool, "Pool", step)

        @block.tensor
        def _(pe):
            pe.wait_ge(padded, 2)
            user = {"out": ("x_new", 0, 0), "turn0": ("oT", -1, 1), "turn1": ("oT", -1, 2)}

            def free(name, cyc):
                kind, t, k = user[name]
                if kind == "ppT":
                    pe.wait_ge(e["ppT"].sem, e["ppT"].at(prev_parts(t, k), cyc))
                else:
                    wait_tile(pe, kind, t, k, cyc)

            def next_cycle():
                for name, (kind, t, k) in user.items():
                    user[name] = (kind, t - TILES, k)

            def step(s_, t, cyc, b, new):
                kind, k = s_[0], s_[-1]
                if kind == "P":
                    m = t + 1
                    if k == 0 and m % TILES == 0:
                        wait(pe, "xs", m // TILES + 1, cyc)
                    if new is not None and m % TILES == 0:
                        pe.wait_ge(p_lo, new * 6 + k + 1)
                    if k in (0, 1):
                        wait_tile(pe, "v", m, k - 1, cyc)
                    else:
                        wait_tile(pe, "rotated", m, k - 1, cyc)
                    tile = slice((m % TILES) * P, (m % TILES + 1) * P)
                    cols = slice(k * CHUNK, (k + 1) * CHUNK)
                    out = proj[k % 2][:, :]
                    nc.tensor.matmul(out, xs_hi[:, tile], qkv_hi[:, cols], start=True, stop=False)
                    nc.tensor.matmul(out, xs_hi[:, tile], qkv_lo[:, cols], start=False, stop=False)
                    nc.tensor.matmul(out, xs_lo[:, tile], qkv_hi[:, cols], start=False,
                                     stop=True).then_inc(e["proj_full"].sem, 1)
                elif kind == "T":
                    m = t + 1
                    free(f"turn{k % 2}", cyc)
                    wait_tile(pe, "qk", m, k + 1, cyc)
                    for i in range(4):
                        last = nc.tensor.transpose(turn[k % 2][:, i * P:(i + 1) * P], qk[:, k % 2, i * P:(i + 1) * P],
                                                   ident[:, :])
                    last.then_inc(e["qkT_full"].sem, 1)
                    user[f"turn{k % 2}"] = ("qkT", m, k + 1)
                elif kind == "S":
                    heads = SCORE_GROUPS[k]
                    n = len(heads)
                    if k == 0:
                        wait_tile(pe, "qkT", t, 4, cyc)
                    if k < 2:
                        wait_tile(pe, "exp", t - 1, GROUP_END[k + 4], cyc)
                    else:
                        wait_tile(pe, "exp", t, GROUP_END[k - 2], cyc)
                    first = 0 if t else WINDOW
                    out = score[k % 2][:, 0:n * KEYS].rearrange("p (h k) -> p h k", k=KEYS)
                    nc.tensor.matmul(out[:, :, first:], ident_bf[:, :], c["mask_band"][:, 0:n, first:],
                                     start=True, stop=False)
                    for i, h in enumerate(heads):
                        rows = slice((h % 2) * DH, (h % 2 + 1) * DH)
                        last = nc.tensor.matmul(out[:, i, first:], qT[rows, t % 2, h // 2, :],
                                                kT[rows, h // 2, t * P - WINDOW + first:(t + 1) * P],
                                                start=False, stop=(i == n - 1))
                    last.then_inc(e["s_full"].sem, 1)
                elif kind == "X":
                    wait_tile(pe, "exp", t, (6, 12, 12, 16)[k], cyc)
                    free(f"turn{k % 2}", cyc)
                    for i in range(4):
                        col = PAD + (4 * k + i) * KEYS + WINDOW
                        last = nc.tensor.transpose(turn[k % 2][:, i * P:(i + 1) * P], probs[:, t % 2, col:col + P],
                                                   ident[:, :])
                    last.then_inc(e["pT_full"].sem, 1)
                    user[f"turn{k % 2}"] = ("pT", t, k + 1)
                elif kind == "XP":
                    free(f"turn{k % 2}", cyc)
                    wait_tile(pe, "exp", t, (12, 16)[k], cyc)
                    for i in range(HEADS_C):
                        col = (HEADS_C * k + i) * KEYS
                        out, part = turn[k % 2][:, i * WINDOW:(i + 1) * WINDOW], probs[0:WINDOW, t % 2, col:col + P]
                        if i == 0:
                            nc.tensor.matmul(out, part, ident[0:WINDOW, 0:WINDOW], start=True, stop=True)
                        else:
                            last = nc.tensor.transpose(out, part, ident[0:WINDOW, 0:WINDOW])
                    last.then_inc(e["ppT_full"].sem, 1)
                    user[f"turn{k % 2}"] = ("ppT", t, k + 1)
                elif kind == "V":
                    wait_tile(pe, "v", t, 2, cyc)
                    wait_tile(pe, "attn", t, k, cyc)
                    if t % TILES:
                        pe.wait_ge(e["ppT"].sem, e["ppT"].at(prev_parts(t, k + 1), cyc))
                    for i in range(HEADS_C):
                        h = HEADS_C * k + i
                        if i % 4 == 0:
                            wait_tile(pe, "pT", t, h // 4 + 1, cyc)
                        cols = slice(h * DH, (h + 1) * DH)
                        last = nc.tensor.matmul(pv_v[:, i, :], pT[:, h // 4 % 2, h % 4, :], v[:, t % TILES, cols],
                                                start=True, stop=True)
                        if t % TILES:
                            last = nc.tensor.matmul(pv_v[0:WINDOW, i, :], ppT[:, k, i, :], v[:, (t - 1) % TILES, cols],
                                                    start=False, stop=True, skip_group_check=True)
                    last.then_inc(e["pv_full"].sem, 1)
                elif kind == "O":
                    wait_tile(pe, "attn", t - 1, k + 1, cyc)
                    free(f"turn{k}", cyc)
                    for i in range(4):
                        last = nc.tensor.transpose(turn[k][:, i * P:(i + 1) * P], attn[:, k, i * P:(i + 1) * P],
                                                   ident[:, :])
                    last.then_inc(e["oT_full"].sem, 1)
                    user[f"turn{k}"] = ("oT", t - 1, k + 1)
                elif kind == "W":
                    wait_tile(pe, "oT", t - 1, 2, cyc)
                    free_out(t, cyc)
                    for i in range(INNER // P):
                        last = nc.tensor.matmul(out_bank[:, 0:P], wo[:, i, :], attnT[:, i, :], start=(i == 0),
                                                stop=(i == INNER // P - 1))
                    last.then_inc(e["w_full"].sem, 1)
                    user["out"] = ("x_mid", t - 1, 1)
                elif kind == "NO":
                    pe.wait_ge(p_wo, new + 1)
                elif kind == "NF":
                    pe.wait_ge(loaded, all_loaded(new))
                    free_out(t, cyc)
                    for n in range(2 * FC):
                        part, j = n // FC, n % FC
                        last = nc.tensor.matmul(out_bank[:, n:n + 1], in_w1[:, part, j * P:(j + 1) * P], in_b[:, :],
                                                start=True, stop=True)
                    last.then_inc(p_bias_full, 1)
                    pe.wait_ge(p_bias, new + 1)
                elif kind in "FGA" or kind[0] == "F":
                    ffn(s_, t, cyc)

            def free_out(t, cyc):
                if t == 0:
                    wait_tile(pe, "x_mid", -1, 0, cyc)
                    wait(pe, "x_new", -1, cyc)
                else:
                    kind, tile, k = user["out"]
                    if kind == "x_mid":
                        wait_tile(pe, kind, tile, k, cyc)
                    else:
                        wait(pe, kind, k, cyc)

            def ffn(s_, t, cyc):
                kind, k = s_[0], s_[-1]
                ahead = 1 if t == TILES else 0
                if kind == "F0":
                    wait(pe, "xf", ahead, cyc)
                    free_out(t or 1, cyc)
                    nc.tensor.matmul(out_bank[:, :], c["mean_of"][:, :], xf[:, :], start=True,
                                     stop=True).then_inc(e["mean_full"].sem, 1)
                    user["out"] = ("centred", 0, ahead)
                elif kind == "F1":
                    wait(pe, "f_square", ahead, cyc)
                    free_out(t, cyc)
                    for i in range(TILES):
                        last = nc.tensor.matmul(out_bank[:, i:i + 1], fsq[:, i * P:(i + 1) * P], c["mean_of"][:, 0:1],
                                                start=True, stop=True)
                    last.then_inc(e["var_full"].sem, 1)
                    user["out"] = ("f_var", 0, ahead)
                elif kind == "F3":
                    wait(pe, "diag", ahead, cyc)
                    free_out(t, cyc)
                    nc.tensor.matmul(out_bank[:, :], ones[:, :], diag[:, :, :].rearrange("p t n -> p (t n)"), start=True,
                                     stop=True).then_inc(e["spread_full"].sem, 1)
                    user["out"] = ("xn", 0, ahead)
                elif kind in "GA":
                    part = 1 if kind == "G" else 0
                    done = ahead * FC + k + 1
                    wait(pe, "xn_lo", ahead, cyc)
                    free_out(t, cyc)
                    cols = slice(k * P, (k + 1) * P)
                    nc.tensor.matmul(out_bank[:, :], w1_hi[:, part, cols], xn_hi[:, :], start=True, stop=False)
                    nc.tensor.matmul(out_bank[:, :], w1_hi[:, part, cols], xn_lo[:, :], start=False, stop=False)
                    nc.tensor.matmul(out_bank[:, :], w1_lo[:, part, cols], xn_hi[:, :], start=False,
                                     stop=True).then_inc(e["gate_full" if part else "up_full"].sem, 1)
                    user["out"] = ("gelu" if part else "gated", 0, done - FC)
                elif kind == "F4":
                    wait(pe, "gated", ahead * FC, cyc)
                    free_out(t, cyc)
                    for j in range(FC):
                        n = P if j < FC - 1 else BIAS_ROW + 1
                        last = nc.tensor.matmul(out_bank[:, :], w2[0:n, j, :], hidden[0:n, j, :], start=(j == 0),
                                                stop=(j == FC - 1))
                    last.then_inc(e["y_full"].sem, 1)
                    user["out"] = ("x_new", 0, ahead)

            run(pe, "PE", step, next_cycle)

        @block.scalar
        def _(act):
            act.wait_ge(padded, 2)

            def copy(out, in_):
                return nc.scalar.activation(out, in_, ACT.Copy)

            def shifted(ahead, cyc, b):
                wait_tile(act, "proj_full", 0 if ahead == 1 else TILES, 0, cyc)
                copy(xs_hi[0:P // 2, :], xT[0:P // 2, bass.ds(b, 1), :].rearrange("p a n -> p (a n)"))
                copy(xs_hi[P // 2:P, 1:S], xT[P // 2:P, bass.ds(b, 1), 0:S - 1].rearrange("p a n -> p (a n)"))\
                    .then_inc(e["xs_hi"].sem, 1)

            def step(s_, t, cyc, b, new):
                kind, k = s_[0], s_[-1]
                if kind == "XS":
                    shifted(*((1, cyc, 0) if t < 0 else (2, cyc, 0 if isinstance(b, int) and b == B - 1 else b + 1)))
                elif kind == "P":
                    m = t + 1
                    wait_tile(act, "proj_full", m, k + 1, cyc)
                    if k < 4:
                        wait_tile(act, "sums", m, k - 1, cyc)
                        nc.scalar.activation(squares[:, k % 2, :], proj[k % 2][:, :], ACT.Square)\
                            .then_inc(e["square"].sem, 1)
                    else:
                        wait_tile(act, "pv_full", m - 3, 2, cyc)
                        copy(v[:, m % TILES, (k - 4) * CHUNK:(k - 3) * CHUNK], proj[k % 2][:, :])\
                            .then_inc(e["v"].sem, 1)
                elif kind == "T":
                    m = t + 1
                    wait_tile(act, "qkT_full", m, k + 1, cyc)
                    bank_ = turn[k % 2][:, :].rearrange("p (a n) -> p a n", n=P)
                    pairs = slice((k % 2) * 4, (k % 2) * 4 + 4)
                    if k < 2:
                        wait_tile(act, "s_full", m - 2, 6, cyc)
                        out = qT[:, m % 2, pairs, :]
                    else:
                        out = kT[:, pairs, (m % TILES) * P:(m % TILES + 1) * P]
                    copy(out, bank_).then_inc(e["qkT"].sem, 1)
                elif kind == "S":
                    wait_tile(act, "bias", t, k + 1, cyc)
                    if k == 0:
                        wait_tile(act, "pT_full", t - 1, 0, cyc)
                        wait_tile(act, "recip", t - 1, 0, cyc)
                    first = 0 if t else WINDOW
                    for i, h in enumerate(SCORE_GROUPS[k]):
                        col = PAD + h * KEYS
                        nc.scalar.activation(
                            probs[:, t % 2, col + first:col + KEYS], score[k % 2][:, i * KEYS + first:(i + 1) * KEYS],
                            ACT.Exp, scale=norms[:, t % 2, h // HEADS_C, h % HEADS_C:h % HEADS_C + 1],
                            bias=bias[:, t % 2, h:h + 1], accum_out=row_sum[:, t % 2, h:h + 1]).then_inc(e["exp"].sem, 1)
                elif kind == "O":
                    wait_tile(act, "oT_full", t - 1, k + 1, cyc)
                    wait_tile(act, "w_full", t - 1, 0, cyc)
                    copy(attnT[:, 4 * k:4 * k + 4, :], turn[k][:, :].rearrange("p (a n) -> p a n", n=P))\
                        .then_inc(e["oT"].sem, 1)
                elif kind == "NQ":
                    if k == 0:
                        act.wait_ge(loaded, all_loaded(new))
                    cols = slice(k * CHUNK, (k + 1) * CHUNK)
                    copy(qkv_hi[:, cols], in_qkv[:, cols]).then_inc(p_hi, 1)
                elif kind == "NF":
                    act.wait_ge(p_scaled, new + 1)
                    wait(act, "up_full", 0, cyc)
                    copy(w1_hi[:, :, :], w1[:, :, :]).then_inc(p_w1_hi, 1)
                elif kind in ("F1", "F3", "G"):
                    ahead = 1 if t == TILES else 0
                    if kind == "F1":
                        wait(act, "centred", ahead, cyc)
                        nc.scalar.activation(fsq[:, :], xc[:, :], ACT.Square).then_inc(e["f_square"].sem, 1)
                    elif kind == "F3":
                        wait(act, "xn", ahead, cyc)
                        copy(xn_hi[:, :], xn[:, :]).then_inc(e["xn_hi"].sem, 1)
                    else:
                        wait(act, "gate_full", ahead * FC + k + 1 - FC, cyc)
                        n = FC + k
                        nc.scalar.activation(gate[:, k, :], out_bank[:, :], ACT.Gelu, bias=b1[:, n:n + 1])\
                            .then_inc(e["gelu"].sem, 1)

            run(act, "Act", step)

        @block.vector
        def _(dve):
            dve.wait_ge(padded, 2)
            dve.wait_ge(tables_loaded, 16 * 4)

            def shifted(ahead, cyc, b):
                wait(dve, "xs_hi", ahead, cyc)
                nc.vector.tensor_tensor(xs_lo[0:P // 2, :], xT[0:P // 2, bass.ds(b, 1), :].rearrange("p a n -> p (a n)"),
                                        xs_hi[0:P // 2, :].bitcast(F32), ALU.subtract)
                nc.vector.tensor_tensor(xs_lo[P // 2:P, 1:S],
                                        xT[P // 2:P, bass.ds(b, 1), 0:S - 1].rearrange("p a n -> p (a n)"),
                                        xs_hi[P // 2:P, 1:S].bitcast(F32), ALU.subtract).then_inc(e["xs"].sem, 1)

            def step(s_, t, cyc, b, new):
                kind, k = s_[0], s_[-1]
                if kind == "XS":
                    shifted(*((1, cyc, 0) if t < 0 else (2, cyc, 0 if isinstance(b, int) and b == B - 1 else b + 1)))
                elif kind == "P" and k < 4:
                    m, j = t + 1, k % 2
                    tile = m % TILES
                    wait_tile(dve, "square", m, k + 1, cyc)
                    if k >= 2:
                        wait_tile(dve, "qk", m, k - 1, cyc)
                    else:
                        wait_tile(dve, "qk", m - 1, k + 3, cyc)
                    heads = proj[j][:, :].rearrange("p (h a d) -> p h a d", a=2, d=DH // 2)
                    which = 0 if k < 2 else 2

                    def table(n):
                        return turns[:, which + n, tile, :].rearrange("p (a d) -> p a d", a=2).unsqueeze(1)\
                            .broadcast_to([P, HEADS_C, 2, DH // 2])

                    nc.vector.tensor_tensor(by_cos[:, j, :].rearrange("p (h a d) -> p h a d", a=2, d=DH // 2), heads,
                                            table(0), ALU.mult)
                    swapped = by_sin[:, j, :].rearrange("p (h a d) -> p h a d", a=2, d=DH // 2)[:, :, ::-1, :]
                    nc.vector.tensor_tensor(swapped, heads, table(1), ALU.mult).then_inc(e["rotated"].sem, 1)
                    if k == 0:
                        wait_tile(dve, "exp", m - 2, H, cyc)
                    nc.vector.tensor_reduce(sums[:, m % 2, k, :], squares[:, j, :].rearrange("p (h d) -> p h d", d=DH),
                                            AX.X, ALU.add).then_inc(e["sums"].sem, 1)
                    wait_tile(dve, "sums", m, k + 1, cyc)
                    unit = 1.0 / (QK_SCALE * QK_SCALE) if k < 2 else 1.0
                    nc.vector.tensor_scalar(sums[:, m % 2, k, :], sums[:, m % 2, k, :], unit, L2_EPS2 * unit,
                                            ALU.mult, ALU.max).then_inc(e["floor"].sem, 1)
                elif kind == "S":
                    n = len(SCORE_GROUPS[k])
                    wait_tile(dve, "s_full", t, k + 1, cyc)
                    first = 0 if t else WINDOW
                    scores = score[k % 2][:, 0:n * KEYS].rearrange("p (h k) -> p h k", k=KEYS)[:, :, first:]
                    nc.vector.tensor_reduce(row_max[:, k % 2, 0:n], scores, AX.X, ALU.max)\
                        .then_inc(e["row_max"].sem, 1)
                    wait_tile(dve, "row_max", t, k + 1, cyc)
                    if k == 0:
                        wait_tile(dve, "norm", t, 2, cyc)
                    h = SCORE_GROUPS[k][0]
                    stop = SCORE_GROUPS[k][-1] + 1
                    scales = norms[:, t % 2, :, :].rearrange("p c h -> p (c h)")[:, h:stop:2]
                    nc.vector.scalar_tensor_tensor(out=bias[:, t % 2, h:stop:2], in0=row_max[:, k % 2, 0:n], scalar=-1.0,
                                                   in1=scales, op0=ALU.mult, op1=ALU.mult).then_inc(e["bias"].sem, 1)
                elif kind == "X":
                    wait_tile(dve, "pT_full", t, k + 1, cyc)
                    wait_tile(dve, "pv_full", t, k // 2, cyc)
                    nc.vector.tensor_copy(pT[:, k % 2, :, :].rearrange("p h q -> p (h q)"), turn[k % 2][:, :])\
                        .then_inc(e["pT"].sem, 1)
                elif kind == "XP":
                    dve.wait_ge(e["ppT_full"].sem, e["ppT_full"].at(prev_parts(t, k + 1), cyc))
                    wait_tile(dve, "pv_full", t - 1, k + 1, cyc)
                    nc.vector.tensor_copy(ppT[:, k, :, :].rearrange("p h q -> p (h q)"),
                                          turn[k % 2][:, 0:HEADS_C * WINDOW]).then_inc(e["ppT"].sem, 1)
                elif kind == "V":
                    wait_tile(dve, "exp", t, H if k else 12, cyc)
                    nc.vector.reciprocal(recip[:, k, :], row_sum[:, t % 2, k * HEADS_C:(k + 1) * HEADS_C])\
                        .then_inc(e["recip"].sem, 1)
                    wait_tile(dve, "recip", t, k + 1, cyc)
                    wait_tile(dve, "pv_full", t, k + 1, cyc)
                    wait_tile(dve, "oT_full", t - 1, k + 1, cyc)
                    nc.vector.tensor_tensor(attn[:, k, :].rearrange("p (h d) -> p h d", d=DH), pv_v[:, :, :],
                                            recip[:, k, :].unsqueeze(2).broadcast_to([P, HEADS_C, DH]),
                                            ALU.mult).then_inc(e["attn"].sem, 1)
                elif kind == "W":
                    wait_tile(dve, "w_full", t - 1, 1, cyc)
                    seq = previous(b) if t == 0 else b
                    tile = (t - 1) % TILES
                    x = xT[:, bass.ds(seq, 1), tile * P:(tile + 1) * P].rearrange("p a n -> p (a n)")
                    nc.vector.tensor_tensor(x, out_bank[:, 0:P], x, ALU.add).then_inc(e["x_mid"].sem, 1)
                elif kind == "NQ":
                    dve.wait_ge(p_hi, new * 6 + k + 1)
                    cols = slice(k * CHUNK, (k + 1) * CHUNK)
                    nc.vector.tensor_tensor(qkv_lo[:, cols], in_qkv[:, cols], qkv_hi[:, cols].bitcast(F32),
                                            ALU.subtract).then_inc(p_lo, 1)
                    if k == 5:
                        for n, scale in enumerate((in_qs, in_qs, in_ks, in_ks)):
                            nc.vector.tensor_tensor(turns[:, n, :, :], tables[:, n, :, :],
                                                    scale[:, :].unsqueeze(1).broadcast_to([P, TILES, DH]), ALU.mult)
                elif kind == "NF":
                    nc.vector.tensor_scalar(w1[:, :, :], in_w1[:, :, :], in_g[:, 0:1], None, ALU.mult).then_inc(p_scaled, 1)
                    dve.wait_ge(p_bias_full, new + 1)
                    nc.vector.tensor_tensor(b1[:, :], out_bank[:, 0:2 * FC], in_b1[:, :, :].rearrange("p a j -> p (a j)"),
                                            ALU.add).then_inc(p_bias, 1)
                    dve.wait_ge(p_w1_hi, new + 1)
                    nc.vector.tensor_tensor(w1_lo[:, :, :], w1[:, :, :], w1_hi[:, :, :].bitcast(F32),
                                            ALU.subtract).then_inc(p_used, 1)
                elif kind in ("F0", "F1", "F2", "F3", "A", "F4"):
                    ffn(s_, t, cyc, b)

            def ffn(s_, t, cyc, b):
                kind, k = s_[0], s_[-1]
                ahead, seq = (1, b) if t == TILES else (0, previous(b))
                rows = lambda lo, hi, stop: xT[lo:hi, bass.ds(seq, 1), 0:stop].rearrange("p a n -> p (a n)")
                if kind == "F0":
                    wait_tile(dve, "x_mid", TILES * ahead, 0, cyc)
                    nc.vector.tensor_copy(xf[0:P // 2, :], rows(0, P // 2, S))
                    nc.vector.tensor_copy(xf[P // 2:P, 1:S], rows(P // 2, P, S - 1)).then_inc(e["xf"].sem, 1)
                    wait(dve, "mean_full", ahead, cyc)
                    nc.vector.tensor_tensor(xc[:, :], xf[:, :], out_bank[:, :], ALU.subtract)\
                        .then_inc(e["centred"].sem, 1)
                elif kind == "F1":
                    wait(dve, "var_full", ahead, cyc)
                    nc.vector.tensor_scalar(f_var[:, :], out_bank[:, 0:TILES], LN_EPS, None, ALU.add)\
                        .then_inc(e["f_var"].sem, 1)
                elif kind == "F2":
                    wait(dve, "f_rstd", ahead, cyc)
                    nc.vector.tensor_tensor(diag[:, :, :], ident[:, :].unsqueeze(1).broadcast_to([P, TILES, P]),
                                            f_rstd[:, :].unsqueeze(2).broadcast_to([P, TILES, P]), ALU.mult)\
                        .then_inc(e["diag"].sem, 1)
                elif kind == "F3":
                    wait(dve, "spread_full", ahead, cyc)
                    nc.vector.tensor_tensor(xn[:, :], xc[:, :], out_bank[:, :], ALU.mult).then_inc(e["xn"].sem, 1)
                    wait(dve, "xn_hi", ahead, cyc)
                    nc.vector.tensor_tensor(xn_lo[:, :], xn[:, :], xn_hi[:, :].bitcast(F32), ALU.subtract)\
                        .then_inc(e["xn_lo"].sem, 1)
                elif kind == "A":
                    n = P if k < FC - 1 else FR
                    wait(dve, "up_full", ahead * FC + k + 1 - FC, cyc)
                    wait(dve, "gelu", ahead * FC + k + 1 - FC, cyc)
                    nc.vector.scalar_tensor_tensor(out=hidden[0:n, k, :], in0=out_bank[0:n, :], scalar=b1[0:n, k:k + 1],
                                                   in1=gate[0:n, k, :], op0=ALU.add, op1=ALU.mult)\
                        .then_inc(e["gated"].sem, 1)
                elif kind == "F4":
                    wait(dve, "y_full", ahead, cyc)
                    x = rows(0, P, S)
                    nc.vector.tensor_tensor(x, out_bank[:, :], x, ALU.add).then_inc(e["x_new"].sem, 1)

            run(dve, "DVE", step)


def output_stage(nc, c, residual, out_dram):
    with ExitStack() as ctx:
        def sb(name, shape, dt=F32):
            return ctx.enter_context(nc.sbuf_tensor(name, shape, dt))

        def sem(name):
            return ctx.enter_context(nc.semaphore(name))

        held, stat6, stat = sb("o_held", [P, S]), sb("o_stat6", [P, TILES, 6]), sb("o_stat", [P, TILES, 2])
        var, rstd, o = sb("o_var", [P, TILES]), sb("o_rstd", [P, TILES]), sb("o_o", [P, TILES, D])
        x = sb("o_x", [P, B * TILES, D])
        carrier = sb("o_carrier", [P, 1])
        turn = ctx.enter_context(nc.psum_tensor("o_turn", [P, 512], F32))
        fetched, turned, stats, summed = sem("o_fetched"), sem("o_turned"), sem("o_stats"), sem("o_summed")
        var_done, rstd_done, normalised, stored = sem("o_vard"), sem("o_rstdd"), sem("o_normalised"), sem("o_stored")
        x_loaded = sem("o_x_loaded")
        block = ctx.enter_context(nc.Block())

        @block.scalar
        def _(act):
            with act.Fori(0, B) as b:
                act.wait_ge(turned, b + 1)
                nc.scalar.activation(held[:, :], c["xT"][:, bass.ds(b, 1), :].rearrange("p a n -> p (a n)"), ACT.Copy)\
                    .then_inc(fetched, 1)

        @block.tensor
        def _(pe):
            with pe.Fori(0, B) as b:
                pe.wait_ge(fetched, b + 1)
                pe.wait_ge(normalised, b + 1)
                for t in range(TILES):
                    last = nc.tensor.transpose(turn[:, t * P:(t + 1) * P], held[:, t * P:(t + 1) * P], c["ident"][:, :])
                last.then_inc(turned, 1)

        @block.gpsimd
        def _(pool):
            with pool.Fori(0, B) as b:
                pool.wait_ge(var_done, b + 1)
                nc.gpsimd.tensor_tensor(rstd[:, :], var[:, :], c["minus_half"][:, 0:TILES], ALU.pow).then_inc(rstd_done, 1)

        @block.vector
        def _(dve):
            dve.wait_ge(x_loaded, 16)
            with dve.Fori(0, B) as b:
                dve.wait_ge(x_loaded, 16)
                dve.wait_ge(turned, b + 2)
                for t in range(TILES):
                    last = nc.vector.bn_stats(stat6[:, t, :], turn[:, t * P:(t + 1) * P])
                last.then_inc(stats, 1)
                dve.wait_ge(stats, b * 2 + 1)
                nc.vector.memset(carrier[:, :], 0.0)
                for t in range(TILES):
                    last = nc.vector.bn_aggr(stat[:, t, :], stat6[:, t, :])
                last.then_inc(stats, 1)
                dve.wait_ge(stats, b * 2 + 2)
                nc.vector.tensor_scalar(var[:, :], stat[:, :, 1], LN_EPS, None, ALU.add).then_inc(var_done, 1)
                dve.wait_ge(rstd_done, b + 1)
                for t in range(TILES):
                    last = nc.vector.tensor_scalar(o[:, t, :], turn[:, t * P:(t + 1) * P], stat[:, t, 0:1],
                                                   rstd[:, t:t + 1], ALU.subtract, ALU.mult)
                last.then_inc(normalised, 1)
                dve.wait_ge(normalised, b + 2)
                four = x[:, bass.ds(b * TILES, TILES), :]
                nc.vector.tensor_tensor(four, four, o[:, :, :], ALU.add).then_inc(summed, 1)

        @block.sync
        def _(sp):
            sp.sem_inc(turned, 1)
            sp.sem_inc(normalised, 1)
            sp.dma_start(x[:, :, :], residual).then_inc(x_loaded, 16)
            with sp.Fori(0, B) as b:
                sp.wait_ge(x_loaded, 16)
                sp.wait_ge(summed, b + 1)
                sp.dma_start(out_dram[bass.ds(b, 1)].rearrange("a (t p) d -> p (a t) d", p=P),
                             x[:, bass.ds(b * TILES, TILES), :]).then_inc(stored, 16)
            sp.wait_ge(stored, 16 * B)


def program(nc, a, out_dram):
    with ExitStack() as ctx:
        def sb(name, shape, dt=F32):
            return ctx.enter_context(nc.sbuf_tensor(name, shape, dt))

        def sem(name):
            return ctx.enter_context(nc.semaphore(name))

        c = {
            "xT": sb("xT", [P, B, S]),
            "ident": sb("ident", [P, P]), "ident_bf": sb("ident_bf", [P, P], BF16),
            "ones": sb("ones", [P, P]), "mean_of": sb("mean_of", [P, P]), "minus_half": sb("minus_half", [P, 8]),
            "mask_qk": sb("mask_qk", [P, P], BF16), "mask_kq": sb("mask_kq", [P, P], BF16),
            "mask_band": sb("mask_band", [P, 3, KEYS], BF16),
        }
        mqa, layers = mqa_events(sem), layer_events(sem)
        residual = nc.dram_tensor("residual", (P, B * TILES, D), F32, kind="Internal").ap()
        with nc.sbuf_tensor("x_tok", [P, B * TILES, D], F32) as x_tok:
            c["x_tok"] = x_tok
            constants_stage(nc, c, a["L0_attn_x"], list(mqa.values()) + list(layers.values()))
            mqa_stage(nc, c, mqa, {n: a["L0_attn_" + n] for n in ("Wq", "bq", "Wk", "bk", "Wv", "bv", "Wo", "bo")},
                      residual)
        layers_stage(nc, c, layers, {n: a["L0_ffn_" + n] for n in FFN_INPUTS}, a["tables"])
        output_stage(nc, c, residual, out_dram)


FFN_INPUTS = ("Wqkv", "q_scale", "k_scale", "Wo", "ln_g", "ln_b", "W1", "b1", "W2", "b2")


def kernel(**inputs):
    import concourse.bacc as bacc
    from concourse.bass_utils import run_bass_kernel_spmd

    nc = bacc.Bacc("TRN2", target_bir_lowering=False, num_devices=1)
    arrays = {name: np.ascontiguousarray(a) for name, a in inputs.items()}
    arrays["tables"] = rotary_tables()
    args = {n: nc.dram_tensor(n, a.shape, mybir.dt.from_np(a.dtype), kind="ExternalInput").ap()
            for n, a in arrays.items()}
    out = nc.dram_tensor("out", (B, S, D), F32, kind="ExternalOutput").ap()
    program(nc, args, out)
    return run_bass_kernel_spmd(nc, [arrays], core_ids=[0]).results[0]["out"]
```

```python
from contextlib import ExitStack

import numpy as np

import concourse.bass as bass
from concourse import mybir
from concourse.alu_op_type import AluOpType as ALU

ACT = mybir.ActivationFunctionType
AX = mybir.AxisListType
F32 = mybir.dt.float32
F32R = mybir.dt.float32r
BF16 = mybir.dt.bfloat16

P = 128
B, S, D = 8, 512, 128
TILES = S // P
MQA_H, MQA_D = 16, 8
DEPTH, H, DH = 6, 16, 64
INNER = H * DH
WINDOW = 32
FF = int(D * 4 * 2 / 3)
FC = -(-FF // P)
FR = FF - (FC - 1) * P
BIAS_ROW = 96
QK_SCALE = 8.0
MASKED = -1e30
LOWEST = -3e38
LN_EPS = 1e-5
L2_EPS2 = 1e-24


class Events:

    def __init__(self, semaphore, per):
        self.sem, self.per = semaphore, per

    def at(self, k, cycle):
        return cycle * self.per + (self.per + k)


def rotary_tables():
    half = np.arange(0, DH, 2, dtype=np.float32)
    inv_freq = (np.float32(1.0) / np.power(np.float32(10000.0), half / np.float32(DH))).astype(np.float32)
    t = np.arange(S, dtype=np.float32)
    freqs = (t[:, None] * inv_freq[None, :]).astype(np.float32)
    base = ((half + np.float32(0.4 * DH)) / np.float32(1.4 * DH)).astype(np.float32)
    power = ((t - S // 2) / np.float32(WINDOW // 2)).astype(np.float32)
    scale = np.power(base[None, :].astype(np.float64), power[:, None].astype(np.float64))
    cos, sin = np.cos(freqs.astype(np.float64)), np.sin(freqs.astype(np.float64))
    both = lambda a, b: np.concatenate([a, b], -1)
    return np.stack([both(cos * scale, cos * scale), both(sin * scale, -sin * scale),
                     both(cos / scale, cos / scale), both(sin / scale, -sin / scale)]).astype(np.float32)


def constants_stage(nc, c, x_in, credits, arrived):
    with ExitStack() as ctx:
        zeroed = ctx.enter_context(nc.semaphore("zeroed"))
        selected = ctx.enter_context(nc.semaphore("selected"))
        loaded = ctx.enter_context(nc.semaphore("loaded"))
        block = ctx.enter_context(nc.Block())

        @block.sync
        def _(sp):
            for b in range(B):
                sp.dma_start(c["x_tok"][:, b * TILES:(b + 1) * TILES, :],
                             x_in[b].rearrange("(t p) d -> p t d", p=P)).then_inc(loaded, 16)
            for e in credits:
                sp.sem_inc(e.sem, e.per)
            sp.wait_ge(loaded, 16 * B)

        @block.vector
        def _(dve):
            nc.vector.memset(arrived["w1"][:, :, :], 0.0)
            nc.vector.memset(arrived["w2"][:, FC - 1, :], 0.0)
            nc.vector.memset(arrived["b1"][:, :, :], 0.0)
            nc.vector.memset(c["ones"][:, :], 1.0)
            nc.vector.memset(c["mean_of"][:, :], 1.0 / D)
            nc.vector.memset(c["minus_half"][:, :], -0.5)
            nc.vector.memset(c["ident"][:, :], 0.0)
            nc.vector.memset(c["ident_bf"][:, :], 0.0)
            nc.vector.memset(c["mask_qk"][:, :], 0.0)
            nc.vector.memset(c["mask_kq"][:, :], 0.0)
            nc.vector.memset(c["mask_band"][:, :], 0.0).then_inc(zeroed, 1)

        @block.gpsimd
        def _(pool):
            pool.wait_ge(zeroed, 1)
            step = [0]

            def select(out, pattern, compare, base, fill, channel):
                nc.gpsimd.affine_select(out=out, in_=out, compare_op=compare, fill=fill, base=base,
                                        pattern=pattern, channel_multiplier=channel).then_inc(selected, 1)
                step[0] += 1
                pool.wait_ge(selected, step[0])

            select(c["ident"][:, :], [[-1, P]], ALU.not_equal, 0, 1.0, 1)
            select(c["ident_bf"][:, :], [[-1, P]], ALU.not_equal, 0, 1.0, 1)
            select(c["mask_qk"][:, :], [[-1, P]], ALU.is_ge, 0, MASKED, 1)
            select(c["mask_kq"][:, :], [[1, P]], ALU.is_ge, 0, MASKED, -1)
            select(c["mask_band"][:, :], [[-1, WINDOW + P]], ALU.is_ge, WINDOW, MASKED, 1)
            select(c["mask_band"][:, :], [[1, WINDOW + P]], ALU.is_ge, 0, MASKED, -1)


SLOTS = 32
AHEAD = 5
GROUPS = MQA_H * SLOTS // P
PER_GROUP = MQA_H // GROUPS
QKV_W = D + 2 * MQA_D
SCORE_SCALE = float(np.float32(1.0) / np.sqrt(np.float32(MQA_D)))
PROB_AT = {0: 0, 1: 512, 3: 896, 2: 1024}
PROB_BANKS = ((0,), (1, 3), (2,))
PROBS_W = 1280


def mqa_events(sem):
    return {
        **{f"{name}{k}": Events(sem(f"a_{name}{k}"), n) for name, n in (("stats", 2), ("var", 1), ("rstd", 1))
           for k in range(3)},
        "kv": Events(sem("a_kv"), 1),
        "xn": Events(sem("a_xn"), 1), "xnT_full": Events(sem("a_xnT_full"), 1), "xnT": Events(sem("a_xnT"), 1),
        "qkv_full": Events(sem("a_qkv_full"), 2), "hi": Events(sem("a_hi"), 2), "lo": Events(sem("a_lo"), 2),
        "t1_full": Events(sem("a_t1_full"), 5), "t1": Events(sem("a_t1"), 5),
        "s_full": Events(sem("a_s_full"), MQA_H * TILES), "s_max": Events(sem("a_s_max"), MQA_H * TILES),
        "m_hi": Events(sem("a_m_hi"), GROUPS), "m": Events(sem("a_m"), GROUPS),
        "t2_full": Events(sem("a_t2_full"), GROUPS), "t2": Events(sem("a_t2"), GROUPS),
        "st_full": Events(sem("a_st_full"), 3 * MQA_H), "exp": Events(sem("a_exp"), 3 * MQA_H),
        "pv_full": Events(sem("a_pv_full"), MQA_H), "pv": Events(sem("a_pv"), GROUPS),
        "pvT_full": Events(sem("a_pvT_full"), GROUPS), "recip": Events(sem("a_recip"), GROUPS),
        "attn": Events(sem("a_attn"), GROUPS),
        "oT_full": Events(sem("a_oT_full"), 1), "oT": Events(sem("a_oT"), 1), "proj": Events(sem("a_proj"), 1),
        "o": Events(sem("a_o"), 1), "x2": Events(sem("a_x2"), 1), "y": Events(sem("a_y"), 1),
        "yT_full": Events(sem("a_yT_full"), 1), "yT": Events(sem("a_yT"), 1),
    }


def mqa_stage(nc, c, e, weights, residual, first_layer):
    with ExitStack() as ctx:
        def sb(name, shape, dt=F32):
            return ctx.enter_context(nc.sbuf_tensor(name, shape, dt))

        def bank(name):
            return ctx.enter_context(nc.psum_tensor(name, [P, 512], F32))

        wqkv = sb("a_wqkv", [P, QKV_W])
        bqkv = sb("a_bqkv", [1, QKV_W])
        wo, bo = sb("a_wo", [P, D]), sb("a_bo", [1, D])
        stat6, stat = sb("a_stat6", [P, 3, TILES, 6]), sb("a_stat", [P, 3, TILES, 2])
        var, rstd = sb("a_varb", [P, 3, TILES]), sb("a_rstdb", [P, 3, TILES])
        xn, xnT = sb("a_xnb", [P, TILES, D]), sb("a_xnTb", [P, S])
        qa = sb("a_qa", [P, TILES, MQA_H, SLOTS], F32R)
        ka = sb("a_ka", [P, TILES, PER_GROUP, SLOTS], F32R)
        va = sb("a_va", [P, TILES, SLOTS])
        qT0 = sb("a_qT0", [P, GROUPS, S], F32R)
        qT1 = sb("a_qT1", [P, GROUPS, S], F32R)
        kT = sb("a_kT", [P, S], F32R)
        kT1 = sb("a_kT1", [P, S], F32R)
        v_next = sb("a_v_next", [P, TILES, MQA_D])
        row_max = sb("a_row_max", [P, TILES, MQA_H])
        probs = sb("a_probs", [P, 2, PROBS_W])
        pv = sb("a_pvb", [P, S])
        recip = sb("a_recipb", [P, GROUPS, TILES, PER_GROUP])
        attn, attnT = sb("a_attnb", [P, TILES, D]), sb("a_attnTb", [P, S])
        o, y = sb("a_ob", [P, TILES, D]), sb("a_yb", [P, TILES, D])
        carrier = sb("a_carrier", [P, 1])
        turn = [bank("a_turn0"), bank("a_turn1")]
        score = [bank("a_score0"), bank("a_score1")]
        scoreT = [bank("a_scoreT0"), bank("a_scoreT1"), bank("a_scoreT2")]
        pv_bank = bank("a_pv_bank")
        w_loaded = ctx.enter_context(nc.semaphore("a_w_loaded"))
        padded = ctx.enter_context(nc.semaphore("a_padded"))
        stored = ctx.enter_context(nc.semaphore("a_stored"))
        block = ctx.enter_context(nc.Block())
        ident, ident_bf, ones = c["ident"], c["ident_bf"], c["ones"]
        x_tok, xT = c["x_tok"], c["xT"]
        pvT = turn[1][:, :].rearrange("p (t h s) -> p t h s", t=TILES, h=PER_GROUP)

        def each(eng, sequence, next_sequence=lambda: None):
            sequence(0, first=True)
            next_sequence()
            with eng.Fori(1, B - 1) as b:
                sequence(b)
            next_sequence()
            sequence(B - 1, last=True)

        @block.sync
        def _(sp):
            at = 0
            for w, b_, n in (("Wq", "bq", D), ("Wk", "bk", MQA_D), ("Wv", "bv", MQA_D)):
                sp.dma_start(wqkv[:, at:at + n], weights[w]).then_inc(w_loaded, 16)
                sp.dma_start(bqkv[:, at:at + n], weights[b_].rearrange("(a n) -> a n", a=1)).then_inc(w_loaded, 16)
                at += n
            sp.dma_start(wo[:, :], weights["Wo"]).then_inc(w_loaded, 16)
            sp.dma_start(bo[:, :], weights["bo"].rearrange("(a n) -> a n", a=1)).then_inc(w_loaded, 16)
            sp.wait_ge(w_loaded, 16 * 8)
            first_layer(sp)
            with sp.Fori(0, B) as b:
                sp.wait_ge(w_loaded, 16 * 8)
                sp.wait_ge(e["x2"].sem, e["x2"].at(1, b))
                sp.dma_start(residual[:, bass.ds(b * TILES, TILES), :], x_tok[:, bass.ds(b * TILES, TILES), :])\
                    .then_inc(stored, 16)
            sp.wait_ge(stored, 16 * B)

        @block.gpsimd
        def _(pool):
            nc.gpsimd.memset(va[:, :, :], 0.0)
            nc.gpsimd.memset(qa[:, :, :, :].bitcast(F32), 0.0)
            nc.gpsimd.memset(ka[:, :, :, :].bitcast(F32), 0.0).then_inc(padded, 1)
            pool.wait_ge(padded, 1)
            nc.gpsimd.memset(ka[:, :, :, 24:26].bitcast(F32), 1.0)
            nc.gpsimd.memset(va[:, :, MQA_D:MQA_D + 1], 1.0).then_inc(padded, 1)

            def inverse_deviation(norm, b):
                pool.wait_ge(e[f"var{norm}"].sem, e[f"var{norm}"].at(1, b))
                nc.gpsimd.tensor_tensor(rstd[:, norm, :], var[:, norm, :], c["minus_half"][:, 0:TILES],
                                        ALU.pow).then_inc(e[f"rstd{norm}"].sem, 1)

            def sequence(b, first=False, last=False):
                if not first:
                    inverse_deviation(1, b - 1)
                    inverse_deviation(2, b - 1)
                if not last:
                    inverse_deviation(0, b + 1)

            inverse_deviation(0, 0)
            each(pool, sequence)
            inverse_deviation(1, B - 1)
            inverse_deviation(2, B - 1)

        @block.tensor
        def _(pe):
            pe.wait_ge(w_loaded, 16 * 8)
            pe.wait_ge(padded, 2)

            def scores(b, g, i, qt):
                s = (g * PER_GROUP + i) * TILES + qt
                n = P * (qt + 1)
                out = score[s % 2]
                pe.wait_ge(e["s_max"].sem, e["s_max"].at(s - 1, b))
                nc.tensor.matmul(out[:, 0:n], qT0[32 * i:32 * i + 32, g, qt * P:(qt + 1) * P],
                                 kT[32 * i:32 * i + 32, 0:n], start=True, stop=False)
                nc.tensor.matmul(out[:, n - P:n], ident_bf[:, :], c["mask_qk"][:, :],
                                 start=False, stop=True).then_inc(e["s_full"].sem, 1)

            def scoresT(b, g, i, n_bank):
                h = g * PER_GROUP + i
                pe.wait_ge(e["exp"].sem, e["exp"].at(3 * h + n_bank - 2, b))
                at = 0
                for kt in PROB_BANKS[n_bank]:
                    n = S - kt * P
                    out = scoreT[n_bank]
                    nc.tensor.matmul(out[:, at:at + n], kT1[32 * i:32 * i + 32, kt * P:(kt + 1) * P],
                                     qT1[32 * i:32 * i + 32, g, kt * P:S], start=True, stop=False)
                    last = nc.tensor.matmul(out[:, at:at + P], ident_bf[:, :], c["mask_kq"][:, :],
                                            start=False, stop=True)
                    at += n
                last.then_inc(e["st_full"].sem, 1)

            def weighted_values(b, h, kt):
                rows = slice(32 * (h % PER_GROUP), 32 * (h % PER_GROUP) + 32)
                if kt == 0:
                    pe.wait_ge(e["exp"].sem, e["exp"].at(3 * (h + 1), b))
                    if h % PER_GROUP == 0:
                        pe.wait_ge(e["pv"].sem, e["pv"].at(h // PER_GROUP, b))
                last = nc.tensor.matmul(pv_bank[rows, kt * P:S], va[:, kt, :],
                                        probs[:, h % 2, PROB_AT[kt]:PROB_AT[kt] + S - kt * P],
                                        start=(kt == 0), stop=(kt == TILES - 1))
                if kt == TILES - 1:
                    last.then_inc(e["pv_full"].sem, 1)

            def turn_with_max(b, g):
                pe.wait_ge(e["m"].sem, e["m"].at(g + 1, b))
                turned(b, 0, stacked(g), "t2_full", ("t2", g + 1, 0))

            def head(b, shifted=None, for_max=None, weighted=None, between=None):
                for what, k in (("T", 0), ("S", 0), ("T", 1), ("S", 1), ("V", 0), ("T", 2), ("S", 2), ("V", 1),
                                ("S", 3), ("V", 2), ("V", 3)):
                    if what == "T" and shifted:
                        scoresT(b, *shifted, k)
                    elif what == "S" and for_max:
                        scores(*for_max, k)
                    elif what == "V" and weighted is not None:
                        weighted_values(b, weighted, k)
                    if (what, k) == ("S", 1) and between:
                        between()

            user = {}

            def free(bank_, b):
                if bank_ in user:
                    name, k, ahead = user[bank_]
                    pe.wait_ge(e[name].sem, e[name].at(k, b + ahead))

            def next_sequence():
                for bank_, (name, k, ahead) in user.items():
                    user[bank_] = (name, k, ahead - 1)

            def turned(b, bank_, sources, full, used):
                free(bank_, b)
                for t, source in enumerate(sources):
                    last = nc.tensor.transpose(turn[bank_][:, t * P:(t + 1) * P], source, ident[:, :])
                last.then_inc(e[full].sem, 1)
                user[bank_] = used

            def turn_values(b, g):
                pe.wait_ge(e["pv"].sem, e["pv"].at(g + 1, b))
                turned(b, 1, [pv[:, t * P:(t + 1) * P] for t in range(TILES)], "pvT_full", ("attn", g + 1, 0))

            def turn_xn(b):
                pe.wait_ge(e["xn"].sem, e["xn"].at(1, b + 1))
                turned(b, 0, [xn[:, t, :] for t in range(TILES)], "xnT_full", ("xnT", 1, 1))

            def project(b, u):
                pe.wait_ge(e["xnT"].sem, e["xnT"].at(1, b + 1))
                free(0, b)
                for t in (2 * u, 2 * u + 1):
                    out = turn[0][:, (t % 2) * QKV_W:(t % 2 + 1) * QKV_W]
                    nc.tensor.matmul(out, xnT[:, t * P:(t + 1) * P], wqkv[:, :], start=True, stop=False)
                    last = nc.tensor.matmul(out, ones[0:1, 0:P], bqkv[0:1, :], start=False, stop=True)
                last.then_inc(e["qkv_full"].sem, 1)
                user[0] = ("lo", u + 1, 1)

            def stacked(g):
                return [qa[:, t, g * PER_GROUP:(g + 1) * PER_GROUP, :].bitcast(F32).rearrange("p r s -> p (r s)")
                        for t in range(TILES)]

            def turn_keys(b):
                pe.wait_ge(e["lo"].sem, e["lo"].at(2, b + 1))
                turned(b, 0, [ka[:, t, :, :].bitcast(F32).rearrange("p r s -> p (r s)") for t in range(TILES)],
                       "t1_full", ("t1", 1, 1))

            def turn_queries(b, g):
                turned(b, 0, stacked(g), "t1_full", ("t1", g + 2, 1))

            def turn_attn(b):
                pe.wait_ge(e["attn"].sem, e["attn"].at(GROUPS, b))
                turned(b, 0, [attn[:, t, :] for t in range(TILES)], "oT_full", ("oT", 1, 0))

            def project_out(b):
                pe.wait_ge(e["oT"].sem, e["oT"].at(1, b))
                free(1, b)
                for t in range(TILES):
                    out = turn[1][:, t * P:(t + 1) * P]
                    nc.tensor.matmul(out, attnT[:, t * P:(t + 1) * P], wo[:, :], start=True, stop=False)
                    last = nc.tensor.matmul(out, ones[0:1, 0:P], bo[0:1, :], start=False, stop=True)
                last.then_inc(e["proj"].sem, 1)
                user[1] = ("o", 1, 0)

            def turn_y(b, ahead):
                pe.wait_ge(e["y"].sem, e["y"].at(1, b + ahead))
                turned(b, 0, [y[:, t, :] for t in range(TILES)], "yT_full", ("yT", 1, ahead))

            def sequence(b, first=False, last=False):
                pe.wait_ge(e["kv"].sem, e["kv"].at(1, b))
                pe.wait_ge(e["t1"].sem, e["t1"].at(5, b))
                for g in range(GROUPS):
                    pe.wait_ge(e["t2"].sem, e["t2"].at(g + 1, b))
                    for i in range(PER_GROUP):
                        h = g * PER_GROUP + i
                        then = h + AHEAD
                        head(b, shifted=(g, i), weighted=h - 1 if h else None,
                             for_max=(b, then // PER_GROUP, then % PER_GROUP) if then < MQA_H else None,
                             between=(lambda: turn_with_max(b, g + 1)) if i == 3 and g + 1 < GROUPS else None)
                        if h > PER_GROUP and i == 1:
                            turn_values(b, g - 1)
                        if (g, i) == (1, 1) and not first:
                            turn_y(b, -1)
                        if last:
                            continue
                        if (g, i) == (2, 2):
                            turn_xn(b)
                        elif g == 3 and i < 2:
                            project(b, i)
                        elif (g, i) == (3, 2):
                            turn_keys(b)
                        elif (g, i) == (3, 3):
                            turn_queries(b, 0)
                if last:
                    head(b, weighted=MQA_H - 1)
                    turn_values(b, GROUPS - 1)
                    turn_attn(b)
                    project_out(b)
                    turn_y(b, 0)
                    return
                pe.wait_ge(e["t1"].sem, e["t1"].at(2, b + 1))
                head(b, for_max=(b + 1, 0, 0), weighted=MQA_H - 1)
                head(b, for_max=(b + 1, 0, 1), between=lambda: turn_queries(b, 1))
                turn_values(b, GROUPS - 1)
                head(b, for_max=(b + 1, 0, 2), between=lambda: turn_queries(b, 2))
                turn_attn(b)
                head(b, for_max=(b + 1, 0, 3))
                turn_queries(b, 3)
                project_out(b)
                head(b, for_max=(b + 1, 1, 0), between=lambda: turn_first(b))

            def turn_first(b):
                pe.wait_ge(e["m"].sem, e["m"].at(1, b + 1))
                turned(b, 0, stacked(0), "t2_full", ("t2", 1, 1))

            turn_xn(-1)
            for u in range(2):
                project(-1, u)
            turn_keys(-1)
            for g in range(GROUPS):
                turn_queries(-1, g)
            pe.wait_ge(e["t1"].sem, e["t1"].at(3, 0))
            for i in range(PER_GROUP):
                head(-1, for_max=(0, 0, i))
            head(-1, for_max=(0, 1, 0), between=lambda: turn_first(-1))
            next_sequence()
            each(pe, sequence, next_sequence)

        @block.scalar
        def _(act):
            act.wait_ge(padded, 2)

            def copy(out, in_):
                return nc.scalar.activation(out, in_, ACT.Copy)

            def exps(b, h):
                for n_bank, (at, n) in enumerate(((0, 512), (512, 512), (1024, 256))):
                    act.wait_ge(e["st_full"].sem, e["st_full"].at(3 * h + n_bank + 1, b))
                    if n_bank == 0:
                        act.wait_ge(e["pv_full"].sem, e["pv_full"].at(h - 1, b))
                    nc.scalar.activation(probs[:, h % 2, at:at + n], scoreT[n_bank][:, 0:n], ACT.Exp,
                                         scale=SCORE_SCALE).then_inc(e["exp"].sem, 1)

            def turned_input(b):
                act.wait_ge(e["xnT_full"].sem, e["xnT_full"].at(1, b + 1))
                copy(xnT[:, :], turn[0][:, :]).then_inc(e["xnT"].sem, 1)

            def hi_parts(b, u):
                act.wait_ge(e["qkv_full"].sem, e["qkv_full"].at(u + 1, b + 1))
                qkv = turn[0][:, 0:2 * QKV_W].rearrange("p (t n) -> p t n", t=2)
                two = slice(2 * u, 2 * u + 2)
                q = qkv[:, :, 0:D].rearrange("p t (h d) -> p t h d", d=MQA_D)
                k = qkv[:, :, D:D + MQA_D].unsqueeze(2).broadcast_to([P, 2, PER_GROUP, MQA_D])
                copy(qa[:, two, :, 0:8], q)
                copy(qa[:, two, :, 16:24], q)
                copy(ka[:, two, :, 0:8], k)
                copy(ka[:, two, :, 8:16], k)
                copy(v_next[:, two, :], qkv[:, :, D + MQA_D:QKV_W]).then_inc(e["hi"].sem, 1)

            def first_turned(b, k):
                act.wait_ge(e["t1_full"].sem, e["t1_full"].at(k + 1, b + 1))
                copy(kT[:, :] if k == 0 else qT0[:, k - 1, :], turn[0][:, :]).then_inc(e["t1"].sem, 1)

            def keys_and_values(b):
                act.wait_ge(e["t1"].sem, e["t1"].at(1, b + 1))
                copy(kT1[:, :], kT[:, :].bitcast(F32))
                copy(va[:, :, 0:MQA_D], v_next[:, :, :]).then_inc(e["kv"].sem, 1)

            def values_group(b, g):
                act.wait_ge(e["pv_full"].sem, e["pv_full"].at((g + 1) * PER_GROUP, b))
                copy(pv[:, :], pv_bank[:, :]).then_inc(e["pv"].sem, 1)

            def attn_turned(b):
                act.wait_ge(e["oT_full"].sem, e["oT_full"].at(1, b))
                copy(attnT[:, :], turn[0][:, :]).then_inc(e["oT"].sem, 1)

            def output_turned(b):
                act.wait_ge(e["yT_full"].sem, e["yT_full"].at(1, b))
                out = xT[:, b, :] if isinstance(b, int) else xT[:, bass.ds(b, 1), :].rearrange("p a n -> p (a n)")
                copy(out, turn[0][:, :]).then_inc(e["yT"].sem, 1)

            def turned_with_max(b, g):
                act.wait_ge(e["t2_full"].sem, e["t2_full"].at(g + 1, b))
                copy(qT1[:, g, :], turn[0][:, :]).then_inc(e["t2"].sem, 1)

            def sequence(b, first=False, last=False):
                for g in range(GROUPS):
                    for i in range(PER_GROUP):
                        exps(b, g * PER_GROUP + i)
                        if i == 3 and g + 1 < GROUPS:
                            turned_with_max(b, g + 1)
                        if g >= 1 and i == 0:
                            values_group(b, g - 1)
                        if (g, i) == (1, 1) and not first:
                            output_turned(b - 1)
                        if last:
                            continue
                        if (g, i) == (2, 2):
                            turned_input(b)
                        elif g == 3 and i < 2:
                            hi_parts(b, i)
                        elif g == 3:
                            first_turned(b, i - 2)
                values_group(b, GROUPS - 1)
                if last:
                    attn_turned(b)
                    output_turned(b)
                    return
                keys_and_values(b)
                first_turned(b, 2)
                first_turned(b, 3)
                attn_turned(b)
                first_turned(b, 4)
                turned_with_max(b + 1, 0)

            turned_input(-1)
            for u in range(2):
                hi_parts(-1, u)
            for k in range(5):
                first_turned(-1, k)
            keys_and_values(-1)
            turned_with_max(0, 0)
            each(act, sequence)

        @block.vector
        def _(dve):
            dve.wait_ge(padded, 2)

            def mean_and_var(b, norm, tiles, after=None):
                stats = e[f"stats{norm}"]
                dve.wait_ge(padded, 2)
                if after:
                    dve.wait_ge(e[after].sem, e[after].at(1, b))
                for t, tile in enumerate(tiles):
                    last = nc.vector.bn_stats(stat6[:, norm, t, :], tile)
                last.then_inc(stats.sem, 1)
                dve.wait_ge(stats.sem, stats.at(1, b))
                nc.vector.memset(carrier[:, :], 0.0)
                for t in range(TILES):
                    last = nc.vector.bn_aggr(stat[:, norm, t, :], stat6[:, norm, t, :])
                last.then_inc(stats.sem, 1)
                dve.wait_ge(stats.sem, stats.at(2, b))
                nc.vector.tensor_scalar(var[:, norm, :], stat[:, norm, :, 1], LN_EPS, None,
                                        ALU.add).then_inc(e[f"var{norm}"].sem, 1)

            def normalised(b, norm, out, tiles):
                dve.wait_ge(e[f"rstd{norm}"].sem, e[f"rstd{norm}"].at(1, b))
                for t, tile in enumerate(tiles):
                    last = nc.vector.tensor_scalar(out[:, t, :], tile, stat[:, norm, t, 0:1], rstd[:, norm, t:t + 1],
                                                   ALU.subtract, ALU.mult)
                return last

            def weighted(b, g):
                dve.wait_ge(e["pvT_full"].sem, e["pvT_full"].at(g + 1, b))
                nc.vector.reciprocal(recip[:, g, :, :], pvT[:, :, :, MQA_D]).then_inc(e["recip"].sem, 1)
                dve.wait_ge(e["recip"].sem, e["recip"].at(g + 1, b))
                width = PER_GROUP * MQA_D
                nc.vector.tensor_tensor(
                    attn[:, :, g * width:(g + 1) * width].rearrange("p t (h d) -> p t h d", d=MQA_D),
                    pvT[:, :, :, 0:MQA_D], recip[:, g, :, :].unsqueeze(3).broadcast_to([P, TILES, PER_GROUP, MQA_D]),
                    ALU.mult).then_inc(e["attn"].sem, 1)

            def lo_parts(b, u):
                dve.wait_ge(e["hi"].sem, e["hi"].at(u + 1, b + 1))
                qkv = turn[0][:, 0:2 * QKV_W].rearrange("p (t n) -> p t n", t=2)
                two = slice(2 * u, 2 * u + 2)
                q = qkv[:, :, 0:D].rearrange("p t (h d) -> p t h d", d=MQA_D)
                k = qkv[:, :, D:D + MQA_D].unsqueeze(2).broadcast_to([P, 2, PER_GROUP, MQA_D])
                nc.vector.tensor_tensor(qa[:, two, :, 8:16], q, qa[:, two, :, 0:8].bitcast(F32), ALU.subtract)
                nc.vector.memset(qa[:, two, :, 24:26].bitcast(F32), 0.0)
                nc.vector.tensor_tensor(ka[:, two, :, 16:24], k, ka[:, two, :, 0:8].bitcast(F32),
                                        ALU.subtract).then_inc(e["lo"].sem, 1)

            def maxima(b, g, i):
                for qt in range(TILES):
                    h = g * PER_GROUP + i
                    s = h * TILES + qt
                    dve.wait_ge(e["s_full"].sem, e["s_full"].at(s + 1, b))
                    nc.vector.tensor_reduce(row_max[:, qt, h:h + 1], score[s % 2][:, 0:P * (qt + 1)], AX.X,
                                            ALU.max).then_inc(e["s_max"].sem, 1)

            def negated_maxima(b, g):
                heads = slice(g * PER_GROUP, (g + 1) * PER_GROUP)
                dve.wait_ge(e["s_max"].sem, e["s_max"].at((g + 1) * PER_GROUP * TILES, b))
                dve.wait_ge(e["t1_full"].sem, e["t1_full"].at(g + 2, b))
                nc.vector.tensor_scalar(qa[:, :, heads, 24], row_max[:, :, heads], -1.0, None,
                                        ALU.mult).then_inc(e["m_hi"].sem, 1)
                dve.wait_ge(e["m_hi"].sem, e["m_hi"].at(g + 1, b))
                nc.vector.scalar_tensor_tensor(out=qa[:, :, heads, 25], in0=row_max[:, :, heads], scalar=-1.0,
                                               in1=qa[:, :, heads, 24].bitcast(F32), op0=ALU.mult,
                                               op1=ALU.subtract).then_inc(e["m"].sem, 1)

            def tiles_of(b):
                return [x_tok[:, b * TILES + t, :] for t in range(TILES)]

            projected = [turn[1][:, t * P:(t + 1) * P] for t in range(TILES)]

            def add_output(b):
                dve.wait_ge(e["o"].sem, e["o"].at(1, b))
                four = x_tok[:, bass.ds(b * TILES, TILES), :]
                nc.vector.tensor_tensor(four, four, o[:, :, :], ALU.add).then_inc(e["x2"].sem, 1)

            def sequence(b, first=False, last=False):
                for g in range(GROUPS):
                    for i in range(PER_GROUP):
                        then = g * PER_GROUP + i + AHEAD
                        if then < MQA_H:
                            maxima(b, then // PER_GROUP, then % PER_GROUP)
                        if i == 2 and g + 1 < GROUPS:
                            negated_maxima(b, g + 1)
                        if g >= 1 and i == 2:
                            weighted(b, g - 1)
                        if not first:
                            if (g, i) == (0, 0):
                                mean_and_var(b - 1, 1, projected, "proj")
                            elif (g, i) == (0, 1):
                                normalised(b - 1, 1, o, projected).then_inc(e["o"].sem, 1)
                            elif (g, i) == (0, 2):
                                add_output(b - 1)
                            elif (g, i) == (0, 3):
                                mean_and_var(b - 1, 2, tiles_of(b - 1), "x2")
                            elif (g, i) == (1, 0):
                                normalised(b - 1, 2, y, tiles_of(b - 1)).then_inc(e["y"].sem, 1)
                        if last:
                            continue
                        if (g, i) == (1, 3):
                            mean_and_var(b + 1, 0, tiles_of(b + 1))
                        elif (g, i) == (2, 0):
                            normalised(b + 1, 0, xn, tiles_of(b + 1)).then_inc(e["xn"].sem, 1)
                        elif g == 3 and i < 2:
                            lo_parts(b, i)
                if last:
                    weighted(b, GROUPS - 1)
                    mean_and_var(b, 1, projected, "proj")
                    normalised(b, 1, o, projected).then_inc(e["o"].sem, 1)
                    add_output(b)
                    mean_and_var(b, 2, tiles_of(b), "x2")
                    normalised(b, 2, y, tiles_of(b)).then_inc(e["y"].sem, 1)
                    return
                for i in range(PER_GROUP):
                    maxima(b + 1, 0, i)
                    if i == 1:
                        weighted(b, GROUPS - 1)
                negated_maxima(b + 1, 0)
                maxima(b + 1, 1, 0)

            mean_and_var(0, 0, tiles_of(0))
            normalised(0, 0, xn, tiles_of(0)).then_inc(e["xn"].sem, 1)
            for u in range(2):
                lo_parts(-1, u)
            for i in range(PER_GROUP):
                maxima(0, 0, i)
            negated_maxima(0, 0)
            maxima(0, 1, 0)
            each(dve, sequence)


QKV = 3 * INNER
CHUNK = 512
HEADS_C = CHUNK // DH
PAIRS = H // 2
KEYS = WINDOW + P
SCORE_GROUPS = ((0, 2, 4), (1, 3, 5), (6, 8, 10), (7, 9, 11), (12, 14), (13, 15))
LOADS = 9 + 2 * FC + 2

SLOT = {
    "PE": (("P", 0), ("P", 1), ("X-", 3), ("S", 0), ("P", 2), ("S", 1), ("S", 2), ("P", 3), ("V-", 1), ("T", 0),
    ("T", 1), ("S", 3), ("O", 0), ("S", 4), ("P", 4), ("O", 1), ("S", 5), ("P", 5), ("X", 0), ("X", 1), ("W",),
    ("T", 2), ("T", 3), ("V", 0), ("X", 2)),
    "Act": (("P", 0), ("P", 1), ("S", 0), ("P", 2), ("S", 1), ("P", 3), ("T", 0), ("T", 1), ("S", 2), ("O", 0),
    ("S", 3), ("O", 1), ("P", 4), ("P", 5), ("S", 4), ("T", 2), ("S", 5), ("T", 3)),
    "DVE": (("XP-", 1), ("P", 0), ("S", 0), ("P", 1), ("X-", 3), ("S", 1), ("P", 2), ("S", 2), ("V-", 1), ("S", 3),
    ("P", 3), ("XP", 0), ("S", 4), ("X", 0), ("X", 1), ("W",), ("S", 5), ("V", 0), ("X", 2)),
    "Pool": (("P", 0), ("P", 1), ("P", 2), ("P", 3)),
}
FFN_AT = {
    "PE": {(0, 22): [("F0",)], (1, 9): [("F1",)], (1, 22): [("F3",)], (2, 1): [("G", 0)], (2, 5): [("A", 0)], (2,
    18): [("G", 1)], (2, 25): [("A", 1)], (3, 3): [("G", 2)], (3, 5): [("A", 2)], (3, 13): [("F4",)]},
    "Act": {(0, 15): [("F1",)], (1, 18): [("F3",)], (2, 1): [("G", 0)], (2, 12): [("G", 1)], (3, 1): [("G", 2)]},
    "DVE": {(0, 16): [("F0",)], (1, 7): [("F1",)], (1, 12): [("F2",)], (1, 17): [("F3",)], (2, 11): [("A", 0)], (3,
    1): [("A", 1)], (3, 7): [("A", 2)], (3, 12): [("F4",)]},
    "Pool": {(1, 2): [("F2",)]},
}
FFN = (("F0",), ("F1",), ("F2",), ("F3",), ("G", 0), ("A", 0), ("G", 1), ("A", 1), ("G", 2), ("A", 2), ("F4",))


def steps_of(engine, kind):
    steps = []
    if kind == "start":
        steps = [(("NQ", k), -1) for k in range(6)] + [(("XS", 0), -1), (("XS", 1), -1)]
        for k in range(6):
            steps += [(("P", k), -1)] + [(("T", k - 2), -1)] * (k >= 2)
        steps += [(("NO",), -1), (("NF",), -1)]
    late = [step for step in SLOT[engine] if step[0][-1] == "-"]
    for t in range(TILES):
        if t == TILES - 1 and kind == "last" and engine == "DVE":
            steps += [(("NQ", 4), t), (("NQ", 5), t)]
        if t == TILES - 2 and kind != "end":
            steps.append((("XS", 0), t))
        for n, step in enumerate(SLOT[engine]):
            tile = t - (step[0][-1] == "-")
            name = step[0].rstrip("-")
            skip = ((name in "OW" or tile < 0) and t == 0 and kind == "start") or \
                   (name in "PT" and t == TILES - 1 and kind == "end") or (name == "XP" and tile % TILES == 0)
            if not skip:
                steps.append(((name, *step[1:]), tile))
                if name == "P" and t == TILES - 2 and kind == "last":
                    steps.append((("NQ", step[1]), t))
                if name == "W" and t == 0 and kind == "first":
                    steps.append((("NO",), t))
            if kind != "start":
                for f in FFN_AT[engine].get((t, n + 1), ()):
                    steps.append((f, t))
        if t == TILES - 1 and kind != "end":
            steps.append((("XS", 1), t))
        if t == TILES - 1 and kind == "first":
            steps.append((("NF",), t))
    if kind == "end":
        steps += [((name[:-1], k), TILES - 1) for name, k in late]
        steps += [(step, TILES) for step in (("O", 0), ("O", 1), ("W",)) + FFN]
    return steps


def layer_events(sem):
    return {
        "xs_hi": Events(sem("xs_hi"), 2), "xs": Events(sem("xs"), 2), "proj_full": Events(sem("proj_full"), 6 * TILES),
        "square": Events(sem("square"), 4 * TILES), "rotated": Events(sem("rotated"), 4 * TILES),
        "sums": Events(sem("sums"), 4 * TILES), "floor": Events(sem("floor"), 4 * TILES),
        "added": Events(sem("added"), 2 * TILES), "norm": Events(sem("norm"), 4 * TILES),
        "qk": Events(sem("qk"), 4 * TILES), "v": Events(sem("v"), 2 * TILES),
        "qkT_full": Events(sem("qkT_full"), 4 * TILES), "qkT": Events(sem("qkT"), 4 * TILES),
        "s_full": Events(sem("s_full"), 6 * TILES), "row_max": Events(sem("row_max"), 6 * TILES),
        "bias": Events(sem("bias"), 6 * TILES), "exp": Events(sem("exp"), H * TILES),
        "pT_full": Events(sem("pT_full"), 4 * TILES), "pT": Events(sem("pT"), 4 * TILES),
        **{f"v_moved{m}": Events(sem(f"v_moved{m}"), 16) for m in range(TILES - 1)}, "ppT": Events(sem("ppT"), 2 * TILES - 2),
        "pv_full": Events(sem("pv_full"), 2 * TILES), "recip": Events(sem("recip"), 2 * TILES),
        "attn": Events(sem("attn"), 2 * TILES),
        "oT_full": Events(sem("oT_full"), 2 * TILES), "oT": Events(sem("oT"), 2 * TILES),
        "w_full": Events(sem("w_full"), TILES), "x_mid": Events(sem("x_mid"), TILES),
        "xf": Events(sem("xf"), 1), "mean_full": Events(sem("mean_full"), 1), "centred": Events(sem("centred"), 1),
        "f_square": Events(sem("f_square"), 1), "var_full": Events(sem("var_full"), 1), "f_var": Events(sem("f_var"), 1),
        "f_rstd": Events(sem("f_rstd"), 1), "diag": Events(sem("diag"), 1), "spread_full": Events(sem("spread_full"), 1),
        "xn": Events(sem("xn"), 1), "xn_hi": Events(sem("xn_hi"), 1), "xn_lo": Events(sem("xn_lo"), 1),
        "gate_full": Events(sem("gate_full"), FC), "gelu": Events(sem("gelu"), FC),
        "up_full": Events(sem("up_full"), FC), "gated": Events(sem("gated"), FC),
        "y_full": Events(sem("y_full"), 1), "x_new": Events(sem("x_new"), 1),
    }


def load_layer(sp, arrived, w, layer):
    one = bass.ds(layer, 1)
    flat = lambda x: x.rearrange("a n -> (a n)")

    def load(out, in_):
        sp.dma_start(out, in_).then_inc(arrived["loaded"], 16)

    for k in range(2):
        half = slice(k * QKV // 2, (k + 1) * QKV // 2)
        load(arrived["qkv"][:, half], w["Wqkv"][one, :, half].rearrange("a k n -> (a k) n"))
    for k in range(2):
        load(arrived["w1"][:, k, 0:FF], w["W1"][one, :, k * FF:(k + 1) * FF].rearrange("a k n -> (a k) n"))
        for j in range(FC):
            n = P if j < FC - 1 else FR
            load(arrived["b1"][0:n, k, j:j + 1],
                 flat(w["b1"][one, k * FF + j * P:k * FF + j * P + n]).rearrange("(n a) -> n a", a=1))
    load(arrived["w2"][:, 0:FC - 1, :], w["W2"][one, 0:(FC - 1) * P, :].rearrange("a (c p) n -> p (a c) n", p=P))
    load(arrived["w2"][0:FR, FC - 1, :], w["W2"][one, (FC - 1) * P:FF, :].rearrange("a p n -> (a p) n"))
    load(arrived["w2"][BIAS_ROW:BIAS_ROW + 1, FC - 1, :], w["b2"][one])
    load(arrived["g"][:, :], flat(w["ln_g"][one]).rearrange("(n a) -> n a", a=1))
    load(arrived["b"][:, :], flat(w["ln_b"][one]).rearrange("(n a) -> n a", a=1))
    load(arrived["qs"][:, :], w["q_scale"][one].broadcast_to([P, DH]))
    load(arrived["ks"][:, :], w["k_scale"][one].broadcast_to([P, DH]))


def arriving(sb, sem):
    return {"qkv": sb("in_qkv", [P, QKV]), "w1": sb("in_w1", [P, 2, FC * P]), "w2": sb("in_w2", [P, FC, D]),
            "b1": sb("in_b1", [P, 2, FC]), "g": sb("in_g", [P, 1]), "b": sb("in_b", [P, 1]),
            "qs": sb("in_qs", [P, DH]), "ks": sb("in_ks", [P, DH]), "tables": sb("tables_sb", [P, 4, TILES, DH]),
            "loaded": sem("w_arrived"), "tables_loaded": sem("tables_loaded")}


def layers_stage(nc, c, e, w, arrived):
    with ExitStack() as ctx:
        def sb(name, shape, dt=F32):
            return ctx.enter_context(nc.sbuf_tensor(name, shape, dt))

        def bank(name):
            return ctx.enter_context(nc.psum_tensor(name, [P, 512], F32))

        def sem(name):
            return ctx.enter_context(nc.semaphore(name))

        in_qkv, in_w1, in_w2, in_b1 = arrived["qkv"], arrived["w1"], arrived["w2"], arrived["b1"]
        in_g, in_b, in_qs, in_ks = arrived["g"], arrived["b"], arrived["qs"], arrived["ks"]
        tables, loaded, tables_loaded = arrived["tables"], arrived["loaded"], arrived["tables_loaded"]
        qkv_hi, qkv_lo = sb("qkv_hi", [P, QKV], F32R), sb("qkv_lo", [P, QKV], F32R)
        wo = sb("wo", [P, INNER // P, D])
        w1_hi, w1_lo = sb("w1_hi", [P, 2, FC * P], F32R), sb("w1_lo", [P, 2, FC * P], F32R)
        b1, w2 = sb("b1", [P, 2 * FC]), sb("w2", [P, FC, D])
        turns = sb("turns", [P, 4, TILES, DH])
        xs_hi, xs_lo = sb("xs_hib", [P, S], F32R), sb("xs_lob", [P, S], F32R)
        squares = sb("squares", [P, 2, CHUNK])
        sums, norms = sb("sumsb", [P, 2, 4, HEADS_C]), sb("norms", [P, 2, 4, HEADS_C])
        by_cos, by_sin = sb("by_cos", [P, 2, CHUNK]), sb("by_sin", [P, 2, CHUNK])
        qk = sb("qkb", [P, 2, CHUNK])
        qT = sb("qT", [P, 2, PAIRS, P])
        kT = sb("kT", [P, PAIRS, S])
        v = sb("vb", [P, TILES, INNER])
        row_max, bias = sb("row_maxb", [P, 2, 3]), sb("biasb", [P, 2, 16])
        probs = sb("probs", [P, 2, H * KEYS])
        row_sum, recip = sb("row_sum", [P, 2, H]), sb("recipb", [P, 2, HEADS_C])
        pT, ppT = sb("pTb", [P, 2, 4, P]), sb("ppTb", [WINDOW, 2, HEADS_C, WINDOW])
        v_before = sb("v_before", [WINDOW, TILES - 1, INNER])
        attn, attnT = sb("attnb", [P, 2, CHUNK]), sb("attnT", [P, INNER // P, P])
        xf, xc = sb("xfb", [P, S]), sb("xcb", [P, S])
        xn_hi, xn_lo = sb("xn_hib", [P, S], F32R), sb("xn_lob", [P, S], F32R)
        f_var, f_rstd = sb("f_varb", [P, TILES]), sb("f_rstdb", [P, TILES])
        carrier = sb("carrier", [P, 1])
        gate, hidden = sb("gateb", [P, FC, S]), sb("hidden", [P, FC, S])
        diag, fsq = gate[:, 0, :].rearrange("p (t n) -> p t n", t=TILES), gate[:, 1, :]
        proj = [bank("proj0"), bank("proj1")]
        score = [bank("score0"), bank("score1")]
        turn = [bank("turn0"), bank("turn1")]
        pv_bank, out_bank = bank("pv_bank"), bank("out_bank")
        padded = sem("padded")
        p_hi, p_lo, wo_loaded, p_scaled = sem("p_hi"), sem("p_lo"), sem("wo_loaded"), sem("p_scaled")
        p_w1_hi, p_bias_full, p_bias, p_used = sem("p_w1_hi"), sem("p_bias_full"), sem("p_bias"), sem("p_used")
        p_turns = sem("p_turns")
        block = ctx.enter_context(nc.Block())
        ident, ident_bf, ones = c["ident"], c["ident_bf"], c["ones"]
        xT = c["xT"]
        pv_v = pv_bank[:, :].rearrange("p (h d) -> p h d", d=DH)

        def at(name, t, k, cyc):
            return e[name].at(t * (e[name].per // TILES) + k, cyc)

        def wait_tile(eng, name, t, k, cyc):
            eng.wait_ge(e[name].sem, at(name, t, k, cyc))

        def wait(eng, name, k, cyc):
            eng.wait_ge(e[name].sem, e[name].at(k, cyc))

        def prev_parts(t, k):
            return 2 * (t - 1 if t > 0 else t) + k

        def run(eng, name, step, next_cycle=lambda: None):
            def cycle(kind, cyc, b, new=None):
                for s_, t in steps_of(name, kind):
                    step(s_, t, cyc, b, new)

            def middle(layer):
                with eng.Fori(1, B - 1) as b:
                    cycle("middle", eng.snap(layer * B + b), b)

            cycle("start", 0, 0, 0)
            next_cycle()
            with eng.Fori(0, DEPTH - 1) as layer:
                middle(layer)
                next_cycle()
                cycle("last", layer * B + (B - 1), B - 1, layer + 1)
                next_cycle()
                cycle("first", layer * B + B, 0, layer + 1)
                next_cycle()
            middle(DEPTH - 1)
            next_cycle()
            cycle("end", DEPTH * B - 1, B - 1)

        def all_loaded(new):
            return new * (16 * LOADS) + 16 * LOADS

        def previous(b):
            return B - 1 if isinstance(b, int) and b == 0 else b - 1

        @block.sync
        def _(sp):

            def load_wo(layer):
                sp.dma_start(wo[:, :, :], w["Wo"][bass.ds(layer, 1)].rearrange("a (c p) n -> p (a c) n", p=P))\
                    .then_inc(wo_loaded, 16)

            load_wo(0)
            sp.wait_ge(padded, 2)
            with sp.Fori(1, DEPTH) as layer:
                sp.wait_ge(padded, 2)
                sp.wait_ge(p_used, layer * 2)
                load_layer(sp, arrived, w, layer)
                sp.wait_ge(padded, 2)
                wait(sp, "w_full", 0, layer * B)
                load_wo(layer)
            sp.wait_ge(loaded, DEPTH * 16 * LOADS)
            sp.wait_ge(wo_loaded, DEPTH * 16)

        @block.gpsimd
        def _(pool):
            nc.gpsimd.memset(xs_hi[:, 0:1].bitcast(F32), 0.0)
            nc.gpsimd.memset(xs_lo[:, 0:1].bitcast(F32), 0.0)
            nc.gpsimd.memset(xf[:, 0:1], 0.0)
            nc.gpsimd.memset(hidden[:, FC - 1, :], 0.0).then_inc(padded, 1)
            pool.wait_ge(padded, 1)
            nc.gpsimd.memset(hidden[BIAS_ROW:BIAS_ROW + 1, FC - 1, :], 1.0).then_inc(padded, 1)

            def step(s_, t, cyc, b, new):
                kind, k = s_[0], s_[-1]
                if kind == "P" and k < 4:
                    m, j = t + 1, k % 2
                    wait_tile(pool, "floor", m, k + 1, cyc)
                    nc.gpsimd.tensor_tensor(norms[:, m % 2, k, :], sums[:, m % 2, k, :], c["minus_half"][:, 0:HEADS_C],
                                            ALU.pow).then_inc(e["norm"].sem, 1)
                    wait_tile(pool, "rotated", m, k + 1, cyc)
                    wait_tile(pool, "qkT_full", m, k - 1, cyc)
                    if k < 2:
                        nc.gpsimd.tensor_tensor(qk[:, j, :], by_cos[:, j, :], by_sin[:, j, :],
                                                ALU.add).then_inc(e["qk"].sem, 1)
                    else:
                        nc.gpsimd.tensor_tensor(by_cos[:, j, :], by_cos[:, j, :], by_sin[:, j, :],
                                                ALU.add).then_inc(e["added"].sem, 1)
                        wait_tile(pool, "added", m, k - 1, cyc)
                        heads = by_cos[:, j, :].rearrange("p (h d) -> p h d", d=DH)
                        nc.gpsimd.tensor_tensor(
                            qk[:, j, :].rearrange("p (h d) -> p h d", d=DH), heads,
                            norms[:, m % 2, k, :].unsqueeze(2).broadcast_to([P, HEADS_C, DH]),
                            ALU.mult).then_inc(e["qk"].sem, 1)
                elif kind == "NF":
                    wait(pool, "y_full", 0, cyc)
                    nc.gpsimd.tensor_tensor(w2[:, :, :], in_w2[:, :, :], ones[:, :].unsqueeze(1).broadcast_to([P, FC, D]),
                                            ALU.mult).then_inc(p_used, 1)
                elif kind == "F2":
                    wait(pool, "f_var", 1 if t == TILES else 0, cyc)
                    nc.gpsimd.tensor_tensor(f_rstd[:, :], f_var[:, :], c["minus_half"][:, 0:TILES],
                                            ALU.pow).then_inc(e["f_rstd"].sem, 1)

            run(pool, "Pool", step)

        @block.tensor
        def _(pe):
            pe.wait_ge(padded, 2)
            user = {"out": ("x_new", 0, 0), "turn0": ("oT", -1, 1), "turn1": ("oT", -1, 2)}

            def free(name, cyc):
                kind, t, k = user[name]
                wait_tile(pe, kind, t, k, cyc)

            def next_cycle():
                for name, (kind, t, k) in user.items():
                    user[name] = (kind, t - TILES, k)

            def step(s_, t, cyc, b, new):
                kind, k = s_[0], s_[-1]
                if kind == "P":
                    m = t + 1
                    if k == 0 and m % 2 == 0:
                        wait(pe, "xs", m // 2 + 1, cyc)
                    if new is not None and m % TILES == 0:
                        pe.wait_ge(p_lo, new * 6 + k + 1)
                    if k in (0, 1):
                        wait_tile(pe, "v", m, k - 1, cyc)
                    else:
                        wait_tile(pe, "rotated", m, k - 1, cyc)
                    tile = slice((m % TILES) * P, (m % TILES + 1) * P)
                    cols = slice(k * CHUNK, (k + 1) * CHUNK)
                    out = proj[k % 2][:, :]
                    nc.tensor.matmul(out, xs_hi[:, tile], qkv_hi[:, cols], start=True, stop=False)
                    nc.tensor.matmul(out, xs_hi[:, tile], qkv_lo[:, cols], start=False, stop=False)
                    nc.tensor.matmul(out, xs_lo[:, tile], qkv_hi[:, cols], start=False,
                                     stop=True).then_inc(e["proj_full"].sem, 1)
                elif kind == "T":
                    m = t + 1
                    free(f"turn{k % 2}", cyc)
                    wait_tile(pe, "qk", m, k + 1, cyc)
                    for i in range(4):
                        last = nc.tensor.transpose(turn[k % 2][:, i * P:(i + 1) * P], qk[:, k % 2, i * P:(i + 1) * P],
                                                   ident[:, :])
                    last.then_inc(e["qkT_full"].sem, 1)
                    user[f"turn{k % 2}"] = ("qkT", m, k + 1)
                elif kind == "S":
                    heads = SCORE_GROUPS[k]
                    n = len(heads)
                    if k == 0:
                        wait_tile(pe, "qkT", t, 4, cyc)
                    wait_tile(pe, "row_max", t, k - 1, cyc)
                    first = 0 if t else WINDOW
                    out = score[k % 2][:, 0:n * KEYS].rearrange("p (h k) -> p h k", k=KEYS)
                    for i, h in enumerate(heads):
                        rows = slice((h % 2) * DH, (h % 2 + 1) * DH)
                        last = nc.tensor.matmul(out[:, i, first:], qT[rows, t % 2, h // 2, :],
                                                kT[rows, h // 2, t * P - WINDOW + first:(t + 1) * P],
                                                start=True, stop=True)
                    last.then_inc(e["s_full"].sem, 1)
                elif kind == "X":
                    wait_tile(pe, "exp", t, (6, 12, 12, 16)[k], cyc)
                    free(f"turn{k % 2}", cyc)
                    for i in range(4):
                        col = (4 * k + i) * KEYS + WINDOW
                        last = nc.tensor.transpose(turn[k % 2][:, i * P:(i + 1) * P], probs[:, t % 2, col:col + P],
                                                   ident[:, :])
                    last.then_inc(e["pT_full"].sem, 1)
                    user[f"turn{k % 2}"] = ("pT", t, k + 1)
                elif kind == "V":
                    wait_tile(pe, "v", t, 2, cyc)
                    wait_tile(pe, "attn", t, k, cyc)
                    if t % TILES:
                        wait(pe, f"v_moved{t % TILES - 1}", 16 if t > 0 else 0, cyc)
                        pe.wait_ge(e["ppT"].sem, e["ppT"].at(prev_parts(t, k + 1), cyc))
                    for i in range(HEADS_C):
                        h = HEADS_C * k + i
                        if i % 4 == 0:
                            wait_tile(pe, "pT", t, h // 4 + 1, cyc)
                        cols = slice(h * DH, (h + 1) * DH)
                        last = nc.tensor.matmul(pv_v[:, i, :], pT[:, h // 4 % 2, h % 4, :], v[:, t % TILES, cols],
                                                start=True, stop=True)
                        if t % TILES:
                            last = nc.tensor.matmul(pv_v[0:WINDOW, i, :], ppT[:, k, i, :],
                                                    v_before[:, t % TILES - 1, cols],
                                                    start=False, stop=True, skip_group_check=True)
                    last.then_inc(e["pv_full"].sem, 1)
                elif kind == "O":
                    wait_tile(pe, "attn", t - 1, k + 1, cyc)
                    free(f"turn{k}", cyc)
                    for i in range(4):
                        last = nc.tensor.transpose(turn[k][:, i * P:(i + 1) * P], attn[:, k, i * P:(i + 1) * P],
                                                   ident[:, :])
                    last.then_inc(e["oT_full"].sem, 1)
                    user[f"turn{k}"] = ("oT", t - 1, k + 1)
                elif kind == "W":
                    wait_tile(pe, "oT", t - 1, 2, cyc)
                    free_out(t, cyc)
                    for i in range(INNER // P):
                        last = nc.tensor.matmul(out_bank[:, 0:P], wo[:, i, :], attnT[:, i, :], start=(i == 0),
                                                stop=(i == INNER // P - 1))
                    last.then_inc(e["w_full"].sem, 1)
                    user["out"] = ("x_mid", t - 1, 1)
                elif kind == "NO":
                    pe.wait_ge(wo_loaded, new * 16 + 16)
                elif kind == "NF":
                    pe.wait_ge(loaded, all_loaded(new))
                    free_out(t, cyc)
                    for n in range(2 * FC):
                        part, j = n // FC, n % FC
                        last = nc.tensor.matmul(out_bank[:, n:n + 1], in_w1[:, part, j * P:(j + 1) * P], in_b[:, :],
                                                start=True, stop=True)
                    last.then_inc(p_bias_full, 1)
                    pe.wait_ge(p_bias, new + 1)
                elif kind in "FGA" or kind[0] == "F":
                    ffn(s_, t, cyc)

            def free_out(t, cyc):
                if t == 0:
                    wait_tile(pe, "x_mid", -1, 0, cyc)
                    wait(pe, "x_new", -1, cyc)
                else:
                    kind, tile, k = user["out"]
                    if kind == "x_mid":
                        wait_tile(pe, kind, tile, k, cyc)
                    else:
                        wait(pe, kind, k, cyc)

            def ffn(s_, t, cyc):
                kind, k = s_[0], s_[-1]
                ahead = 1 if t == TILES else 0
                if kind == "F0":
                    wait(pe, "xf", ahead, cyc)
                    free_out(t or 1, cyc)
                    nc.tensor.matmul(out_bank[:, :], c["mean_of"][:, :], xf[:, :], start=True,
                                     stop=True).then_inc(e["mean_full"].sem, 1)
                    user["out"] = ("centred", 0, ahead)
                elif kind == "F1":
                    wait(pe, "f_square", ahead, cyc)
                    free_out(t, cyc)
                    for i in range(TILES):
                        last = nc.tensor.matmul(out_bank[:, i:i + 1], fsq[:, i * P:(i + 1) * P], c["mean_of"][:, 0:1],
                                                start=True, stop=True)
                    last.then_inc(e["var_full"].sem, 1)
                    user["out"] = ("f_var", 0, ahead)
                elif kind == "F3":
                    wait(pe, "diag", ahead, cyc)
                    free_out(t, cyc)
                    nc.tensor.matmul(out_bank[:, :], ones[:, :], diag[:, :, :].rearrange("p t n -> p (t n)"), start=True,
                                     stop=True).then_inc(e["spread_full"].sem, 1)
                    user["out"] = ("xn", 0, ahead)
                elif kind in "GA":
                    part = 1 if kind == "G" else 0
                    done = ahead * FC + k + 1
                    wait(pe, "xn_lo", ahead, cyc)
                    free_out(t, cyc)
                    cols = slice(k * P, (k + 1) * P)
                    nc.tensor.matmul(out_bank[:, :], w1_hi[:, part, cols], xn_hi[:, :], start=True, stop=False)
                    nc.tensor.matmul(out_bank[:, :], w1_hi[:, part, cols], xn_lo[:, :], start=False, stop=False)
                    nc.tensor.matmul(out_bank[:, :], w1_lo[:, part, cols], xn_hi[:, :], start=False,
                                     stop=True).then_inc(e["gate_full" if part else "up_full"].sem, 1)
                    user["out"] = ("gelu" if part else "gated", 0, done - FC)
                elif kind == "F4":
                    wait(pe, "gated", ahead * FC, cyc)
                    free_out(t, cyc)
                    for j in range(FC):
                        n = P if j < FC - 1 else BIAS_ROW + 1
                        last = nc.tensor.matmul(out_bank[:, :], w2[0:n, j, :], hidden[0:n, j, :], start=(j == 0),
                                                stop=(j == FC - 1))
                    last.then_inc(e["y_full"].sem, 1)
                    user["out"] = ("x_new", 0, ahead)

            run(pe, "PE", step, next_cycle)

        @block.scalar
        def _(act):
            act.wait_ge(padded, 2)

            def copy(out, in_):
                return nc.scalar.activation(out, in_, ACT.Copy)

            def shifted(half, ahead, cyc, b):
                wait_tile(act, "proj_full", 2 * (half + 1) if ahead else 0, 0, cyc)
                lo, hi = half * S // 2, (half + 1) * S // 2
                late = max(lo, 1)
                copy(xs_hi[0:P // 2, lo:hi], xT[0:P // 2, bass.ds(b, 1), lo:hi].rearrange("p a n -> p (a n)"))
                copy(xs_hi[P // 2:P, late:hi], xT[P // 2:P, bass.ds(b, 1), late - 1:hi - 1].rearrange("p a n -> p (a n)"))\
                    .then_inc(e["xs_hi"].sem, 1)

            def step(s_, t, cyc, b, new):
                kind, k = s_[0], s_[-1]
                if kind == "XS":
                    shifted(k, *((0, cyc, 0) if t < 0 else (1, cyc, 0 if isinstance(b, int) and b == B - 1 else b + 1)))
                elif kind == "P":
                    m = t + 1
                    wait_tile(act, "proj_full", m, k + 1, cyc)
                    if k < 4:
                        wait_tile(act, "sums", m, k - 1, cyc)
                        nc.scalar.activation(squares[:, k % 2, :], proj[k % 2][:, :], ACT.Square)\
                            .then_inc(e["square"].sem, 1)
                    else:
                        wait_tile(act, "pv_full", m - 3, 2, cyc)
                        copy(v[:, m % TILES, (k - 4) * CHUNK:(k - 3) * CHUNK], proj[k % 2][:, :])\
                            .then_inc(e["v"].sem, 1)
                        if k == 5 and m % TILES < TILES - 1:
                            wait_tile(act, "v", m, 2, cyc)
                            act.dma_start(v_before[:, m % TILES, :], v[P - WINDOW:P, m % TILES, :])\
                                .then_inc(e[f"v_moved{m % TILES}"].sem, 16)
                elif kind == "T":
                    m = t + 1
                    wait_tile(act, "qkT_full", m, k + 1, cyc)
                    bank_ = turn[k % 2][:, :].rearrange("p (a n) -> p a n", n=P)
                    pairs = slice((k % 2) * 4, (k % 2) * 4 + 4)
                    if k < 2:
                        wait_tile(act, "s_full", m - 2, 6, cyc)
                        out = qT[:, m % 2, pairs, :]
                    else:
                        out = kT[:, pairs, (m % TILES) * P:(m % TILES + 1) * P]
                    copy(out, bank_).then_inc(e["qkT"].sem, 1)
                elif kind == "S":
                    wait_tile(act, "bias", t, k + 1, cyc)
                    if k == 0:
                        wait_tile(act, "recip", t - 1, 0, cyc)
                    first = 0 if t else WINDOW
                    for h in SCORE_GROUPS[k]:
                        col = h * KEYS
                        heads_probs = probs[:, t % 2, col + first:col + KEYS]
                        nc.scalar.activation(
                            heads_probs, heads_probs, ACT.Exp,
                            scale=norms[:, t % 2, h // HEADS_C, h % HEADS_C:h % HEADS_C + 1],
                            bias=bias[:, t % 2, h:h + 1], accum_out=row_sum[:, t % 2, h:h + 1]).then_inc(e["exp"].sem, 1)
                elif kind == "O":
                    wait_tile(act, "oT_full", t - 1, k + 1, cyc)
                    wait_tile(act, "w_full", t - 1, 0, cyc)
                    copy(attnT[:, 4 * k:4 * k + 4, :], turn[k][:, :].rearrange("p (a n) -> p a n", n=P))\
                        .then_inc(e["oT"].sem, 1)
                elif kind == "NQ":
                    if k == 0:
                        act.wait_ge(loaded, all_loaded(new))
                    cols = slice(k * CHUNK, (k + 1) * CHUNK)
                    copy(qkv_hi[:, cols], in_qkv[:, cols]).then_inc(p_hi, 1)
                elif kind == "NF":
                    act.wait_ge(p_scaled, new + 1)
                    wait(act, "up_full", 0, cyc)
                    copy(w1_hi[:, :, :], in_w1[:, :, :]).then_inc(p_w1_hi, 1)
                elif kind in ("F1", "F3", "G"):
                    ahead = 1 if t == TILES else 0
                    if kind == "F1":
                        wait(act, "centred", ahead, cyc)
                        nc.scalar.activation(fsq, xc[:, :], ACT.Square).then_inc(e["f_square"].sem, 1)
                    elif kind == "F3":
                        wait(act, "xn", ahead, cyc)
                        copy(xn_hi[:, :], xc[:, :]).then_inc(e["xn_hi"].sem, 1)
                    else:
                        wait(act, "gate_full", ahead * FC + k + 1 - FC, cyc)
                        n = FC + k
                        nc.scalar.activation(gate[:, k, :], out_bank[:, :], ACT.Gelu, bias=b1[:, n:n + 1])\
                            .then_inc(e["gelu"].sem, 1)

            run(act, "Act", step)

        @block.vector
        def _(dve):
            dve.wait_ge(padded, 2)
            dve.wait_ge(tables_loaded, 16 * 4)

            def shifted(half, ahead, cyc, b):
                wait(dve, "xs_hi", 2 * ahead + half + 1, cyc)
                lo, hi = half * S // 2, (half + 1) * S // 2
                late = max(lo, 1)
                nc.vector.tensor_tensor(xs_lo[0:P // 2, lo:hi],
                                        xT[0:P // 2, bass.ds(b, 1), lo:hi].rearrange("p a n -> p (a n)"),
                                        xs_hi[0:P // 2, lo:hi].bitcast(F32), ALU.subtract)
                nc.vector.tensor_tensor(xs_lo[P // 2:P, late:hi],
                                        xT[P // 2:P, bass.ds(b, 1), late - 1:hi - 1].rearrange("p a n -> p (a n)"),
                                        xs_hi[P // 2:P, late:hi].bitcast(F32), ALU.subtract).then_inc(e["xs"].sem, 1)

            def step(s_, t, cyc, b, new):
                kind, k = s_[0], s_[-1]
                if kind == "XS":
                    shifted(k, *((0, cyc, 0) if t < 0 else (1, cyc, 0 if isinstance(b, int) and b == B - 1 else b + 1)))
                elif kind == "P" and k < 4:
                    m, j = t + 1, k % 2
                    tile = m % TILES
                    if new is not None and k == 0 and tile == 0:
                        dve.wait_ge(p_turns, new + 1)
                    wait_tile(dve, "square", m, k + 1, cyc)
                    if k >= 2:
                        wait_tile(dve, "qk", m, k - 1, cyc)
                    else:
                        wait_tile(dve, "qk", m - 1, k + 3, cyc)
                    heads = proj[j][:, :].rearrange("p (h a d) -> p h a d", a=2, d=DH // 2)
                    which = 0 if k < 2 else 2

                    def table(n):
                        return turns[:, which + n, tile, :].rearrange("p (a d) -> p a d", a=2).unsqueeze(1)\
                            .broadcast_to([P, HEADS_C, 2, DH // 2])

                    nc.vector.tensor_tensor(by_cos[:, j, :].rearrange("p (h a d) -> p h a d", a=2, d=DH // 2), heads,
                                            table(0), ALU.mult)
                    swapped = by_sin[:, j, :].rearrange("p (h a d) -> p h a d", a=2, d=DH // 2)[:, :, ::-1, :]
                    nc.vector.tensor_tensor(swapped, heads, table(1), ALU.mult).then_inc(e["rotated"].sem, 1)
                    if k == 0:
                        wait_tile(dve, "exp", m - 2, H, cyc)
                    nc.vector.tensor_reduce(sums[:, m % 2, k, :], squares[:, j, :].rearrange("p (h d) -> p h d", d=DH),
                                            AX.X, ALU.add).then_inc(e["sums"].sem, 1)
                    wait_tile(dve, "sums", m, k + 1, cyc)
                    unit = 1.0 / (QK_SCALE * QK_SCALE) if k < 2 else 1.0
                    nc.vector.tensor_scalar(sums[:, m % 2, k, :], sums[:, m % 2, k, :], unit, L2_EPS2 * unit,
                                            ALU.mult, ALU.max).then_inc(e["floor"].sem, 1)
                elif kind == "S":
                    n = len(SCORE_GROUPS[k])
                    if k == 0:
                        wait_tile(dve, "pT_full", t - 1, 0, cyc)
                    wait_tile(dve, "s_full", t, k + 1, cyc)
                    nc.vector.memset(carrier[:, :], 0.0)
                    first = 0 if t else WINDOW
                    for i, h in enumerate(SCORE_GROUPS[k]):
                        col = h * KEYS
                        last = nc.vector.tensor_tensor_reduce(
                            out=probs[:, t % 2, col + first:col + KEYS],
                            in0=score[k % 2][:, i * KEYS + first:(i + 1) * KEYS], in1=c["mask_band"][:, first:],
                            scale=1.0, scalar=LOWEST, op0=ALU.add, op1=ALU.max, accum_out=row_max[:, k % 2, i:i + 1])
                    last.then_inc(e["row_max"].sem, 1)
                    wait_tile(dve, "row_max", t, k + 1, cyc)
                    if k == 0:
                        wait_tile(dve, "norm", t, 2, cyc)
                    h = SCORE_GROUPS[k][0]
                    stop = SCORE_GROUPS[k][-1] + 1
                    scales = norms[:, t % 2, :, :].rearrange("p c h -> p (c h)")[:, h:stop:2]
                    nc.vector.scalar_tensor_tensor(out=bias[:, t % 2, h:stop:2], in0=row_max[:, k % 2, 0:n], scalar=-1.0,
                                                   in1=scales, op0=ALU.mult, op1=ALU.mult).then_inc(e["bias"].sem, 1)
                elif kind == "X":
                    wait_tile(dve, "pT_full", t, k + 1, cyc)
                    wait_tile(dve, "pv_full", t, k // 2, cyc)
                    nc.vector.tensor_copy(pT[:, k % 2, :, :].rearrange("p h q -> p (h q)"), turn[k % 2][:, :])\
                        .then_inc(e["pT"].sem, 1)
                elif kind == "XP":
                    wait_tile(dve, "exp", t, (12, 16)[k], cyc)
                    wait_tile(dve, "pv_full", t - 1, k + 1, cyc)
                    heads = probs[0:WINDOW, t % 2, HEADS_C * k * KEYS:HEADS_C * (k + 1) * KEYS]
                    nc.vector.transpose(ppT[:, k, :, :], heads.rearrange("p (h n) -> p h n", n=KEYS)[:, :, 0:WINDOW])\
                        .then_inc(e["ppT"].sem, 1)
                elif kind == "V":
                    wait_tile(dve, "exp", t, H if k else 12, cyc)
                    nc.vector.reciprocal(recip[:, k, :], row_sum[:, t % 2, k * HEADS_C:(k + 1) * HEADS_C])\
                        .then_inc(e["recip"].sem, 1)
                    wait_tile(dve, "recip", t, k + 1, cyc)
                    wait_tile(dve, "pv_full", t, k + 1, cyc)
                    wait_tile(dve, "oT_full", t - 1, k + 1, cyc)
                    nc.vector.tensor_tensor(attn[:, k, :].rearrange("p (h d) -> p h d", d=DH), pv_v[:, :, :],
                                            recip[:, k, :].unsqueeze(2).broadcast_to([P, HEADS_C, DH]),
                                            ALU.mult).then_inc(e["attn"].sem, 1)
                elif kind == "W":
                    wait_tile(dve, "w_full", t - 1, 1, cyc)
                    seq = previous(b) if t == 0 else b
                    tile = (t - 1) % TILES
                    x = xT[:, bass.ds(seq, 1), tile * P:(tile + 1) * P].rearrange("p a n -> p (a n)")
                    nc.vector.tensor_tensor(x, out_bank[:, 0:P], x, ALU.add).then_inc(e["x_mid"].sem, 1)
                elif kind == "NQ":
                    dve.wait_ge(p_hi, new * 6 + k + 1)
                    cols = slice(k * CHUNK, (k + 1) * CHUNK)
                    nc.vector.tensor_tensor(qkv_lo[:, cols], in_qkv[:, cols], qkv_hi[:, cols].bitcast(F32),
                                            ALU.subtract).then_inc(p_lo, 1)
                    if k == 5:
                        for n, scale in enumerate((in_qs, in_qs, in_ks, in_ks)):
                            last = nc.vector.tensor_tensor(turns[:, n, :, :], tables[:, n, :, :],
                                                           scale[:, :].unsqueeze(1).broadcast_to([P, TILES, DH]),
                                                           ALU.mult)
                        last.then_inc(p_turns, 1)
                elif kind == "NF":
                    dve.wait_ge(p_bias_full, new + 1)
                    nc.vector.tensor_scalar(in_w1[:, :, :], in_w1[:, :, :], in_g[:, 0:1], None, ALU.mult)\
                        .then_inc(p_scaled, 1)
                    nc.vector.tensor_tensor(b1[:, :], out_bank[:, 0:2 * FC], in_b1[:, :, :].rearrange("p a j -> p (a j)"),
                                            ALU.add).then_inc(p_bias, 1)
                    dve.wait_ge(p_w1_hi, new + 1)
                    nc.vector.tensor_tensor(w1_lo[:, :, :], in_w1[:, :, :], w1_hi[:, :, :].bitcast(F32),
                                            ALU.subtract).then_inc(p_used, 1)
                elif kind in ("F0", "F1", "F2", "F3", "A", "F4"):
                    ffn(s_, t, cyc, b)

            def ffn(s_, t, cyc, b):
                kind, k = s_[0], s_[-1]
                ahead, seq = (1, b) if t == TILES else (0, previous(b))
                rows = lambda lo, hi, stop: xT[lo:hi, bass.ds(seq, 1), 0:stop].rearrange("p a n -> p (a n)")
                if kind == "F0":
                    wait_tile(dve, "x_mid", TILES * ahead, 0, cyc)
                    nc.vector.tensor_copy(xf[0:P // 2, :], rows(0, P // 2, S))
                    nc.vector.tensor_copy(xf[P // 2:P, 1:S], rows(P // 2, P, S - 1)).then_inc(e["xf"].sem, 1)
                    wait(dve, "mean_full", ahead, cyc)
                    nc.vector.tensor_tensor(xc[:, :], xf[:, :], out_bank[:, :], ALU.subtract)\
                        .then_inc(e["centred"].sem, 1)
                elif kind == "F1":
                    wait(dve, "var_full", ahead, cyc)
                    nc.vector.tensor_scalar(f_var[:, :], out_bank[:, 0:TILES], LN_EPS, None, ALU.add)\
                        .then_inc(e["f_var"].sem, 1)
                elif kind == "F2":
                    wait(dve, "f_rstd", ahead, cyc)
                    nc.vector.tensor_tensor(diag[:, :, :], ident[:, :].unsqueeze(1).broadcast_to([P, TILES, P]),
                                            f_rstd[:, :].unsqueeze(2).broadcast_to([P, TILES, P]), ALU.mult)\
                        .then_inc(e["diag"].sem, 1)
                elif kind == "F3":
                    wait(dve, "spread_full", ahead, cyc)
                    nc.vector.tensor_tensor(xc[:, :], xc[:, :], out_bank[:, :], ALU.mult).then_inc(e["xn"].sem, 1)
                    wait(dve, "xn_hi", ahead, cyc)
                    nc.vector.tensor_tensor(xn_lo[:, :], xc[:, :], xn_hi[:, :].bitcast(F32), ALU.subtract)\
                        .then_inc(e["xn_lo"].sem, 1)
                elif kind == "A":
                    n = P if k < FC - 1 else FR
                    wait(dve, "up_full", ahead * FC + k + 1 - FC, cyc)
                    wait(dve, "gelu", ahead * FC + k + 1 - FC, cyc)
                    nc.vector.scalar_tensor_tensor(out=hidden[0:n, k, :], in0=out_bank[0:n, :], scalar=b1[0:n, k:k + 1],
                                                   in1=gate[0:n, k, :], op0=ALU.add, op1=ALU.mult)\
                        .then_inc(e["gated"].sem, 1)
                elif kind == "F4":
                    wait(dve, "y_full", ahead, cyc)
                    x = rows(0, P, S)
                    nc.vector.tensor_tensor(x, out_bank[:, :], x, ALU.add).then_inc(e["x_new"].sem, 1)

            run(dve, "DVE", step)


def output_stage(nc, c, residual, out_dram):
    with ExitStack() as ctx:
        def sb(name, shape, dt=F32):
            return ctx.enter_context(nc.sbuf_tensor(name, shape, dt))

        def sem(name):
            return ctx.enter_context(nc.semaphore(name))

        stat6, stat = sb("o_stat6", [P, 2, TILES, 6]), sb("o_stat", [P, B, TILES, 2])
        var, rstd, o = sb("o_var", [P, B, TILES]), sb("o_rstd", [P, B, TILES]), sb("o_o", [P, 2, TILES, D])
        x = sb("o_x", [P, B * TILES, D])
        turn = [ctx.enter_context(nc.psum_tensor(f"o_turn{b}", [P, S], F32)) for b in range(B)]
        turned, stats, var_done, rstd_done = sem("o_turned"), sem("o_stats"), sem("o_vard"), sem("o_rstdd")
        normalised, summed, stored, x_loaded = sem("o_normalised"), sem("o_summed"), sem("o_stored"), sem("o_x_loaded")
        block = ctx.enter_context(nc.Block())

        @block.tensor
        def _(pe):
            for b in range(B):
                for t in range(TILES):
                    last = nc.tensor.transpose(turn[b][:, t * P:(t + 1) * P], c["xT"][:, b, t * P:(t + 1) * P],
                                               c["ident"][:, :])
                last.then_inc(turned, 1)

        @block.gpsimd
        def _(pool):
            pool.wait_ge(x_loaded, 16)
            for b in range(B + 1):
                if b < B:
                    pool.wait_ge(var_done, b + 1)
                    nc.gpsimd.tensor_tensor(rstd[:, b, :], var[:, b, :], c["minus_half"][:, 0:TILES],
                                            ALU.pow).then_inc(rstd_done, 1)
                if b >= 1:
                    pool.wait_ge(normalised, b)
                    four = x[:, (b - 1) * TILES:b * TILES, :]
                    nc.gpsimd.tensor_tensor(four, four, o[:, (b - 1) % 2, :, :], ALU.add).then_inc(summed, 1)

        @block.vector
        def _(dve):
            for b in range(B + 1):
                if b < B:
                    dve.wait_ge(turned, b + 1)
                    for t in range(TILES):
                        last = nc.vector.bn_stats(stat6[:, b % 2, t, :], turn[b][:, t * P:(t + 1) * P])
                    last.then_inc(stats, 1)
                    dve.wait_ge(stats, 2 * b + 1)
                    for t in range(TILES):
                        last = nc.vector.bn_aggr(stat[:, b, t, :], stat6[:, b % 2, t, :])
                    last.then_inc(stats, 1)
                    dve.wait_ge(stats, 2 * b + 2)
                    nc.vector.tensor_scalar(var[:, b, :], stat[:, b, :, 1], LN_EPS, None, ALU.add).then_inc(var_done, 1)
                if b >= 1:
                    dve.wait_ge(rstd_done, b)
                    if b >= 3:
                        dve.wait_ge(summed, b - 2)
                    for t in range(TILES):
                        last = nc.vector.tensor_scalar(o[:, (b - 1) % 2, t, :], turn[b - 1][:, t * P:(t + 1) * P],
                                                       stat[:, b - 1, t, 0:1], rstd[:, b - 1, t:t + 1],
                                                       ALU.subtract, ALU.mult)
                    last.then_inc(normalised, 1)

        @block.sync
        def _(sp):
            sp.dma_start(x[:, :, :], residual).then_inc(x_loaded, 16)
            for b in range(B):
                sp.wait_ge(summed, b + 1)
                sp.dma_start(out_dram[b].rearrange("(t p) d -> p t d", p=P),
                             x[:, b * TILES:(b + 1) * TILES, :]).then_inc(stored, 16)
            sp.wait_ge(stored, 16 * B)


def program(nc, a, out_dram):
    with ExitStack() as ctx:
        def sb(name, shape, dt=F32):
            return ctx.enter_context(nc.sbuf_tensor(name, shape, dt))

        def sem(name):
            return ctx.enter_context(nc.semaphore(name))

        c = {
            "xT": sb("xT", [P, B, S]),
            "ident": sb("ident", [P, P]), "ident_bf": sb("ident_bf", [P, P], BF16),
            "ones": sb("ones", [P, P]), "mean_of": sb("mean_of", [P, P]), "minus_half": sb("minus_half", [P, 8]),
            "mask_qk": sb("mask_qk", [P, P], BF16), "mask_kq": sb("mask_kq", [P, P], BF16),
            "mask_band": sb("mask_band", [P, KEYS]),
        }
        mqa, layers = mqa_events(sem), layer_events(sem)
        arrived = arriving(sb, sem)
        ffn_inputs = {n: a["L0_ffn_" + n] for n in FFN_INPUTS}

        def first_layer(sp):
            for k in range(4):
                sp.dma_start(arrived["tables"][:, k, :, :], a["tables"][k].rearrange("(t p) d -> p t d", p=P))\
                    .then_inc(arrived["tables_loaded"], 16)
            load_layer(sp, arrived, ffn_inputs, 0)

        residual = nc.dram_tensor("residual", (P, B * TILES, D), F32, kind="Internal").ap()
        with nc.sbuf_tensor("x_tok", [P, B * TILES, D], F32) as x_tok:
            c["x_tok"] = x_tok
            constants_stage(nc, c, a["L0_attn_x"], list(mqa.values()) + list(layers.values()), arrived)
            mqa_stage(nc, c, mqa, {n: a["L0_attn_" + n] for n in ("Wq", "bq", "Wk", "bk", "Wv", "bv", "Wo", "bo")},
                      residual, first_layer)
        layers_stage(nc, c, layers, ffn_inputs, arrived)
        output_stage(nc, c, residual, out_dram)


FFN_INPUTS = ("Wqkv", "q_scale", "k_scale", "Wo", "ln_g", "ln_b", "W1", "b1", "W2", "b2")


def kernel(**inputs):
    import concourse.bacc as bacc
    from concourse.bass_utils import run_bass_kernel_spmd

    nc = bacc.Bacc("TRN2", target_bir_lowering=False, num_devices=1)
    arrays = {name: np.ascontiguousarray(a) for name, a in inputs.items()}
    arrays["tables"] = rotary_tables()
    args = {n: nc.dram_tensor(n, a.shape, mybir.dt.from_np(a.dtype), kind="ExternalInput").ap()
            for n, a in arrays.items()}
    out = nc.dram_tensor("out", (B, S, D), F32, kind="ExternalOutput").ap()
    program(nc, args, out)
    return run_bass_kernel_spmd(nc, [arrays], core_ids=[0]).results[0]["out"]
```
